# Optimizing a Trainium2 kernel written in Bass

```python
import numpy as np
import jax
import jax.numpy as jnp

def _softmax(x, axis=-1):
    return jax.nn.softmax(x, axis=axis)

def _gelu(x):
    return jax.nn.gelu(x, approximate=True)

def _silu(x):
    return jax.nn.silu(x)

def _sigmoid(x):
    return jax.nn.sigmoid(x)

def _layernorm(x, axis=-1, eps=1e-05):
    m = jnp.mean(x, axis=axis, keepdims=True)
    v = jnp.var(x, axis=axis, keepdims=True)
    return (x - m) / jnp.sqrt(v + eps)

def _scatter_add(tgt, idx, src, axis=0):
    return tgt.at[idx].add(src)

def _segment_sum(src, seg, n):
    return jax.ops.segment_sum(src, seg, n)
kernel_name = 'mk_gnn_resnorm_d4_gnn_r16_93faec'

def setup_inputs(seed: int=0):
    np.random.seed(seed)
    _w = jnp.asarray

    def _rec_inputs():
        import jax
        import jax.numpy as jnp
        _gk = jax.random.key(seed)
        x = -0.0003713 + 1 * jax.random.normal(jax.random.fold_in(_gk, 1), (6250, 128), jnp.float32)
        src = jax.random.randint(jax.random.fold_in(_gk, 2), (100000,), 0, 6250, jnp.int32)
        dst = jax.random.randint(jax.random.fold_in(_gk, 3), (100000,), 0, 6250, jnp.int32)
        _o = jnp.argsort(dst, stable=True)
        src = src[_o]
        dst = dst[_o]
        edge_attr_16 = 0.000254156 + 0.999948 * jax.random.normal(jax.random.fold_in(_gk, 12), (100000, 16), jnp.float32)
        edge_type_8 = jax.random.randint(jax.random.fold_in(_gk, 14), (100000,), 0, 8, jnp.int32)
        edge_weight1 = jax.random.uniform(jax.random.fold_in(_gk, 15), (100000, 1), jnp.float32, 0.0, 1)
        return (x, src, dst, edge_attr_16, edge_type_8, edge_weight1)
    x, src, dst, edge_attr_16, edge_type_8, edge_weight1 = _rec_inputs()

    def _L0_gnn_setup():
        import jax, jax.numpy as jnp
        import numpy as np
        N_NODES = 6250
        N_EDGES = 100000
        D_IN = 128
        D_OUT = 128
        EPS = 1e-12
        key = jax.random.key(seed)
        k1, k2, k3, k4, k5 = jax.random.split(key, 5)
        x = jax.random.normal(k1, (N_NODES, D_IN), dtype=jnp.float32)
        edge_index = jax.random.randint(k2, (2, N_EDGES), 0, N_NODES, dtype=jnp.int64)
        s = 1.0 / np.sqrt(D_IN)
        W_l = jax.random.uniform(k3, (D_IN, D_OUT), jnp.float32, -s, s)
        b_l = jax.random.uniform(k4, (D_OUT,), jnp.float32, -s, s)
        W_r = jax.random.uniform(k5, (D_IN, D_OUT), jnp.float32, -s, s)
        return {'x': x, 'edge_index': edge_index, 'W_l': W_l, 'b_l': b_l, 'W_r': W_r}
    _L0_gnn_all = _L0_gnn_setup()
    _L0_gnn_in = {k: v for k, v in _L0_gnn_all.items() if k in ('W_l', 'b_l', 'W_r')}
    del _L0_gnn_all

    def _L1_gnn_setup():
        import jax, jax.numpy as jnp
        import numpy as np
        N_NODES = 3125
        N_EDGES = 100000
        IN_FEAT = 128
        OUT_FEAT = 128
        NUM_RELS = 8
        key = jax.random.key(seed)
        k1, k2, k3, k4, k5, k6, k7 = jax.random.split(key, 7)
        x = jax.random.normal(k1, (N_NODES, IN_FEAT), dtype=jnp.float32)
        norm = jax.random.uniform(k2, (N_EDGES, 1), dtype=jnp.float32)
        src = jax.random.randint(k3, (N_EDGES,), 0, N_NODES)
        dst = jax.random.randint(k4, (N_EDGES,), 0, N_NODES)
        rel_type = jax.random.randint(k5, (N_EDGES,), 0, NUM_RELS)
        gain = float(np.sqrt(2.0))
        bound = gain * float(np.sqrt(6.0 / (IN_FEAT + OUT_FEAT)))
        weight = jax.random.uniform(k6, (NUM_RELS, IN_FEAT, OUT_FEAT), dtype=jnp.float32, minval=-bound, maxval=bound)
        bias = jax.random.uniform(k7, (OUT_FEAT,), dtype=jnp.float32, minval=-0.1, maxval=0.1)
        return {'x': x, 'norm': norm, 'weight': weight, 'bias': bias, 'src': src, 'dst': dst, 'rel_type': rel_type}
    _L1_gnn_all = _L1_gnn_setup()
    _L1_gnn_in = {k: v for k, v in _L1_gnn_all.items() if k in ('weight', 'bias')}
    del _L1_gnn_all

    def _L2_gnn_setup():
        import jax, jax.numpy as jnp
        import numpy as np
        N = 6250
        E = 100000
        ANN = 128
        HID = 128
        S = ANN + HID
        L = 5
        MLP_H = 256
        OUT = 128

        def _forward(x, edge_index, W, w_ih, w_hh, b_ih, b_hh, l0_w, l0_b, l1_w, l1_b):
            n = x.shape[0]
            s = W.shape[-1]
            src, dst = (edge_index[0], edge_index[1])
            h = jnp.pad(x, ((0, 0), (0, s - x.shape[-1])))

            def step(h, Wl):
                m = h @ Wl
                agg = jax.ops.segment_sum(m[src], dst, num_segments=n)
                gi = agg @ w_ih.T + b_ih
                gh = h @ w_hh.T + b_hh
                ir, iz, in_ = jnp.split(gi, 3, axis=-1)
                hr, hz, hn = jnp.split(gh, 3, axis=-1)
                r = jax.nn.sigmoid(ir + hr)
                z = jax.nn.sigmoid(iz + hz)
                ng = jnp.tanh(in_ + r * hn)
                h_new = (1.0 - z) * ng + z * h
                return (h_new, None)
            h, _ = jax.lax.scan(step, h, W)
            cat = jnp.concatenate([h, x], axis=-1)
            y = jax.nn.relu(cat @ l0_w.T + l0_b)
            y = jax.nn.relu(y @ l1_w.T + l1_b)
            return y
        key = jax.random.key(seed)
        ks = jax.random.split(key, 12)
        sc = 0.05
        return {'x': jax.random.normal(ks[0], (N, ANN), dtype=jnp.float32), 'edge_index': jax.random.randint(ks[1], (2, E), 0, N, dtype=jnp.int64), 'W': jax.random.normal(ks[2], (L, S, S), dtype=jnp.float32) * sc, 'w_ih': jax.random.normal(ks[3], (3 * S, S), dtype=jnp.float32) * sc, 'w_hh': jax.random.normal(ks[4], (3 * S, S), dtype=jnp.float32) * sc, 'b_ih': jax.random.normal(ks[5], (3 * S,), dtype=jnp.float32) * sc, 'b_hh': jax.random.normal(ks[6], (3 * S,), dtype=jnp.float32) * sc, 'l0_w': jax.random.normal(ks[7], (MLP_H, S + ANN), dtype=jnp.float32) * sc, 'l0_b': jax.random.normal(ks[8], (MLP_H,), dtype=jnp.float32) * sc, 'l1_w': jax.random.normal(ks[9], (OUT, MLP_H), dtype=jnp.float32) * sc, 'l1_b': jax.random.normal(ks[10], (OUT,), dtype=jnp.float32) * sc}
    _L2_gnn_all = _L2_gnn_setup()
    _L2_gnn_in = {k: v for k, v in _L2_gnn_all.items() if k in ('W', 'w_ih', 'w_hh', 'b_ih', 'b_hh', 'l0_w', 'l0_b', 'l1_w', 'l1_b')}
    del _L2_gnn_all

    def _L3_gnn_setup():
        import jax, jax.numpy as jnp
        import numpy as np
        N = 3125
        E = 50000
        D = 128
        DE = 16
        key = jax.random.key(seed)
        ks = jax.random.split(key, 12)

        def lin(k, fan_in, fan_out):
            bound = 1.0 / np.sqrt(fan_in)
            kw, kb = jax.random.split(k)
            W = jax.random.uniform(kw, (fan_in, fan_out), jnp.float32, -bound, bound)
            b = jax.random.uniform(kb, (fan_out,), jnp.float32, -bound, bound)
            return (W, b)
        x = jax.random.normal(ks[0], (N, D), jnp.float32)
        edge_index = jax.random.randint(ks[1], (2, E), 0, N, jnp.int64)
        edge_attr = jax.random.normal(ks[2], (E, DE), jnp.float32)
        eW1, eb1 = lin(ks[3], 2 * D + DE, D)
        eW2, eb2 = lin(ks[4], D, D)
        nW1, nb1 = lin(ks[5], 2 * D, D)
        nW2, nb2 = lin(ks[6], D, D)
        return {'x': x, 'edge_index': edge_index, 'edge_attr': edge_attr, 'eW1': eW1, 'eb1': eb1, 'eW2': eW2, 'eb2': eb2, 'nW1': nW1, 'nb1': nb1, 'nW2': nW2, 'nb2': nb2}
    _L3_gnn_all = _L3_gnn_setup()
    _L3_gnn_in = {k: v for k, v in _L3_gnn_all.items() if k in ('eW1', 'eb1', 'eW2', 'eb2', 'nW1', 'nb1', 'nW2', 'nb2')}
    del _L3_gnn_all
    return {'x': x, 'src': src, 'dst': dst, 'edge_attr_16': edge_attr_16, 'edge_type_8': edge_type_8, 'edge_weight1': edge_weight1, 'L0_gnn_W_l': _L0_gnn_in['W_l'], 'L0_gnn_b_l': _L0_gnn_in['b_l'], 'L0_gnn_W_r': _L0_gnn_in['W_r'], 'L1_gnn_weight': _L1_gnn_in['weight'], 'L1_gnn_bias': _L1_gnn_in['bias'], 'L2_gnn_W': _L2_gnn_in['W'], 'L2_gnn_w_ih': _L2_gnn_in['w_ih'], 'L2_gnn_w_hh': _L2_gnn_in['w_hh'], 'L2_gnn_b_ih': _L2_gnn_in['b_ih'], 'L2_gnn_b_hh': _L2_gnn_in['b_hh'], 'L2_gnn_l0_w': _L2_gnn_in['l0_w'], 'L2_gnn_l0_b': _L2_gnn_in['l0_b'], 'L2_gnn_l1_w': _L2_gnn_in['l1_w'], 'L2_gnn_l1_b': _L2_gnn_in['l1_b'], 'L3_gnn_eW1': _L3_gnn_in['eW1'], 'L3_gnn_eb1': _L3_gnn_in['eb1'], 'L3_gnn_eW2': _L3_gnn_in['eW2'], 'L3_gnn_eb2': _L3_gnn_in['eb2'], 'L3_gnn_nW1': _L3_gnn_in['nW1'], 'L3_gnn_nb1': _L3_gnn_in['nb1'], 'L3_gnn_nW2': _L3_gnn_in['nW2'], 'L3_gnn_nb2': _L3_gnn_in['nb2']}

def reference(x, src, dst, edge_attr_16, edge_type_8, edge_weight1, L0_gnn_W_l, L0_gnn_b_l, L0_gnn_W_r, L1_gnn_weight, L1_gnn_bias, L2_gnn_W, L2_gnn_w_ih, L2_gnn_w_hh, L2_gnn_b_ih, L2_gnn_b_hh, L2_gnn_l0_w, L2_gnn_l0_b, L2_gnn_l1_w, L2_gnn_l1_b, L3_gnn_eW1, L3_gnn_eb1, L3_gnn_eW2, L3_gnn_eb2, L3_gnn_nW1, L3_gnn_nb1, L3_gnn_nW2, L3_gnn_nb2):
    import jax
    import jax.numpy as jnp

    def _L0_gnn_ref(x, edge_index, W_l, b_l, W_r):
        import jax, jax.numpy as jnp
        import numpy as np
        N_NODES = 6250
        N_EDGES = 100000
        D_IN = 128
        D_OUT = 128
        EPS = 1e-12
        n = x.shape[0]
        src = edge_index[0]
        dst = edge_index[1]
        msg = x[src]
        summed = jax.ops.segment_sum(msg, dst, num_segments=n)
        cnt = jax.ops.segment_sum(jnp.ones((msg.shape[0],), x.dtype), dst, num_segments=n)
        mean = summed / jnp.maximum(cnt, 1.0)[:, None]
        out = mean @ W_l + b_l + x @ W_r
        norm = jnp.sqrt(jnp.sum(out * out, axis=-1, keepdims=True))
        return out / jnp.maximum(norm, EPS)

    def _L1_gnn_ref(x, norm, weight, bias, src, dst, rel_type):
        import jax, jax.numpy as jnp
        import numpy as np
        N_NODES = 3125
        N_EDGES = 100000
        IN_FEAT = 128
        OUT_FEAT = 128
        NUM_RELS = 8
        n_nodes = x.shape[0]
        hw = jnp.einsum('ni,rio->rno', x, weight)
        msg = hw[rel_type, src] * norm
        h = jax.ops.segment_sum(msg, dst, num_segments=n_nodes)
        h = jax.nn.relu(h + bias)
        return h

    def _L2_gnn_ref(x, edge_index, W, w_ih, w_hh, b_ih, b_hh, l0_w, l0_b, l1_w, l1_b):
        import jax, jax.numpy as jnp
        import numpy as np
        N = 6250
        E = 100000
        ANN = 128
        HID = 128
        S = ANN + HID
        L = 5
        MLP_H = 256
        OUT = 128

        def _forward(x, edge_index, W, w_ih, w_hh, b_ih, b_hh, l0_w, l0_b, l1_w, l1_b):
            n = x.shape[0]
            s = W.shape[-1]
            src, dst = (edge_index[0], edge_index[1])
            h = jnp.pad(x, ((0, 0), (0, s - x.shape[-1])))

            def step(h, Wl):
                m = h @ Wl
                agg = jax.ops.segment_sum(m[src], dst, num_segments=n)
                gi = agg @ w_ih.T + b_ih
                gh = h @ w_hh.T + b_hh
                ir, iz, in_ = jnp.split(gi, 3, axis=-1)
                hr, hz, hn = jnp.split(gh, 3, axis=-1)
                r = jax.nn.sigmoid(ir + hr)
                z = jax.nn.sigmoid(iz + hz)
                ng = jnp.tanh(in_ + r * hn)
                h_new = (1.0 - z) * ng + z * h
                return (h_new, None)
            h, _ = jax.lax.scan(step, h, W)
            cat = jnp.concatenate([h, x], axis=-1)
            y = jax.nn.relu(cat @ l0_w.T + l0_b)
            y = jax.nn.relu(y @ l1_w.T + l1_b)
            return y
        return _forward(x, edge_index, W, w_ih, w_hh, b_ih, b_hh, l0_w, l0_b, l1_w, l1_b)

    def _L3_gnn_ref(x, edge_index, edge_attr, eW1, eb1, eW2, eb2, nW1, nb1, nW2, nb2):
        import jax, jax.numpy as jnp
        import numpy as np
        N = 3125
        E = 50000
        D = 128
        DE = 16
        row, col = (edge_index[0], edge_index[1])
        edge_input = jnp.concatenate([x[row], x[col], edge_attr], axis=-1)
        h = jax.nn.silu(edge_input @ eW1 + eb1)
        m_ij = jax.nn.silu(h @ eW2 + eb2)
        agg = jax.ops.segment_sum(m_ij, row, num_segments=x.shape[0])
        node_input = jnp.concatenate([x, agg], axis=-1)
        update = jax.nn.silu(node_input @ nW1 + nb1) @ nW2 + nb2
        return x + update
    edge_index = jnp.stack([src, dst])
    x = _layernorm(x + _L0_gnn_ref(x, edge_index, L0_gnn_W_l, L0_gnn_b_l, L0_gnn_W_r), axis=-1)
    x = _layernorm(x + _L1_gnn_ref(x, edge_weight1, L1_gnn_weight, L1_gnn_bias, src, dst, edge_type_8), axis=-1)
    x = _layernorm(x + _L2_gnn_ref(x, edge_index, L2_gnn_W, L2_gnn_w_ih, L2_gnn_w_hh, L2_gnn_b_ih, L2_gnn_b_hh, L2_gnn_l0_w, L2_gnn_l0_b, L2_gnn_l1_w, L2_gnn_l1_b), axis=-1)
    x = _layernorm(x + _L3_gnn_ref(x, edge_index, edge_attr_16, L3_gnn_eW1, L3_gnn_eb1, L3_gnn_eW2, L3_gnn_eb2, L3_gnn_nW1, L3_gnn_nb1, L3_gnn_nW2, L3_gnn_nb2), axis=-1)
    return x

_drawn_inputs = setup_inputs


def setup_inputs(seed=0):
    import zlib

    import numpy as np

    out = dict(_drawn_inputs(seed))
    spreads = {}
    factors = {'edge_attr_16': 8.0, 'L2_gnn_l0_b': 3.191, 'L3_gnn_eb1': 8.0, 'L3_gnn_nb1': 8.0}
    for name, (base, spread) in spreads.items():
        noise = np.random.default_rng([zlib.crc32(name.encode()), seed]).standard_normal(out[name].shape)
        drawn = base * np.exp(spread * noise) if base else spread * noise
        out[name] = jnp.asarray(drawn.astype(out[name].dtype))
    for name, factor in factors.items():
        out[name] = (out[name] * factor).astype(out[name].dtype)
    return out
```

```python
from contextlib import ExitStack

import concourse.bass as bass
from concourse import mybir

F32 = mybir.dt.float32
I32 = mybir.dt.int32
ALU = mybir.AluOpType
ACT = mybir.ActivationFunctionType
AX = mybir.AxisListType

D = 128
LANES = 125
TILES = 50
NODES = LANES * TILES
PAIRS = TILES // 2
PAIR = 2 * LANES
EDGE_COLS = 800
RELS = 8
ATTR = 16
HALF = 4
RING = 2 * HALF
SLOT = 128
CHUNKS = -(-((LANES * EDGE_COLS + TILES * (SLOT - 1)) // SLOT) // RING) * RING
TURNS = CHUNKS // RING
DEEP = 4
PAD_CHUNKS = CHUNKS + HALF
TILE_COLS = 7
REC1 = 4
REC2 = 2 + ATTR
STATE = 2 * D
GATES = 3 * STATE
LN_EPS = 1e-5
NORM_EPS = 1e-12


class Steps:

    def __init__(self, eng, sem, start=0):
        self.eng, self.sem, self.done = eng, sem, start

    def __call__(self, ins):
        ins.then_inc(self.sem, 1)
        self.done = self.done + 1
        self.eng.wait_ge(self.sem, self.done)


def semaphores(nc, c):
    made = []

    def clear():
        nc.clear_and_free_semaphores(made)
        nc.all_engine_barrier()

    def sem(name):
        made.append(nc.alloc_semaphore(name))
        return made[-1]
    c.callback(clear)
    return sem


def tables(nc, c):
    def dram(name, shape, dt=F32):
        return nc.dram_tensor(f"{name}_table", shape, dt, kind="Internal").ap()
    return dict(
        slots1=dram("slots1", (SLOT * CHUNKS, REC1)),
        slots2=dram("slots2", (SLOT * CHUNKS, REC2)),
        tile_of_chunk1=dram("tile_of_chunk1", (SLOT * TILE_COLS,), I32),
        tile_of_chunk2=dram("tile_of_chunk2", (SLOT * TILE_COLS,), I32),
        x2=dram("x2", (NODES, D)),
        rel=dram("rel", (NODES * RELS, D)),
        state=dram("state", (NODES, STATE)),
        xcol=dram("xcol", (NODES, D)),
    )


def constants(nc, K):
    with ExitStack() as c:
        sem = semaphores(nc, c)
        made, cast = sem("const_made"), sem("const_cast")
        iota_i = c.enter_context(nc.sbuf_tensor("iota_i", [128, 128], I32))
        chunk_i = c.enter_context(nc.sbuf_tensor("chunk_i", [128, TILE_COLS], I32))
        block = c.enter_context(nc.Block())

        @block.gpsimd
        def _(pool):
            pool.iota(iota_i[:], pattern=[[1, 128]], base=0, channel_multiplier=0).then_inc(made, 1)
            pool.iota(chunk_i[:], pattern=[[1, TILE_COLS]], base=0, channel_multiplier=TILE_COLS).then_inc(made, 1)
            pool.memset(K["ident"][:], 0.0).then_inc(made, 1)
            pool.memset(K["ones"][:], 1.0).then_inc(made, 1)
            pool.memset(K["eps"][:], LN_EPS).then_inc(made, 1)
            pool.wait_ge(made, 5)
            pool.affine_select(out=K["ident"][:], in_=K["ident"][:], compare_op=ALU.not_equal, fill=1.0,
                               base=0, pattern=[[-1, 128]], channel_multiplier=1).then_inc(made, 1)
            pool.affine_select(out=K["before"][:], in_=K["ones"][:], compare_op=ALU.is_gt, fill=0.0,
                               base=0, pattern=[[1, 128]], channel_multiplier=-1).then_inc(made, 1)

        @block.vector
        def _(dve):
            dve.wait_ge(made, 2)
            dve.tensor_copy(K["iota_row"][:], iota_i[:]).then_inc(cast, 1)
            dve.tensor_copy(K["chunk_no"][:], chunk_i[:]).then_inc(cast, 1)


def sort_edges(nc, K, T, scattered, src, dst, edge_attr, edge_type, edge_weight):
    with ExitStack() as c:
        def sb(name, shape, dt=F32):
            return c.enter_context(nc.sbuf_tensor(name, shape, dt))

        sem = semaphores(nc, c)
        L, C = LANES, EDGE_COLS
        key_i = [sb("dst_i", [L, C], I32), sb("src_i", [L, C], I32)]
        type_i = sb("type_i", [L, C], I32)
        key = [sb("dst_f", [L, C]), sb("src_f", [L, C])]
        bucket = sb("bucket", [L, C])
        lane = [sb("dst_lane", [L, C]), sb("src_lane", [L, C])]
        row = [sb("dst_row", [L, C]), sb("src_row", [L, C])]
        tmp = sb("tmp", [L, C])
        tmp_i = sb("tmp_i", [L, C], I32)
        ones_c = sb("ones_c", [L, C])
        norm = sb("norm", [L, C])
        rel_row = sb("rel_row", [L, C])
        attr = sb("attr", [L, C * ATTR])
        hist = sb("hist", [L, TILES])
        total = sb("total", [128, TILES])
        total_i = sb("total_i", [128, TILES], I32)
        chunks = sb("chunks", [128, TILES])
        chunks_end = sb("chunks_end", [128, TILES])
        base = sb("base", [L, TILES])
        over = sb("over", [128, TILE_COLS, TILES])
        tile_f = sb("tile_f", [128, TILE_COLS])
        tile_i = [sb("tile1_i", [128, TILE_COLS], I32), sb("tile2_i", [128, TILE_COLS], I32)]
        fill2 = sb("fill2", [128, CHUNKS // 8, REC2])
        row_stage = sb("row_stage", [L, RING], I32)
        rec1_stage = sb("rec1_stage", [L, RING, REC1])
        rec2_stage = sb("rec2_stage", [L, RING, REC2])
        count_ps = c.enter_context(nc.psum_tensor("count_ps", [128, 2, 256], F32))

        keys_in, rest_in = sem("keys_in"), sem("rest_in")
        filled, filled_rows = sem("filled"), sem("filled_rows")
        step_s = sem("dve_step")
        hist_done, counted = sem("hist_done"), sem("counted")
        tile_done, tile_out = sem("tile_done"), sem("tile_out")
        rows_done = sem("rows_done")
        staged, stage_step = sem("staged"), sem("stage_step")
        issued, passed = sem("issued"), sem("passed")
        block = c.enter_context(nc.Block())
        SC_TURNS = EDGE_COLS // RING

        @block.sync
        def _(sp):
            for t, a in ((key_i[0], dst), (key_i[1], src)):
                sp.dma_start(t[:], a.rearrange("(p c) -> p c", p=L)).then_inc(keys_in, 16)
            sp.dma_start(type_i[:], edge_type.rearrange("(p c) -> p c", p=L)).then_inc(rest_in, 16)
            sp.dma_start(norm[:], edge_weight.rearrange("(p c) o -> p (c o)", p=L)).then_inc(rest_in, 16)
            sp.dma_start(attr[:], edge_attr.rearrange("(p c) k -> p (c k)", p=L)).then_inc(rest_in, 16)
            sp.wait_ge(filled, 2)
            sp.dma_start(T["slots1"].rearrange("(p q) w -> p (q w)", p=128),
                         K["rec"][:, 0:CHUNKS, :].rearrange("p q w -> p (q w)")).then_inc(filled_rows, 16)
            sp.wait_ge(filled, 4)
            slots2 = T["slots2"].rearrange("(p e q) w -> p e (q w)", p=128, e=8)
            for e in range(8):
                sp.dma_start(slots2[:, e, :], fill2[:].rearrange("p q w -> p (q w)")).then_inc(filled_rows, 16)
            for k in range(2):
                sp.wait_ge(tile_done, k + 1)
                sp.dma_start(T[f"tile_of_chunk{k + 1}"].rearrange("(p j) -> p j", p=128), tile_i[k][:])\
                    .then_inc(tile_out, 16)
            sp.wait_ge(tile_out, 32)

        @block.gpsimd
        def _(pool):
            pool.memset(K["rec"][:], 0.0).then_inc(filled, 1)
            pool.wait_ge(filled, 1)
            pool.memset(K["rec"][:, :, 1:2], -1.0).then_inc(filled, 1)
            pool.memset(fill2[:], 0.0).then_inc(filled, 1)
            pool.wait_ge(filled, 3)
            pool.memset(fill2[:, :, 1:2], -1.0).then_inc(filled, 1)
            pool.wait_ge(filled_rows, 16 * 9)
            for k, (table, stage) in enumerate(((T["slots1"], rec1_stage), (T["slots2"], rec2_stage))):
                with pool.Fori(0, SC_TURNS) as i:
                    for r in range(RING):
                        if r % HALF == 0:
                            pool.wait_ge(staged, i * 2 + (k * SC_TURNS * 2 + r // HALF + 1))
                            pool.sem_inc(issued, 1)
                        pool.indirect_dma_start(
                            out=table, out_offset=bass.IndirectOffsetOnAxis(ap=row_stage[:, r:r + 1], axis=0),
                            in_=stage[:, r, :], in_offset=None).then_inc(scattered[k][r], 16)
            for k in range(2):
                for r in range(RING):
                    pool.wait_ge(scattered[k][r], 16 * SC_TURNS)

        @block.scalar
        def _(act):
            def stage(k, i, h, first):
                s = slice(h * HALF, h * HALF + HALF)
                cols = bass.ds(i * RING + h * HALF, HALF)
                if first and k == 1:
                    for r in range(h * HALF, h * HALF + HALF):
                        act.wait_ge(scattered[0][r], 16 * SC_TURNS)
                if not first:
                    for r in range(h * HALF, h * HALF + HALF):
                        act.wait_ge(scattered[k][r], i * 16)
                act.copy(row_stage[:, s], row[k][:, cols]).then_inc(stage_step, 1)
                if k == 0:
                    for w, t in enumerate((key[1], lane[0], rel_row)):
                        act.copy(rec1_stage[:, s, w], t[:, cols]).then_inc(stage_step, 1)
                    act.copy(rec1_stage[:, s, 3], norm[:, cols]).then_inc(staged, 1)
                else:
                    for w, t in enumerate((key[0], lane[1])):
                        act.copy(rec2_stage[:, s, w], t[:, cols]).then_inc(stage_step, 1)
                    act.copy(rec2_stage[:, s, 2:REC2],
                             attr[:, bass.ds((i * RING + h * HALF) * ATTR, HALF * ATTR)]
                             .rearrange("p (c k) -> p c k", k=ATTR)).then_inc(staged, 1)

            act.wait_ge(rest_in, 48)
            for k in range(2):
                act.wait_ge(rows_done, k + 1)
                for h in range(2):
                    stage(k, 0, h, True)
                with act.Fori(1, SC_TURNS) as i:
                    for h in range(2):
                        stage(k, i, h, False)

        @block.tensor
        def _(pe):
            for k in range(2):
                pe.wait_ge(hist_done, k + 1)
                pe.matmul(count_ps[0:L, 0, 0:TILES], K["before"][0:L, 0:L], hist[:], start=True, stop=True)
                pe.matmul(count_ps[:, 1, 0:TILES], K["ones"][0:L, :], hist[:], start=True, stop=True)\
                    .then_inc(counted, 1)

        @block.vector
        def _(dve):
            step = Steps(dve, step_s)
            step(dve.memset(ones_c[:], 1.0))
            dve.wait_ge(keys_in, 32)
            step(dve.tensor_copy(key[0][:], key_i[0][:]))
            step(dve.tensor_copy(key[1][:], key_i[1][:]))
            dve.wait_ge(rest_in, 48)
            step(dve.tensor_copy(tmp[:], type_i[:]))
            step(dve.scalar_tensor_tensor(rel_row[:], key[1][:], float(RELS), tmp[:], ALU.mult, ALU.add))
            for k in range(2):
                step(dve.tensor_scalar(tmp_i[:], key[k][:], 1.0 / TILES, -0.49, ALU.mult, ALU.add))
                step(dve.tensor_copy(lane[k][:], tmp_i[:]))
                step(dve.scalar_tensor_tensor(bucket[:], lane[k][:], -float(TILES), key[k][:], ALU.mult, ALU.add))
                step(dve.tensor_single_scalar(tmp[:], bucket[:], 0.0, ALU.is_lt))
                step(dve.tensor_tensor(lane[k][:], lane[k][:], tmp[:], ALU.subtract))
                step(dve.scalar_tensor_tensor(bucket[:], tmp[:], float(TILES), bucket[:], ALU.mult, ALU.add))
                step(dve.tensor_single_scalar(tmp[:], bucket[:], float(TILES), ALU.is_ge))
                step(dve.tensor_tensor(lane[k][:], lane[k][:], tmp[:], ALU.add))
                step(dve.scalar_tensor_tensor(bucket[:], tmp[:], -float(TILES), bucket[:], ALU.mult, ALU.add))
                at = step.done
                with dve.Fori(0, TILES) as t:
                    step.done = at + t
                    step(dve.tensor_scalar(tmp[:], bucket[:], K["iota_row"][0:L, bass.ds(t, 1)], 0.0,
                                           ALU.is_equal, ALU.add, accum_out=hist[:, bass.ds(t, 1)]))
                step.done = at + TILES
                dve.sem_inc(hist_done, 1)
                dve.wait_ge(counted, k + 1)
                step(dve.tensor_scalar(total_i[:], count_ps[:, 1, 0:TILES], float(SLOT - 1), None, ALU.add))
                step(dve.tensor_scalar(total_i[:], total_i[:], 7, None, ALU.arith_shift_right))
                step(dve.tensor_copy(chunks[:], total_i[:]))
                step(dve.tensor_tensor_scan(chunks_end[:], K["ones"][:, 0:TILES], chunks[:], 0.0, ALU.mult, ALU.add))
                step(dve.tensor_tensor(total[:], chunks_end[:], chunks[:], ALU.subtract))
                step(dve.tensor_scalar(total[:], total[:], float(SLOT), -1.0, ALU.mult, ALU.add))
                step(dve.tensor_tensor(base[:], total[0:L, :], count_ps[0:L, 0, 0:TILES], ALU.add))
                step(dve.tensor_tensor(
                    over[:], chunks_end[:, None, :].to_broadcast([128, TILE_COLS, TILES]),
                    K["chunk_no"][:, :, None].to_broadcast([128, TILE_COLS, TILES]), ALU.is_le))
                step(dve.tensor_reduce(tile_f[:], over[:], AX.X, ALU.add))
                step(dve.tensor_single_scalar(tile_i[k][:], tile_f[:], float(TILES - 1), ALU.min))
                dve.sem_inc(tile_done, 1)
                at = step.done
                with dve.Fori(0, TILES) as t:
                    step.done = at + t * 3
                    step(dve.tensor_scalar(tmp[:], bucket[:], K["iota_row"][0:L, bass.ds(t, 1)], None, ALU.is_equal))
                    step(dve.tensor_tensor_scan(norm_free(key_i[0]), ones_c[:], tmp[:],
                                                base[:, bass.ds(t, 1)], ALU.mult, ALU.add))
                    dve.sem_inc(passed, 1)
                    step(dve.copy_predicated(row[k][:], tmp[:].bitcast(I32), norm_free(key_i[0])))
                step.done = at + TILES * 3
                step(dve.tensor_copy(tmp_i[:], row[k][:]))
                step(dve.tensor_scalar(key_i[0][:], tmp_i[:], 7, None, ALU.arith_shift_right))
                step(dve.tensor_scalar(tmp_i[:], tmp_i[:], SLOT - 1, None, ALU.bitwise_and))
                step(dve.tensor_copy(bucket[:], key_i[0][:]))
                step(dve.tensor_copy(tmp[:], tmp_i[:]))
                step(dve.scalar_tensor_tensor(row[k][:], tmp[:], float(CHUNKS), bucket[:], ALU.mult, ALU.add))
                dve.sem_inc(rows_done, 1)


def norm_free(t):
    return t[:].bitcast(F32)


def load_slots(nc, K, T):
    with ExitStack() as c:
        loaded = semaphores(nc, c)("slots_loaded")
        block = c.enter_context(nc.Block())

        @block.sync
        def _(sp):
            sp.dma_start(K["rec"][:, 0:CHUNKS, :].rearrange("p q w -> p (q w)"),
                         T["slots1"].rearrange("(p q) w -> p (q w)", p=128)).then_inc(loaded, 16)
            for k in (1, 2):
                sp.dma_start(K[f"tile{k}"][:], T[f"tile_of_chunk{k}"][0:CHUNKS]
                             .rearrange("(a q) -> a q", a=1)).then_inc(loaded, 16)
            sp.wait_ge(loaded, 48)


class GatherSems:
    def __init__(self, make, row_in, name):
        self.name = name

        def sem(n):
            return make(f"{name}_{n}")
        self.idx_staged = sem("idx_staged")
        self.issued = sem("issued")
        self.row_in = row_in
        self.onehot = sem("onehot")
        self.masked = sem("masked")
        self.summed = sem("summed")
        self.psum_free = sem("psum_free")
        self.zeroed = sem("zeroed")
        self.started = sem("started")


def gather_sum(nc, K, S, rnd, table, word, width, by_row=False, weighted=False, count=False):
    NPS = 4
    onehot, rows, idx = K["onehot"], K["rows"], K["idx"]
    agg, rec = K["agg"], K["rec"]
    halves = width // D
    agg_t = agg[:, 0:halves * NODES].rearrange("p (s n) -> p s n", s=halves)
    with ExitStack() as c:
        prod = [c.enter_context(nc.psum_tensor(f"{S.name}_prod{b}", [128, 512], F32)) for b in range(NPS)]
        block = c.enter_context(nc.Block())
        s_base = rnd * (CHUNKS + RING)
        f_base = rnd * (CHUNKS + NPS)
        z_base = rnd * 1

        @block.scalar
        def _(act):
            act.wait_ge(S.summed, s_base + RING)
            act.sem_inc(S.started, 1)
            with act.Fori(0, TURNS) as i:
                for h in range(2):
                    act.wait_ge(S.summed, s_base + i * RING + (h * HALF + HALF))
                    act.copy(idx[:, h * HALF:h * HALF + HALF],
                             rec[:, bass.ds(i * RING + h * HALF, HALF), word]).then_inc(S.idx_staged, 1)

        @block.gpsimd
        def _(pool):
            with pool.Fori(0, TURNS) as i:
                for r in range(RING):
                    if r % HALF == 0:
                        pool.wait_ge(S.idx_staged, rnd * (TURNS * 2) + i * 2 + (r // HALF + 1))
                        pool.sem_inc(S.issued, 1)
                    pool.indirect_dma_start(
                        out=rows[:, r, 0:width], out_offset=None, in_=table,
                        in_offset=bass.IndirectOffsetOnAxis(ap=idx[:, r:r + 1], axis=0)).then_inc(S.row_in[r], 16)

        @block.tensor
        def _(pe):
            pe.sem_inc(S.summed, RING)
            with pe.Fori(0, TURNS) as i:
                for r in range(RING):
                    if r % HALF == 0:
                        pe.wait_ge(S.onehot, rnd * (TURNS * 2 + 1) + i * 2 + (r // HALF + 1))
                    pe.wait_ge(S.row_in[r], (rnd * TURNS + i) * 16 + 16)
                    pe.wait_ge(S.psum_free, f_base + i * RING + (r + 1))
                    p = prod[r % NPS]
                    oh = onehot[:, r // HALF, r % HALF, :]
                    if count:
                        pe.matmul(p[0:LANES, 2 * LANES:2 * LANES + 1], oh, K["ones"][:, 0:1], start=True, stop=True)
                    if by_row:
                        pe.matmul(p[0:LANES, 0:D], oh, rows[:, r, 0:D], start=True, stop=True)\
                            .then_inc(S.summed, 1)
                    else:
                        for s in range(halves):
                            last = pe.matmul(p[:, s * LANES:(s + 1) * LANES], rows[:, r, s * D:(s + 1) * D], oh,
                                             start=True, stop=True)
                        last.then_inc(S.summed, 1)

        @block.vector
        def _(dve):
            def build(chunk, h, n):
                lanes = rec[:, bass.ds(chunk, HALF), 1:2].to_broadcast([128, HALF, LANES])
                oh = onehot[:, h, :, :]
                ins = dve.tensor_tensor(oh, K["iota_row"][:, None, 0:LANES].to_broadcast([128, HALF, LANES]),
                                        lanes, ALU.is_equal)
                if weighted:
                    ins.then_inc(S.masked, 1)
                    dve.wait_ge(S.masked, n)
                    ins = dve.tensor_tensor(oh, oh, rec[:, bass.ds(chunk, HALF), 3:4]
                                            .to_broadcast([128, HALF, LANES]), ALU.mult)
                ins.then_inc(S.onehot, 1)

            dve.memset(agg[:], 0.0).then_inc(S.zeroed, 1)
            if count:
                dve.memset(K["cnt"][:], 0.0).then_inc(S.zeroed, 1)
            dve.sem_inc(S.psum_free, NPS)
            build(0, 0, 1)
            dve.wait_ge(S.zeroed, z_base + (2 if count else 1))
            dve.sem_inc(S.started, 1)
            with dve.Fori(0, TURNS) as i:
                for h in range(2):
                    dve.wait_ge(S.summed, s_base + i * RING + (h * HALF + RING))
                    build(i * RING + (h * HALF + HALF), 1 - h, i * 2 + (h + 2))
                    for r in range(h * HALF, h * HALF + HALF):
                        tile = dve.value_load(K["tile1"][0:1, bass.ds(i * RING + r, 1)],
                                              min_val=0, max_val=TILES - 1)
                        dve.wait_ge(S.summed, s_base + i * RING + (r + RING + 1))
                        dve.wait_ge(S.psum_free, f_base + i * RING + (r + NPS))
                        p = prod[r % NPS]
                        if count:
                            dve.tensor_tensor(K["cnt"][:, bass.ds(tile, 1)], K["cnt"][:, bass.ds(tile, 1)],
                                              p[0:LANES, 2 * LANES:2 * LANES + 1], ALU.add)
                        if by_row:
                            a = agg[0:LANES, bass.ds(tile * D, D)]
                            dve.tensor_tensor(a, a, p[0:LANES, 0:D], ALU.add).then_inc(S.psum_free, 1)
                        else:
                            a = agg_t[:, :, bass.ds(tile * LANES, LANES)]
                            dve.tensor_tensor(a, a, p[:, 0:halves * LANES]
                                              .rearrange("p (s n) -> p s n", s=halves), ALU.add)\
                                .then_inc(S.psum_free, 1)


def rows_of(area, at):
    return area[0:LANES, at:at + TILES * D].rearrange("p (t f) -> p t f", t=TILES)


def transposed(area, halves):
    return area[:, 0:halves * NODES].rearrange("p (s n) -> p s n", s=halves)


ROWS_A, ROWS_B = 0, TILES * D


class Norm:

    def __init__(self, sb, sem):
        self.stats, self.mean_var, self.rstd = sb("stats", [LANES, 2, 6]), sb("mv", [LANES, 2, 2]), sb("rstd", [LANES, 2])
        self.std = sb("std", [LANES, 2])
        self.var_ok, self.std_ok, self.dve_passed = sem("var_ok"), sem("std_ok"), sem("dve_passed")


def layer_norm(dve, step, g, out, y, norm):
    for j in range(2):
        ins = dve.bn_stats(norm.stats[:, j, :], y[:, j, :])
    step(ins)
    dve.sem_inc(norm.dve_passed, 1)
    for j in range(2):
        ins = dve.bn_aggr(norm.mean_var[:, j, :], norm.stats[:, j, :])
    ins.then_inc(norm.var_ok, 1)
    dve.wait_ge(norm.std_ok, g + 1)
    step(dve.reciprocal(norm.rstd[:], norm.std[:]))
    for j in range(2):
        ins = dve.tensor_scalar(out[:, j, :], y[:, j, :], norm.mean_var[:, j, 0:1], norm.rstd[:, j:j + 1],
                                ALU.subtract, ALU.mult)
    step(ins)


def deviation(act, K, g, norm):
    act.wait_ge(norm.var_ok, g + 1)
    act.activation(norm.std[:], norm.mean_var[:, :, 1], ACT.Sqrt, bias=K["eps"][0:LANES, :]).then_inc(norm.std_ok, 1)


LN_STEPS = 3


def phase(nc, name):
    c = ExitStack()

    def sb(n, shape, dt=F32):
        return c.enter_context(nc.sbuf_tensor(f"{name}_{n}", shape, dt))

    make = semaphores(nc, c)

    def sem(n):
        return make(f"{name}_{n}")

    def bank(n):
        return c.enter_context(nc.psum_tensor(f"{name}_{n}", [128, 512], F32))
    return c, sb, sem, bank


def layer0_nodes(nc, K, T, x, w_l, b_l, w_r, rel_weight):
    c, sb, sem, bank = phase(nc, "l0")
    with c:
        wl, wr, bl = sb("wl", [D, D]), sb("wr", [D, D]), sb("bl", [1, D])
        relw = sb("relw", [D, RELS * D])
        xs, aggs = sb("xs", [LANES, 2, D]), sb("aggs", [D, PAIR])
        xt, x1t = sb("xt", [D, PAIR]), sb("x1t", [D, PAIR])
        inv = sb("inv", [LANES, TILES])
        o, sq, y, x1 = (sb(n, [LANES, 2, D]) for n in ("o", "sq", "y", "x1"))
        ss, l2, inv_norm = sb("ss", [LANES, 2]), sb("norm", [LANES, 2]), sb("inv_norm", [LANES, 2])
        norm = Norm(sb, sem)
        relrow = sb("relrow", [LANES, 2, RELS * D])
        xt_ps, mean_ps, self_ps, x1t_ps = bank("xt_ps"), bank("mean_ps"), bank("self_ps"), bank("x1t_ps")
        rel_ps = [bank(f"rel_ps{i}") for i in range(4)]
        loaded, step_s, ss_ok, norm_ok = sem("loaded"), sem("step"), sem("ss_ok"), sem("norm_ok")
        staged = sem("staged")
        xt_ps_ok, xt_ok = sem("xt_ps_ok"), sem("xt_ok")
        sums_ok, sums_used = sem("sums_ok"), sem("sums_used")
        x1_ok, x1_kept = sem("x1_ok"), sem("x1_kept")
        x1t_ps_ok, x1t_ok = sem("x1t_ps_ok"), sem("x1t_ok")
        rel_ps_ok, rel_ok = sem("rel_ps_ok"), sem("rel_ok")
        relrow_free, stored = sem("relrow_free"), sem("stored")
        block = c.enter_context(nc.Block())
        xrows, x1rows = rows_of(K["state"], ROWS_A), rows_of(K["state"], ROWS_B)
        agg = K["agg"]

        @block.sync
        def _(sp):
            sp.dma_start(K["state"][0:LANES, 0:TILES * D], x.rearrange("(p t) f -> p (t f)", p=LANES))\
                .then_inc(loaded, 16)
            sp.dma_start(wl[:], w_l).then_inc(loaded, 16)
            sp.dma_start(wr[:], w_r).then_inc(loaded, 16)
            sp.dma_start(bl[:], b_l.rearrange("(a f) -> a f", a=1)).then_inc(loaded, 16)
            for r in range(RELS):
                sp.dma_start(relw[:, r * D:(r + 1) * D], rel_weight[r]).then_inc(loaded, 16)
            sp.sem_inc(relrow_free, 1)
            with sp.Fori(0, PAIRS) as g:
                sp.wait_ge(rel_ok, g + 2)
                sp.dma_start(T["rel"].rearrange("(p t r) f -> p t (r f)", p=LANES, r=RELS)[:, bass.ds(g * 2, 2), :],
                             relrow[:]).then_inc(stored, 16)
                sp.wait_ge(stored, g * 16 + 16)
                sp.sem_inc(relrow_free, 1)

        @block.gpsimd
        def _(pool):
            def stage(g):
                pool.tensor_copy(xs[:], xrows[:, bass.ds(g * 2, 2), :]).then_inc(staged, 1)
                pool.tensor_copy(aggs[:], agg[:, bass.ds(g * PAIR, PAIR)]).then_inc(staged, 1)

            pool.wait_ge(loaded, 16 * 12)
            pool.sem_inc(x1_kept, 1)
            stage(0)
            with pool.Fori(0, PAIRS - 1) as g:
                pool.wait_ge(sums_ok, g + 1)
                pool.wait_ge(x1_ok, g + 1)
                pool.tensor_copy(x1rows[:, bass.ds(g * 2, 2), :], x1[:]).then_inc(x1_kept, 1)
                stage(g + 1)
            pool.wait_ge(x1_ok, PAIRS)
            pool.tensor_copy(x1rows[:, TILES - 2:TILES, :], x1[:]).then_inc(x1_kept, 1)

        @block.tensor
        def _(pe):
            def front(g, first):
                pe.wait_ge(staged, g * 2 + 2)
                for j in range(2):
                    last = pe.transpose(xt_ps[:, j * LANES:(j + 1) * LANES], xs[:, j, :],
                                        K["ident"][0:LANES, 0:LANES])
                last.then_inc(xt_ps_ok, 1)
                if not first:
                    pe.wait_ge(sums_used, g)
                for j in range(2):
                    pe.matmul(mean_ps[0:LANES, j * D:(j + 1) * D], aggs[:, j * LANES:(j + 1) * LANES], wl[:],
                              start=True, stop=True)
                pe.wait_ge(xt_ok, g + 1)
                for j in range(2):
                    out = self_ps[0:LANES, j * D:(j + 1) * D]
                    pe.matmul(out, xt[:, j * LANES:(j + 1) * LANES], wr[:], start=True, stop=False)
                    last = pe.matmul(out, K["ones"][0:1, 0:LANES], bl[:], start=False, stop=True)
                last.then_inc(sums_ok, 1)

            def back(g):
                pe.wait_ge(x1_ok, g + 1)
                for j in range(2):
                    last = pe.transpose(x1t_ps[:, j * LANES:(j + 1) * LANES], x1[:, j, :],
                                        K["ident"][0:LANES, 0:LANES])
                last.then_inc(x1t_ps_ok, 1)
                pe.wait_ge(x1t_ok, g + 1)
                pe.wait_ge(rel_ok, g + 1)
                for j in range(2):
                    for h in range(2):
                        last = pe.matmul(rel_ps[2 * j + h][0:LANES, :], x1t[:, j * LANES:(j + 1) * LANES],
                                         relw[:, h * 512:(h + 1) * 512], start=True, stop=True)
                last.then_inc(rel_ps_ok, 1)

            pe.wait_ge(loaded, 16 * 12)
            pe.sem_inc(x1t_ps_ok, 1)
            front(0, True)
            with pe.Fori(0, PAIRS - 1) as g:
                front(g + 1, False)
                back(g)
            back(PAIRS - 1)

        @block.scalar
        def _(act):
            def copy_xt(g):
                act.wait_ge(xt_ps_ok, g + 1)
                act.copy(xt[:], xt_ps[:, 0:PAIR]).then_inc(xt_ok, 1)

            def norms(g):
                act.wait_ge(ss_ok, g + 1)
                act.activation(l2[:], ss[:], ACT.Sqrt).then_inc(norm_ok, 1)
                deviation(act, K, g, norm)

            def copy_rel(g):
                act.wait_ge(x1t_ps_ok, g + 2)
                act.copy(x1t[:], x1t_ps[:, 0:PAIR]).then_inc(x1t_ok, 1)
                act.wait_ge(rel_ps_ok, g + 1)
                act.wait_ge(relrow_free, g + 1)
                for q in range(4):
                    last = act.copy(relrow[:, q // 2, (q % 2) * 512:(q % 2 + 1) * 512], rel_ps[q][0:LANES, :])
                last.then_inc(rel_ok, 1)

            act.sem_inc(rel_ok, 1)
            copy_xt(0)
            with act.Fori(0, PAIRS - 1) as g:
                norms(g)
                copy_xt(g + 1)
                copy_rel(g)
            norms(PAIRS - 1)
            copy_rel(PAIRS - 1)

        @block.vector
        def _(dve):
            step = Steps(dve, step_s)
            step(dve.tensor_single_scalar(inv[:], K["cnt"][:], 1.0, ALU.max))
            step(dve.reciprocal(inv[:], inv[:]))
            at = step.done
            per_pair = 6 + LN_STEPS
            with dve.Fori(0, PAIRS) as g:
                step.done = at + g * per_pair
                dve.wait_ge(sums_ok, g + 1)
                for j in range(2):
                    ins = dve.tensor_scalar(o[:, j, :], mean_ps[0:LANES, j * D:(j + 1) * D],
                                            inv[:, bass.ds(g * 2 + j, 1)], None, ALU.mult)
                step(ins)
                step(dve.tensor_tensor(o[:], o[:], self_ps[0:LANES, 0:2 * D].rearrange("p (j f) -> p j f", j=2),
                                       ALU.add))
                dve.sem_inc(sums_used, 1)
                step(dve.tensor_tensor(sq[:], o[:], o[:], ALU.mult))
                step(dve.tensor_reduce(ss[:], sq[:], AX.X, ALU.add))
                dve.tensor_single_scalar(ss[:], ss[:], NORM_EPS * NORM_EPS, ALU.max).then_inc(ss_ok, 1)
                dve.wait_ge(norm_ok, g + 1)
                step(dve.reciprocal(inv_norm[:], l2[:]))
                for j in range(2):
                    ins = dve.scalar_tensor_tensor(y[:, j, :], o[:, j, :], inv_norm[:, j:j + 1],
                                                   xrows[:, bass.ds(g * 2 + j, 1), :].rearrange("p a f -> p (a f)"),
                                                   ALU.mult, ALU.add)
                step(ins)
                dve.wait_ge(x1_kept, g + 1)
                dve.wait_ge(x1t_ps_ok, g + 1)
                layer_norm(dve, step, g, x1, y, norm)
                dve.sem_inc(x1_ok, 1)


def layer1_nodes(nc, K, T, bias):
    c, sb, sem, bank = phase(nc, "l1")
    with c:
        bias_all = sb("bias_all", [LANES, D])
        y, x2 = sb("y", [LANES, 2, D]), sb("x2", [LANES, 2, D])
        norm = Norm(sb, sem)
        tr = bank("tr")
        loaded, step_s = sem("loaded"), sem("step")
        x2_ok, x2_kept = sem("x2_ok"), sem("x2_kept")
        tr_ok, tr_free = sem("tr_ok"), sem("tr_free")
        block = c.enter_context(nc.Block())
        sums = rows_of(K["agg"], ROWS_A)
        rows = rows_of(K["state"], ROWS_B)

        @block.sync
        def _(sp):
            sp.dma_start(bias_all[:], bias.rearrange("(a f) -> a f", a=1).to_broadcast([LANES, D]))\
                .then_inc(loaded, 16)

        @block.gpsimd
        def _(pool):
            pool.sem_inc(x2_kept, 1)
            with pool.Fori(0, PAIRS) as g:
                pool.wait_ge(x2_ok, g + 1)
                pool.tensor_copy(rows[:, bass.ds(g * 2, 2), :], x2[:]).then_inc(x2_kept, 1)

        @block.tensor
        def _(pe):
            pe.sem_inc(tr_ok, 1)
            with pe.Fori(0, PAIRS) as g:
                pe.wait_ge(x2_ok, g + 1)
                pe.wait_ge(tr_free, g + 1)
                for j in range(2):
                    last = pe.transpose(tr[:, j * LANES:(j + 1) * LANES], x2[:, j, :], K["ident"][0:LANES, 0:LANES])
                last.then_inc(tr_ok, 1)

        @block.scalar
        def _(act):
            act.sem_inc(tr_free, 1)
            with act.Fori(0, PAIRS) as g:
                deviation(act, K, g, norm)
                act.wait_ge(tr_ok, g + 2)
                act.copy(K["state"][:, bass.ds(g * PAIR, PAIR)], tr[:, 0:PAIR]).then_inc(tr_free, 1)

        @block.vector
        def _(dve):
            step = Steps(dve, step_s)
            dve.wait_ge(loaded, 16)
            dve.sem_inc(step_s, 1)
            with dve.Fori(0, PAIRS) as g:
                step.done = g * (2 + LN_STEPS) + 1
                pair = bass.ds(g * 2, 2)
                step(dve.tensor_tensor(y[:], sums[:, pair, :], bias_all[:, None, :].to_broadcast([LANES, 2, D]),
                                       ALU.add))
                step(dve.scalar_tensor_tensor(y[:], y[:], 0.0, rows[:, pair, :], ALU.max, ALU.add))
                dve.wait_ge(x2_kept, g + 1)
                dve.wait_ge(tr_ok, g + 1)
                layer_norm(dve, step, g, x2, y, norm)
                dve.sem_inc(x2_ok, 1)


def first_state(nc, K, T):
    c, sb, sem, bank = phase(nc, "fs")
    with c:
        stored, cleared = sem("stored"), sem("cleared")
        zeros = sb("zeros", [LANES, 10 * D])
        block = c.enter_context(nc.Block())
        rows = rows_of(K["state"], ROWS_B)

        @block.sync
        def _(sp):
            state = T["state"].rearrange("(p t) w -> p t w", p=LANES)
            sp.dma_start(T["x2"].rearrange("(p t) f -> p t f", p=LANES), rows).then_inc(stored, 16)
            sp.dma_start(state[:, :, 0:D], rows).then_inc(stored, 16)
            sp.wait_ge(cleared, 1)
            for q in range(5):
                sp.dma_start(state[:, q * 10:(q + 1) * 10, D:STATE], zeros[:].rearrange("p (t f) -> p t f", t=10))\
                    .then_inc(stored, 16)
            sp.wait_ge(stored, 16 * 7)

        @block.vector
        def _(dve):
            dve.memset(zeros[:], 0.0).then_inc(cleared, 1)
            dve.wait_ge(stored, 16 * 7)
            dve.memset(K["state"][:, NODES:2 * NODES], 0.0).then_inc(cleared, 1)


def gated_weights(nc, K, w_ih, w_hh, b_ih, b_hh, l0_w, l1_w):
    c, sb, sem, bank = phase(nc, "gw")
    with c:
        jobs = []
        plan = (("w_ih", w_ih, K["w_ih_t"]), ("w_hh", w_hh, K["w_hh_t"]), ("l0_w", l0_w, K["l0_t"]),
                ("l1_w", l1_w, K["l1_t"]))
        raw = []
        for name, w, t in plan:
            raw.append(sb(name, [128, w.shape[0] // 128, w.shape[1]]))
            for q in range(w.shape[0] // 128):
                for k in range(w.shape[1] // 128):
                    jobs.append((raw[-1][:, q, k * 128:(k + 1) * 128], t[:, k, q * 128:(q + 1) * 128]))
        b_raw = [sb("b_ih", [128, 6]), sb("b_hh", [128, 6])]
        tr = [bank("tr0"), bank("tr1")]
        loaded, tr_ok, tr_used = sem("loaded"), sem("tr_ok"), sem("tr_used")
        block = c.enter_context(nc.Block())

        @block.sync
        def _(sp):
            for (name, w, t), r in zip(plan, raw):
                sp.dma_start(r[:], w.rearrange("(q p) k -> p q k", p=128)).then_inc(loaded, 16)
            with nc.allow_non_contiguous_dma(reason="a few biases by partition"):
                for b, r in zip((b_ih, b_hh), b_raw):
                    sp.dma_start(r[:], b.rearrange("(q p) -> p q", p=128)).then_inc(loaded, 16)

        @block.tensor
        def _(pe):
            pe.wait_ge(loaded, 16 * 6)
            for n, (src, _) in enumerate(jobs):
                if n >= 2:
                    pe.wait_ge(tr_used, n - 1)
                pe.transpose(tr[n % 2][:, 0:128], src, K["ident"][:]).then_inc(tr_ok, 1)

        @block.scalar
        def _(act):
            for n, (_, dst) in enumerate(jobs):
                act.wait_ge(tr_ok, n + 1)
                act.copy(dst, tr[n % 2][:, 0:128]).then_inc(tr_used, 1)

        @block.vector
        def _(dve):
            dve.wait_ge(loaded, 16 * 6)
            dve.tensor_tensor(K["b_rz"][:], b_raw[0][:, 0:4], b_raw[1][:, 0:4], ALU.add)
            dve.tensor_copy(K["b_n"][:, 0, :], b_raw[0][:, 4:6])
            dve.tensor_copy(K["b_n"][:, 1, :], b_raw[1][:, 4:6])


class WeightSems:
    def __init__(self, make):
        def sem(n):
            return make(f"cw_{n}")
        self.loaded, self.tr_ok, self.wt_ok, self.prod_ok = sem("loaded"), sem("tr_ok"), sem("wt_ok"), sem("prod_ok")


def combined_weight(nc, K, S, rnd, w):
    c, sb, sem, bank = phase(nc, "cw")
    with c:
        raw = sb("raw", [128, 2, STATE])
        wt = sb("wt", [128, 2, STATE])
        tr = bank("tr")
        prod = [bank(f"prod{i}") for i in range(4)]
        block = c.enter_context(nc.Block())
        N3 = GATES // 2

        @block.sync
        def _(sp):
            sp.dma_start(raw[:], w[bass.ds(rnd, 1), :, :].rearrange("a (s p) m -> p (a s) m", p=128))\
                .then_inc(S.loaded, 16)

        @block.tensor
        def _(pe):
            pe.wait_ge(S.loaded, rnd * 16 + 16)
            for s in range(2):
                for m in range(2):
                    last = pe.transpose(tr[:, (m * 2 + s) * 128:(m * 2 + s + 1) * 128],
                                        raw[:, s, m * 128:(m + 1) * 128], K["ident"][:])
            last.then_inc(S.tr_ok, 1)
            pe.wait_ge(S.wt_ok, rnd + 1)
            for s in range(2):
                for h in range(2):
                    for m in range(2):
                        last = pe.matmul(prod[2 * s + h][:, 0:N3], wt[:, m, s * 128:(s + 1) * 128],
                                         K["w_ih_t"][:, m, h * N3:(h + 1) * N3], start=(m == 0), stop=(m == 1))
            last.then_inc(S.prod_ok, 1)

        @block.scalar
        def _(act):
            act.wait_ge(S.tr_ok, rnd + 1)
            act.copy(wt[:].rearrange("p m s -> p (m s)"), tr[:]).then_inc(S.wt_ok, 1)
            act.wait_ge(S.prod_ok, rnd + 1)
            for s in range(2):
                act.copy(K["w_comb"][:, s, 0:N3], prod[2 * s][:, 0:N3])

        @block.vector
        def _(dve):
            dve.wait_ge(S.prod_ok, rnd + 1)
            for s in range(2):
                dve.tensor_copy(K["w_comb"][:, s, N3:GATES], prod[2 * s + 1][:, 0:N3])


class GateSems:
    def __init__(self, make):
        def sem(n):
            return make(f"gru_{n}")
        self.r_ps, self.z_ps, self.n_ps, self.h_ps = sem("r_ps"), sem("z_ps"), sem("n_ps"), sem("h_ps")
        self.r_ok, self.z_ok = sem("r_ok"), sem("z_ok")
        self.t_ok, self.u_ok, self.n_ok = sem("t_ok"), sem("u_ok"), sem("n_ok")
        self.step, self.new_ok = sem("step"), sem("new_ok")
        self.kept, self.tr_ok, self.row_ok = sem("kept"), sem("tr_ok"), sem("row_ok")
        self.row_free, self.stored = sem("row_free"), sem("stored")


def gated_update(nc, K, T, S, rnd):
    c, sb, sem, bank = phase(nc, "gru")
    with c:
        gr, gz, u, ng, dd, new = (sb(n, [128, 2, PAIR]) for n in ("gr", "gz", "u", "ng", "dd", "new"))
        row = sb("row", [LANES, 2, STATE])
        r_b, z_b, n_b, h_b, tr = (bank(n) for n in ("r", "z", "n", "h", "tr"))
        block = c.enter_context(nc.Block())
        state, agg = transposed(K["state"], 2), transposed(K["agg"], 2)
        w_comb, w_hh = K["w_comb"], K["w_hh_t"]
        base = rnd * PAIRS
        credit = rnd * (PAIRS + 1)

        def half(b, s):
            return b[:, s * PAIR:(s + 1) * PAIR]

        @block.tensor
        def _(pe):
            def gates(g, first):
                cols = bass.ds(g * PAIR, PAIR)

                def product(b, gate, sums, states):
                    for s in range(2):
                        terms = [(w_comb, agg, k) for k in range(2) if sums] + \
                                [(w_hh, state, k) for k in range(2) if states]
                        out = slice(gate * STATE + s * 128, gate * STATE + (s + 1) * 128)
                        for n, (w, v, k) in enumerate(terms):
                            last = pe.matmul(half(b, s), w[:, k, out], v[:, k, cols],
                                             start=(n == 0), stop=(n == len(terms) - 1))
                    return last

                if not first:
                    pe.wait_ge(S.r_ok, base + g)
                product(r_b, 0, True, True).then_inc(S.r_ps, 1)
                if not first:
                    pe.wait_ge(S.t_ok, base + g)
                product(h_b, 2, False, True).then_inc(S.h_ps, 1)
                if not first:
                    pe.wait_ge(S.u_ok, base + g)
                product(n_b, 2, True, False).then_inc(S.n_ps, 1)
                if not first:
                    pe.wait_ge(S.z_ok, base + g)
                product(z_b, 1, True, True).then_inc(S.z_ps, 1)

            def rows(g):
                pe.wait_ge(S.new_ok, base + g + 1)
                pe.wait_ge(S.row_ok, credit + g + 1)
                for j in range(2):
                    for s in range(2):
                        last = pe.transpose(tr[0:LANES, (j * 2 + s) * 128:(j * 2 + s + 1) * 128],
                                            new[:, s, j * LANES:(j + 1) * LANES], K["ident"][:])
                last.then_inc(S.tr_ok, 1)

            pe.sem_inc(S.tr_ok, 1)
            gates(0, True)
            with pe.Fori(0, PAIRS - 1) as g:
                gates(g + 1, False)
                rows(g)
            rows(PAIRS - 1)

        @block.scalar
        def _(act):
            def gate(g):
                act.wait_ge(S.r_ps, base + g + 1)
                act.activation(gr[:, 0, :], half(r_b, 0), ACT.Sigmoid, bias=K["b_rz"][:, 0:1])
                act.activation(gr[:, 1, :], half(r_b, 1), ACT.Sigmoid, bias=K["b_rz"][:, 1:2]).then_inc(S.r_ok, 1)
                act.wait_ge(S.z_ps, base + g + 1)
                act.activation(gz[:, 0, :], half(z_b, 0), ACT.Sigmoid, bias=K["b_rz"][:, 2:3])
                act.activation(gz[:, 1, :], half(z_b, 1), ACT.Sigmoid, bias=K["b_rz"][:, 3:4]).then_inc(S.z_ok, 1)
                act.wait_ge(S.u_ok, base + g + 1)
                act.activation(ng[:, 0, :], u[:, 0, :], ACT.Tanh, bias=K["b_n"][:, 0, 0:1])
                act.activation(ng[:, 1, :], u[:, 1, :], ACT.Tanh, bias=K["b_n"][:, 0, 1:2]).then_inc(S.n_ok, 1)

            def rows(g):
                act.wait_ge(S.tr_ok, credit + g + 2)
                act.wait_ge(S.row_free, credit + g + 1)
                act.copy(row[:].rearrange("p j w -> p (j w)"), tr[0:LANES, :]).then_inc(S.row_ok, 1)

            act.sem_inc(S.row_ok, 1)
            gate(0)
            with act.Fori(0, PAIRS - 1) as g:
                act.wait_ge(S.new_ok, base + g + 1)
                gate(g + 1)
                rows(g)
            rows(PAIRS - 1)

        @block.vector
        def _(dve):
            step = Steps(dve, S.step)
            with dve.Fori(0, PAIRS) as g:
                step.done = (base + g) * 5
                cols = bass.ds(g * PAIR, PAIR)
                dve.wait_ge(S.r_ok, base + g + 1)
                dve.wait_ge(S.h_ps, base + g + 1)
                for s in range(2):
                    last = dve.scalar_tensor_tensor(u[:, s, :], half(h_b, s), K["b_n"][:, 1, s:s + 1], gr[:, s, :],
                                                    ALU.add, ALU.mult)
                step(last)
                dve.sem_inc(S.t_ok, 1)
                dve.wait_ge(S.n_ps, base + g + 1)
                step(dve.tensor_tensor(u[:], u[:], n_b[:, 0:2 * PAIR].rearrange("p (s n) -> p s n", s=2), ALU.add))
                dve.sem_inc(S.u_ok, 1)
                dve.wait_ge(S.n_ok, base + g + 1)
                dve.wait_ge(S.z_ok, base + g + 1)
                step(dve.tensor_tensor(dd[:], state[:, :, cols], ng[:], ALU.subtract))
                step(dve.tensor_tensor(dd[:], dd[:], gz[:], ALU.mult))
                dve.wait_ge(S.kept, credit + g + 1)
                dve.wait_ge(S.tr_ok, credit + g + 1)
                step(dve.tensor_tensor(new[:], dd[:], ng[:], ALU.add))
                dve.sem_inc(S.new_ok, 1)

        @block.gpsimd
        def _(pool):
            pool.sem_inc(S.kept, 1)
            with pool.Fori(0, PAIRS) as g:
                pool.wait_ge(S.new_ok, base + g + 1)
                pool.tensor_copy(state[:, :, bass.ds(g * PAIR, PAIR)], new[:]).then_inc(S.kept, 1)

        @block.sync
        def _(sp):
            table = T["state"].rearrange("(p t) w -> p t w", p=LANES)
            sp.sem_inc(S.row_free, 1)
            with sp.Fori(0, PAIRS) as g:
                sp.wait_ge(S.row_ok, credit + g + 2)
                sp.dma_start(table[:, bass.ds(g * 2, 2), :], row[:]).then_inc(S.stored, 16)
                sp.wait_ge(S.stored, (base + g) * 16 + 16)
                sp.sem_inc(S.row_free, 1)


def layer2_nodes(nc, K, T, l0_b, l1_b, e_w1):
    c, sb, sem, bank = phase(nc, "l2")
    with c:
        b0, b1 = sb("b0", [128, 2]), sb("b1", [LANES, D])
        w_edge = sb("w_edge", [D, 2, D])
        xs, xt = sb("xs", [LANES, 2, D]), sb("xt", [D, PAIR])
        hid = sb("hid", [D, 2, PAIR])
        y, x3, x3t = sb("y", [LANES, 2, D]), sb("x3", [LANES, 2, D]), sb("x3t", [D, PAIR])
        colrow = sb("colrow", [LANES, 2, D])
        norm = Norm(sb, sem)
        xt_ps, hid_ps, y_ps, x3t_ps, proj_ps = (bank(n) for n in ("xt_ps", "hid_ps", "y_ps", "x3t_ps", "proj_ps"))
        loaded, staged, step_s = sem("loaded"), sem("staged"), sem("step")
        xt_ps_ok, xt_ok, hid_ps_ok, hid_ok, y_ps_ok, y_used = (
            sem("xt_ps_ok"), sem("xt_ok"), sem("hid_ps_ok"), sem("hid_ok"), sem("y_ps_ok"), sem("y_used"))
        x3_ok, x3_kept, x3t_ps_ok, x3t_ok = sem("x3_ok"), sem("x3_kept"), sem("x3t_ps_ok"), sem("x3t_ok")
        proj_ps_ok, proj_ok, col_free, stored = sem("proj_ps_ok"), sem("proj_ok"), sem("col_free"), sem("stored")
        block = c.enter_context(nc.Block())
        rows, source_rows = rows_of(K["agg"], ROWS_A), rows_of(K["agg"], ROWS_B)
        state = transposed(K["state"], 2)
        LOADED = 16 * 5

        @block.sync
        def _(sp):
            sp.dma_start(rows, T["x2"].rearrange("(p t) f -> p t f", p=LANES)).then_inc(loaded, 16)
            with nc.allow_non_contiguous_dma(reason="a few biases by partition"):
                sp.dma_start(b0[:], l0_b.rearrange("(q p) -> p q", p=128)).then_inc(loaded, 16)
            sp.dma_start(b1[:], l1_b.rearrange("(a f) -> a f", a=1).to_broadcast([LANES, D])).then_inc(loaded, 16)
            for k in range(2):
                sp.dma_start(w_edge[:, k, :], e_w1[k * D:(k + 1) * D, :]).then_inc(loaded, 16)
            sp.sem_inc(col_free, 1)
            with sp.Fori(0, PAIRS) as g:
                sp.wait_ge(proj_ok, g + 2)
                sp.dma_start(T["xcol"].rearrange("(p t) f -> p t f", p=LANES)[:, bass.ds(g * 2, 2), :], colrow[:])\
                    .then_inc(stored, 16)
                sp.wait_ge(stored, g * 16 + 16)
                sp.sem_inc(col_free, 1)

        @block.gpsimd
        def _(pool):
            def stage(g):
                pool.tensor_copy(xs[:], rows[:, bass.ds(g * 2, 2), :]).then_inc(staged, 1)

            pool.wait_ge(loaded, LOADED)
            pool.sem_inc(x3_kept, 1)
            stage(0)
            with pool.Fori(0, PAIRS - 1) as g:
                pool.wait_ge(y_ps_ok, g + 1)
                pool.wait_ge(x3_ok, g + 1)
                stage(g + 1)
                pool.tensor_copy(rows[:, bass.ds(g * 2, 2), :], x3[:]).then_inc(x3_kept, 1)
            pool.wait_ge(x3_ok, PAIRS)
            pool.tensor_copy(rows[:, TILES - 2:TILES, :], x3[:]).then_inc(x3_kept, 1)

        @block.tensor
        def _(pe):
            def front(g):
                pe.wait_ge(staged, g + 1)
                for j in range(2):
                    last = pe.transpose(xt_ps[:, j * LANES:(j + 1) * LANES], xs[:, j, :],
                                        K["ident"][0:LANES, 0:LANES])
                last.then_inc(xt_ps_ok, 1)
                pe.wait_ge(xt_ok, g + 1)
                pe.wait_ge(hid_ok, g + 1)
                for s in range(2):
                    for k in range(3):
                        v = xt[:] if k == 2 else state[:, k, bass.ds(g * PAIR, PAIR)]
                        last = pe.matmul(hid_ps[:, s * PAIR:(s + 1) * PAIR], K["l0_t"][:, k, s * 128:(s + 1) * 128],
                                         v, start=(k == 0), stop=(k == 2))
                last.then_inc(hid_ps_ok, 1)

            def middle(g):
                pe.wait_ge(hid_ok, g + 2)
                pe.wait_ge(y_used, g + 1)
                for j in range(2):
                    for k in range(2):
                        last = pe.matmul(y_ps[0:LANES, j * D:(j + 1) * D], hid[:, k, j * LANES:(j + 1) * LANES],
                                         K["l1_t"][:, k, :], start=(k == 0), stop=(k == 1))
                last.then_inc(y_ps_ok, 1)

            def back(g):
                pe.wait_ge(x3_ok, g + 1)
                for j in range(2):
                    last = pe.transpose(x3t_ps[:, j * LANES:(j + 1) * LANES], x3[:, j, :],
                                        K["ident"][0:LANES, 0:LANES])
                last.then_inc(x3t_ps_ok, 1)
                pe.wait_ge(x3t_ok, g + 1)
                pe.wait_ge(proj_ok, g + 1)
                for j in range(2):
                    last = pe.matmul(proj_ps[0:LANES, j * 2 * D:(j + 1) * 2 * D], x3t[:, j * LANES:(j + 1) * LANES],
                                     w_edge[:].rearrange("p k f -> p (k f)"), start=True, stop=True)
                last.then_inc(proj_ps_ok, 1)

            pe.wait_ge(loaded, LOADED)
            pe.sem_inc(x3t_ps_ok, 1)
            front(0)
            middle(0)
            with pe.Fori(0, PAIRS - 1) as g:
                front(g + 1)
                back(g)
                middle(g + 1)
            back(PAIRS - 1)

        @block.scalar
        def _(act):
            def front(g):
                act.wait_ge(xt_ps_ok, g + 1)
                act.copy(xt[:], xt_ps[:, 0:PAIR]).then_inc(xt_ok, 1)
                act.wait_ge(hid_ps_ok, g + 1)
                for s in range(2):
                    last = act.activation(hid[:, s, :], hid_ps[:, s * PAIR:(s + 1) * PAIR], ACT.Relu,
                                          bias=b0[:, s:s + 1])
                last.then_inc(hid_ok, 1)

            def back(g):
                act.wait_ge(x3t_ps_ok, g + 2)
                act.copy(x3t[:], x3t_ps[:, 0:PAIR]).then_inc(x3t_ok, 1)
                act.wait_ge(proj_ps_ok, g + 1)
                act.wait_ge(col_free, g + 1)
                proj = proj_ps[0:LANES, :].rearrange("p (j k f) -> p j k f", j=2, k=2)
                act.copy(source_rows[:, bass.ds(g * 2, 2), :], proj[:, :, 0, :])
                act.copy(colrow[:], proj[:, :, 1, :]).then_inc(proj_ok, 1)

            act.wait_ge(loaded, LOADED)
            act.sem_inc(hid_ok, 1)
            act.sem_inc(proj_ok, 1)
            front(0)
            with act.Fori(0, PAIRS - 1) as g:
                deviation(act, K, g, norm)
                act.wait_ge(y_ps_ok, g + 1)
                front(g + 1)
                back(g)
            deviation(act, K, PAIRS - 1, norm)
            back(PAIRS - 1)

        @block.vector
        def _(dve):
            step = Steps(dve, step_s)
            dve.wait_ge(loaded, LOADED)
            dve.sem_inc(y_used, 1)
            with dve.Fori(0, PAIRS) as g:
                step.done = g * (2 + LN_STEPS)
                dve.wait_ge(y_ps_ok, g + 1)
                step(dve.tensor_tensor(y[:], y_ps[0:LANES, 0:2 * D].rearrange("p (j f) -> p j f", j=2),
                                       b1[:, None, :].to_broadcast([LANES, 2, D]), ALU.add))
                dve.sem_inc(y_used, 1)
                step(dve.scalar_tensor_tensor(y[:], y[:], 0.0, rows[:, bass.ds(g * 2, 2), :], ALU.max, ALU.add))
                dve.wait_ge(x3_kept, g + 1)
                dve.wait_ge(x3t_ps_ok, g + 1)
                layer_norm(dve, step, g, x3, y, norm)
                dve.sem_inc(x3_ok, 1)


def edge_mlp(nc, K, T, row_in, e_w1, e_b1, e_w2, e_b2):
    c, sb, sem, bank = phase(nc, "l3")
    with c:
        HALVES = CHUNKS // HALF
        W = HALF * SLOT
        w_attr, w2, b1, b2 = sb("w_attr", [ATTR, D]), sb("w2", [D, D]), sb("b1", [D, 1]), sb("b2", [128, D])
        slots = sb("slots", [128, DEEP, HALF, REC2])
        idx = sb("idx", [128, DEEP * HALF], I32)
        gathered = sb("gathered", [128, DEEP * HALF, D])
        onehot = sb("onehot", [128, DEEP, HALF, LANES])
        source = sb("source", [LANES, 2, HALF, D])
        onehot_t, attr_t = sb("onehot_t", [LANES, 2, W]), sb("attr_t", [ATTR, 2, W])
        hid, pre, msg = sb("hid", [D, 2, W]), sb("pre", [128, W]), sb("msg", [128, 2, W])
        onehot_ps, attr_ps, hid_ps, msg_ps, sum_ps = (bank(n) for n in ("onehot_ps", "attr_ps", "hid_ps", "msg_ps",
                                                                        "sum_ps"))
        loaded, zeroed = sem("loaded"), sem("zeroed")
        slots_in = [sem(f"slots_in{q}") for q in range(DEEP)]
        idx_ok, issued = sem("idx_ok"), sem("issued")
        onehot_ok, source_ok = sem("onehot_ok"), sem("source_ok")
        tr_ok, tr_used = sem("tr_ok"), sem("tr_used")
        hid_ps_ok, hid_ok, msg_ps_ok, pre_ok, msg_ok = (sem("hid_ps_ok"), sem("hid_ok"), sem("msg_ps_ok"),
                                                        sem("pre_ok"), sem("msg_ok"))
        sum_ok, added = sem("sum_ok"), sem("added")
        block = c.enter_context(nc.Block())
        source_rows = rows_of(K["agg"], ROWS_B)
        sums = K["state"]

        def number(i, off):
            return off if i is None else i * DEEP + off

        def turn(i, off):
            return off // DEEP if i is None else i + off // DEEP

        def run(eng, step):
            for j in range(-2, DEEP):
                step(None, j)
            with eng.Fori(0, HALVES // DEEP - 2) as i:
                for q in range(DEEP):
                    step(i, DEEP + q)
            for j in range(HALVES - DEEP, HALVES + 2):
                step(None, j)

        def exists(i, off):
            return i is not None or 0 <= off < HALVES

        def wait_half(eng, s, i, off):
            if i is not None or off >= 0:
                eng.wait_ge(s, number(i, off) + 1)

        @block.sync
        def _(sp):
            sp.dma_start(w_attr[:], e_w1[2 * D:2 * D + ATTR, :]).then_inc(loaded, 16)
            sp.dma_start(w2[:], e_w2).then_inc(loaded, 16)
            sp.dma_start(b1[:], e_b1.rearrange("(p a) -> p a", a=1)).then_inc(loaded, 16)
            sp.dma_start(b2[:], e_b2.rearrange("(a f) -> a f", a=1).to_broadcast([128, D])).then_inc(loaded, 16)
            table = T["slots2"].rearrange("(p q) w -> p q w", p=128)

            def load(i, off):
                if exists(i, off):
                    wait_half(sp, hid_ps_ok, i, off - DEEP)
                    sp.dma_start(slots[:, off % DEEP], table[:, bass.ds(number(i, off) * HALF, HALF), :])\
                        .then_inc(slots_in[off % DEEP], 16)
            for j in range(DEEP):
                load(None, j)
            with sp.Fori(0, HALVES // DEEP - 1) as i:
                for q in range(DEEP):
                    load(i, DEEP + q)

        @block.gpsimd
        def _(pool):
            with pool.Fori(0, HALVES // DEEP) as i:
                for q in range(DEEP):
                    pool.wait_ge(idx_ok, i * DEEP + (q + 1))
                    pool.sem_inc(issued, 1)
                    for r in range(q * HALF, (q + 1) * HALF):
                        pool.indirect_dma_start(
                            out=gathered[:, r, :], out_offset=None, in_=T["xcol"],
                            in_offset=bass.IndirectOffsetOnAxis(ap=idx[:, r:r + 1], axis=0)).then_inc(row_in[r], 16)

        @block.scalar
        def _(act):
            def step(i, off):
                if exists(i, off + 1):
                    wait_half(act, tr_ok, i, off + 1)
                    b = (off + 1) % 2
                    act.copy(onehot_t[:, b, :], onehot_ps[0:LANES, :])
                    act.copy(attr_t[:, b, :], attr_ps[0:ATTR, :]).then_inc(tr_used, 1)
                if exists(i, off):
                    wait_half(act, hid_ps_ok, i, off)
                    act.activation(hid[:, off % 2, :], hid_ps[:], ACT.Silu, bias=b1[:]).then_inc(hid_ok, 1)
                if exists(i, off - 1):
                    wait_half(act, pre_ok, i, off - 1)
                    act.activation(msg[:, (off - 1) % 2, :], pre[:], ACT.Silu).then_inc(msg_ok, 1)
                if exists(i, off + 3):
                    q = (off + 3) % DEEP
                    act.wait_ge(slots_in[q], turn(i, off + 3) * 16 + 16)
                    act.copy(idx[:, q * HALF:(q + 1) * HALF], slots[:, q, :, 0]).then_inc(idx_ok, 1)

            act.wait_ge(loaded, 64)
            act.wait_ge(slots_in[0], 16)
            act.copy(idx[:, 0:HALF], slots[:, 0, :, 0]).then_inc(idx_ok, 1)
            run(act, step)

        @block.tensor
        def _(pe):
            def step(i, off):
                if exists(i, off + 1):
                    q = (off + 1) % DEEP
                    wait_half(pe, onehot_ok, i, off + 1)
                    wait_half(pe, tr_used, i, off)
                    for k in range(HALF):
                        pe.transpose(onehot_ps[0:LANES, k * SLOT:(k + 1) * SLOT], onehot[:, q, k, :], K["ident"][:])
                    for k in range(HALF):
                        last = pe.transpose(attr_ps[0:ATTR, k * SLOT:(k + 1) * SLOT], slots[:, q, k, 2:REC2],
                                            K["ident"][:])
                    last.then_inc(tr_ok, 1)
                if exists(i, off):
                    q = off % DEEP
                    wait_half(pe, tr_used, i, off)
                    wait_half(pe, source_ok, i, off)
                    wait_half(pe, hid_ok, i, off - 1)
                    for k in range(HALF):
                        pe.wait_ge(row_in[q * HALF + k], turn(i, off) * 16 + 16)
                        out = hid_ps[:, k * SLOT:(k + 1) * SLOT]
                        pe.matmul(out, source[:, off % 2, k, :], onehot_t[:, off % 2, k * SLOT:(k + 1) * SLOT],
                                  start=True, stop=False)
                        pe.matmul(out, gathered[:, q * HALF + k, :], K["ident"][:], start=False, stop=False)
                        last = pe.matmul(out, w_attr[:], attr_t[:, off % 2, k * SLOT:(k + 1) * SLOT],
                                         start=False, stop=True)
                    last.then_inc(hid_ps_ok, 1)
                if exists(i, off - 1):
                    wait_half(pe, hid_ok, i, off - 1)
                    wait_half(pe, pre_ok, i, off - 2)
                    for k in range(HALF):
                        last = pe.matmul(msg_ps[:, k * D:(k + 1) * D],
                                         hid[:, (off - 1) % 2, k * SLOT:(k + 1) * SLOT], w2[:], start=True, stop=True)
                    last.then_inc(msg_ps_ok, 1)
                if exists(i, off - 2):
                    wait_half(pe, msg_ok, i, off - 2)
                    if i is not None or off - 3 >= 0:
                        pe.wait_ge(added, number(i, off - 2) * HALF)
                    for k in range(HALF):
                        last = pe.matmul(sum_ps[:, k * LANES:(k + 1) * LANES],
                                         msg[:, (off - 2) % 2, k * D:(k + 1) * D], onehot[:, (off - 2) % DEEP, k, :],
                                         start=True, stop=True)
                    last.then_inc(sum_ok, 1)

            pe.wait_ge(loaded, 64)
            run(pe, step)

        @block.vector
        def _(dve):
            def tile_of(i, off, k):
                return dve.value_load(K["tile2"][0:1, bass.ds(number(i, off) * HALF + k, 1)],
                                      min_val=0, max_val=TILES - 1)

            def build(i, off):
                q = off % DEEP
                dve.wait_ge(slots_in[q], turn(i, off) * 16 + 16)
                dve.tensor_tensor(onehot[:, q], K["iota_row"][:, None, 0:LANES].to_broadcast([128, HALF, LANES]),
                                  slots[:, q, :, 1:2].to_broadcast([128, HALF, LANES]), ALU.is_equal)\
                    .then_inc(onehot_ok, 1)

            def step(i, off):
                if exists(i, off + 1):
                    tiles = [tile_of(i, off + 1, k) for k in range(HALF)]
                    wait_half(dve, hid_ps_ok, i, off - 1)
                    for k, tile in enumerate(tiles):
                        last = dve.tensor_copy(source[:, (off + 1) % 2, k, :],
                                               source_rows[:, bass.ds(tile, 1), :].rearrange("p a f -> p (a f)"))
                    last.then_inc(source_ok, 1)
                if exists(i, off - 1):
                    wait_half(dve, msg_ps_ok, i, off - 1)
                    wait_half(dve, msg_ok, i, off - 2)
                    dve.tensor_tensor(pre[:].rearrange("p (k f) -> p k f", k=HALF),
                                      msg_ps[:].rearrange("p (k f) -> p k f", k=HALF),
                                      b2[:, None, :].to_broadcast([128, HALF, D]), ALU.add).then_inc(pre_ok, 1)
                if exists(i, off - 2):
                    tiles = [tile_of(i, off - 2, k) for k in range(HALF)]
                    wait_half(dve, sum_ok, i, off - 2)
                    for k, tile in enumerate(tiles):
                        if i is not None or (off - 2) * HALF + k > 0:
                            dve.wait_ge(added, number(i, off - 2) * HALF + k)
                        a = sums[:, bass.ds(tile * LANES, LANES)]
                        dve.tensor_tensor(a, a, sum_ps[:, k * LANES:(k + 1) * LANES], ALU.add).then_inc(added, 1)
                if exists(i, off + 2):
                    build(i, off + 2)

            dve.memset(sums[:, 0:NODES], 0.0).then_inc(zeroed, 1)
            dve.wait_ge(loaded, 64)
            dve.wait_ge(zeroed, 1)
            run(dve, step)


def layer3_nodes(nc, K, T, n_w1, n_b1, n_w2, n_b2, out):
    c, sb, sem, bank = phase(nc, "l4")
    with c:
        w1, w2 = sb("w1", [D, 2, D]), sb("w2", [D, D])
        b1, b2 = sb("b1", [D, 1]), sb("b2", [LANES, D])
        xs, xt, hid = sb("xs", [LANES, 2, D]), sb("xt", [D, PAIR]), sb("hid", [D, PAIR])
        y = sb("y", [LANES, 2, D])
        stats, mean_var = sb("stats", [LANES, 2, 6]), sb("mv", [LANES, TILES, 2])
        pair_var = sb("pair_mv", [LANES, 2, 2])
        y_ok, y_kept, var_kept = sem("y_ok"), sem("y_kept"), sem("var_kept")
        std, rstd = sb("std", [LANES, TILES]), sb("rstd", [LANES, TILES])
        PARTS = 5
        xt_ps, hid_ps, y_ps = bank("xt_ps"), bank("hid_ps"), bank("y_ps")
        loaded, staged, step_s = sem("loaded"), sem("staged"), sem("step")
        xt_ps_ok, xt_ok, hid_ps_ok, hid_ok, y_ps_ok, y_used = (
            sem("xt_ps_ok"), sem("xt_ok"), sem("hid_ps_ok"), sem("hid_ok"), sem("y_ps_ok"), sem("y_used"))
        var_ok, std_ok, part_ok, stored, passed = (sem("var_ok"), sem("std_ok"), sem("part_ok"), sem("stored"),
                                                   sem("passed"))
        block = c.enter_context(nc.Block())
        rows = rows_of(K["agg"], ROWS_A)
        sums = K["state"]

        @block.sync
        def _(sp):
            for k in range(2):
                sp.dma_start(w1[:, k, :], n_w1[k * D:(k + 1) * D, :]).then_inc(loaded, 16)
            sp.dma_start(w2[:], n_w2).then_inc(loaded, 16)
            sp.dma_start(b1[:], n_b1.rearrange("(p a) -> p a", a=1)).then_inc(loaded, 16)
            sp.dma_start(b2[:], n_b2.rearrange("(a f) -> a f", a=1).to_broadcast([LANES, D])).then_inc(loaded, 16)
            for q in range(PARTS):
                t = slice(q * TILES // PARTS, (q + 1) * TILES // PARTS)
                sp.wait_ge(part_ok, q + 1)
                sp.dma_start(out.rearrange("(p t) f -> p t f", p=LANES)[:, t, :], rows[:, t, :]).then_inc(stored, 16)
            sp.wait_ge(stored, 16 * PARTS)

        @block.gpsimd
        def _(pool):
            pool.sem_inc(y_kept, 1)
            pool.tensor_copy(xs[:], rows[:, 0:2, :]).then_inc(staged, 1)
            with pool.Fori(0, PAIRS - 1) as g:
                pool.wait_ge(hid_ps_ok, g + 1)
                pool.tensor_copy(xs[:], rows[:, bass.ds(g * 2 + 2, 2), :]).then_inc(staged, 1)
                pool.wait_ge(y_ok, g + 1)
                pool.tensor_copy(rows[:, bass.ds(g * 2, 2), :], y[:]).then_inc(y_kept, 1)
            pool.wait_ge(y_ok, PAIRS)
            pool.tensor_copy(rows[:, TILES - 2:TILES, :], y[:]).then_inc(y_kept, 1)

        @block.tensor
        def _(pe):
            def front(g):
                pe.wait_ge(staged, g + 1)
                for j in range(2):
                    last = pe.transpose(xt_ps[:, j * LANES:(j + 1) * LANES], xs[:, j, :],
                                        K["ident"][0:LANES, 0:LANES])
                last.then_inc(xt_ps_ok, 1)
                pe.wait_ge(xt_ok, g + 1)
                pe.wait_ge(hid_ok, g + 1)
                pe.matmul(hid_ps[:, 0:PAIR], w1[:, 0, :], xt[:], start=True, stop=False)
                pe.matmul(hid_ps[:, 0:PAIR], w1[:, 1, :], sums[:, bass.ds(g * PAIR, PAIR)],
                          start=False, stop=True).then_inc(hid_ps_ok, 1)

            def back(g):
                pe.wait_ge(hid_ok, g + 2)
                pe.wait_ge(y_used, g + 1)
                for j in range(2):
                    last = pe.matmul(y_ps[0:LANES, j * D:(j + 1) * D], hid[:, j * LANES:(j + 1) * LANES], w2[:],
                                     start=True, stop=True)
                last.then_inc(y_ps_ok, 1)

            pe.wait_ge(loaded, 80)
            pe.sem_inc(y_ps_ok, 1)
            with pe.Fori(0, PAIRS) as g:
                front(g)
                back(g)

        @block.scalar
        def _(act):
            act.wait_ge(loaded, 80)
            act.sem_inc(hid_ok, 1)
            with act.Fori(0, PAIRS) as g:
                act.wait_ge(xt_ps_ok, g + 1)
                act.copy(xt[:], xt_ps[:, 0:PAIR]).then_inc(xt_ok, 1)
                act.wait_ge(hid_ps_ok, g + 1)
                act.wait_ge(y_ps_ok, g + 1)
                act.activation(hid[:], hid_ps[:, 0:PAIR], ACT.Silu, bias=b1[:]).then_inc(hid_ok, 1)
            act.wait_ge(var_ok, 1)
            act.activation(std[:], mean_var[:, :, 1], ACT.Sqrt, bias=K["eps"][0:LANES, :]).then_inc(std_ok, 1)

        @block.vector
        def _(dve):
            step = Steps(dve, step_s)
            dve.wait_ge(loaded, 80)
            dve.sem_inc(y_used, 1)
            with dve.Fori(0, PAIRS) as g:
                step.done = g * 4
                dve.wait_ge(y_kept, g + 1)
                dve.wait_ge(y_ps_ok, g + 2)
                step(dve.tensor_tensor(y[:], y_ps[0:LANES, 0:2 * D].rearrange("p (j f) -> p j f", j=2),
                                       b2[:, None, :].to_broadcast([LANES, 2, D]), ALU.add))
                dve.sem_inc(y_used, 1)
                step(dve.scalar_tensor_tensor(y[:], rows[:, bass.ds(g * 2, 2), :], 2.0, y[:], ALU.mult, ALU.add))
                dve.sem_inc(y_ok, 1)
                for j in range(2):
                    ins = dve.bn_stats(stats[:, j, :], y[:, j, :])
                step(ins)
                dve.sem_inc(passed, 1)
                for j in range(2):
                    ins = dve.bn_aggr(pair_var[:, j, :], stats[:, j, :])
                step(ins)
                dve.tensor_copy(mean_var[:, bass.ds(g * 2, 2), :], pair_var[:]).then_inc(var_kept, 1)
            dve.wait_ge(var_kept, PAIRS)
            dve.wait_ge(y_kept, PAIRS + 1)
            step.done = PAIRS * 4
            dve.sem_inc(var_ok, 1)
            dve.wait_ge(std_ok, 1)
            step(dve.reciprocal(rstd[:], std[:]))
            for q in range(PARTS):
                for t in range(q * TILES // PARTS, (q + 1) * TILES // PARTS):
                    ins = dve.tensor_scalar(rows[:, t, :], rows[:, t, :], mean_var[:, t, 0:1], rstd[:, t:t + 1],
                                            ALU.subtract, ALU.mult)
                ins.then_inc(part_ok, 1)


def gnn(nc, x, src, dst, edge_attr_16, edge_type_8, edge_weight1, L0_gnn_W_l, L0_gnn_b_l, L0_gnn_W_r,
        L1_gnn_weight, L1_gnn_bias, L2_gnn_W, L2_gnn_w_ih, L2_gnn_w_hh, L2_gnn_b_ih, L2_gnn_b_hh,
        L2_gnn_l0_w, L2_gnn_l0_b, L2_gnn_l1_w, L2_gnn_l1_b, L3_gnn_eW1, L3_gnn_eb1, L3_gnn_eW2, L3_gnn_eb2,
        L3_gnn_nW1, L3_gnn_nb1, L3_gnn_nW2, L3_gnn_nb2, out):
    with ExitStack() as c:
        K = {}

        def buffers(*specs):
            for name, shape, *dt in specs:
                K[name] = c.enter_context(nc.sbuf_tensor(name, shape, *(dt or [F32])))

        T = tables(nc, c)
        buffers(("ident", [128, 128]), ("iota_row", [128, 128]), ("ones", [128, 128]), ("before", [128, 128]),
                ("chunk_no", [128, TILE_COLS]), ("eps", [128, 1]), ("rec", [128, PAD_CHUNKS, REC1]),
                ("tile1", [1, CHUNKS], I32), ("tile2", [1, CHUNKS], I32))
        constants(nc, K)

        def sems(name, n):
            return [c.enter_context(nc.semaphore(f"{name}{r}")) for r in range(n)]

        sort_edges(nc, K, T, [sems("scattered1_", RING), sems("scattered2_", RING)], src, dst, edge_attr_16, edge_type_8, edge_weight1)
        load_slots(nc, K, T)
        buffers(("agg", [128, 2 * TILES * D]), ("state", [128, 2 * TILES * D]))
        with ExitStack() as g:
            def scoped(*specs):
                for name, shape, *dt in specs:
                    K[name] = g.enter_context(nc.sbuf_tensor(name, shape, *(dt or [F32])))

            scoped(("onehot", [128, 2, HALF, LANES]), ("rows", [128, RING, STATE]), ("idx", [128, RING], I32))
            with ExitStack() as q:
                K["cnt"] = q.enter_context(nc.sbuf_tensor("cnt", [LANES, TILES], F32))
                gather_sum(nc, K, GatherSems(semaphores(nc, q), sems("g0_row_in", RING), "g0"), 0, x, 0, D, count=True)
                layer0_nodes(nc, K, T, x, L0_gnn_W_l, L0_gnn_b_l, L0_gnn_W_r, L1_gnn_weight)
            with ExitStack() as q:
                gather_sum(nc, K, GatherSems(semaphores(nc, q), sems("g1_row_in", RING), "g1"), 0, T["rel"], 2, D, by_row=True, weighted=True)
                layer1_nodes(nc, K, T, L1_gnn_bias)
                first_state(nc, K, T)
            scoped(("w_ih_t", [128, 2, GATES]), ("w_hh_t", [128, 2, GATES]), ("w_comb", [128, 2, GATES]),
                   ("l0_t", [128, 3, 256]), ("l1_t", [128, 2, D]), ("b_rz", [128, 4]), ("b_n", [128, 2, 2]))
            gated_weights(nc, K, L2_gnn_w_ih, L2_gnn_w_hh, L2_gnn_b_ih, L2_gnn_b_hh, L2_gnn_l0_w, L2_gnn_l1_w)
            with ExitStack() as q:
                gather_s, weight_s, gate_s = GatherSems(semaphores(nc, q), sems("g2_row_in", RING), "g2"), WeightSems(semaphores(nc, q)), GateSems(semaphores(nc, q))
                with nc.Fori(0, L2_gnn_W.shape[0]) as rnd:
                    combined_weight(nc, K, weight_s, rnd, L2_gnn_W)
                    gather_sum(nc, K, gather_s, rnd, T["state"], 0, STATE)
                    gated_update(nc, K, T, gate_s, rnd)
            layer2_nodes(nc, K, T, L2_gnn_l0_b, L2_gnn_l1_b, L3_gnn_eW1)
        edge_mlp(nc, K, T, sems("edge_row_in", DEEP * HALF), L3_gnn_eW1, L3_gnn_eb1, L3_gnn_eW2, L3_gnn_eb2)
        layer3_nodes(nc, K, T, L3_gnn_nW1, L3_gnn_nb1, L3_gnn_nW2, L3_gnn_nb2, out)


_INS = ["x", "src", "dst", "edge_attr_16", "edge_type_8", "edge_weight1", "L0_gnn_W_l", "L0_gnn_b_l", "L0_gnn_W_r",
        "L1_gnn_weight", "L1_gnn_bias", "L2_gnn_W", "L2_gnn_w_ih", "L2_gnn_w_hh", "L2_gnn_b_ih", "L2_gnn_b_hh",
        "L2_gnn_l0_w", "L2_gnn_l0_b", "L2_gnn_l1_w", "L2_gnn_l1_b", "L3_gnn_eW1", "L3_gnn_eb1", "L3_gnn_eW2",
        "L3_gnn_eb2", "L3_gnn_nW1", "L3_gnn_nb1", "L3_gnn_nW2", "L3_gnn_nb2"]
_OUTS = [((NODES, D), "float32")]


def kernel(**inputs):
    import numpy as _np
    import concourse.bacc as _bacc
    from concourse import mybir as _mybir
    from concourse.bass_utils import run_bass_kernel_spmd as _run

    nc = _bacc.Bacc("TRN2", target_bir_lowering=False, num_devices=1)
    arrays, args = {}, []
    for name in _INS:
        a = _np.ascontiguousarray(inputs[name])
        arrays[f"in_{name}_dram"] = a
        args.append(nc.dram_tensor(f"in_{name}_dram", a.shape, _mybir.dt.from_np(a.dtype), kind="ExternalInput").ap())
    for i, (shape, dtype) in enumerate(_OUTS):
        dt = _mybir.dt.from_np(_np.dtype(dtype))
        args.append(nc.dram_tensor(f"out_{i}_dram", shape, dt, kind="ExternalOutput").ap())
    gnn(nc, *args)
    r = _run(nc, [arrays], core_ids=[0])
    got = tuple(r.results[0][f"out_{i}_dram"] for i in range(len(_OUTS)))
    return got[0]
```

```python
from contextlib import ExitStack

import concourse.bass as bass
from concourse import mybir

F32 = mybir.dt.float32
I32 = mybir.dt.int32
ALU = mybir.AluOpType
ACT = mybir.ActivationFunctionType
AX = mybir.AxisListType

D = 128
LANES = 125
TILES = 50
NODES = LANES * TILES
PAIRS = TILES // 2
PAIR = 2 * LANES
EDGE_COLS = 800
RELS = 8
ATTR = 16
HALF = 4
RING = 8
G_HALVES = 4
G_RING = G_HALVES * HALF
SLOT = 128
CHUNKS = -(-((LANES * EDGE_COLS + TILES * (SLOT - 1)) // SLOT) // (8 * HALF)) * 8 * HALF
TURNS = CHUNKS // G_RING
DEEP = 8
FETCH = 4
PAD_CHUNKS = CHUNKS + HALF
TILE_COLS = 7
REC1 = 4
REC2 = 2 + ATTR
STATE = 2 * D
GATES = 3 * STATE
LN_EPS = 1e-5
NORM_EPS = 1e-12


class Steps:

    def __init__(self, eng, sem, start=0):
        self.eng, self.sem, self.done = eng, sem, start

    def __call__(self, ins):
        ins.then_inc(self.sem, 1)
        self.done = self.done + 1
        self.eng.wait_ge(self.sem, self.done)


def semaphores(nc, c):
    made = []

    def clear():
        nc.clear_and_free_semaphores(made)
        nc.all_engine_barrier()

    def sem(name):
        made.append(nc.alloc_semaphore(name))
        return made[-1]
    c.callback(clear)
    return sem


def tables(nc, c):
    def dram(name, shape, dt=F32):
        return nc.dram_tensor(f"{name}_table", shape, dt, kind="Internal").ap()
    return dict(
        slots1=dram("slots1", (SLOT * CHUNKS, REC1)),
        slots2=dram("slots2", (SLOT * CHUNKS, REC2)),
        edges2=dram("edges2", (LANES * EDGE_COLS, REC2)),
        rows2=dram("rows2", (LANES * EDGE_COLS,), I32),
        tile_of_chunk1=dram("tile_of_chunk1", (SLOT * TILE_COLS,), I32),
        tile_of_chunk2=dram("tile_of_chunk2", (SLOT * TILE_COLS,), I32),
        x2=dram("x2", (NODES, D)),
        rel=dram("rel", (NODES * RELS, D)),
        state=dram("state", (NODES, STATE)),
        xcol=dram("xcol", (NODES, D)),
    )


def constants(nc, K):
    with ExitStack() as c:
        sem = semaphores(nc, c)
        made, cast = sem("const_made"), sem("const_cast")
        iota_i = c.enter_context(nc.sbuf_tensor("iota_i", [128, 128], I32))
        chunk_i = c.enter_context(nc.sbuf_tensor("chunk_i", [128, TILE_COLS], I32))
        block = c.enter_context(nc.Block())

        @block.gpsimd
        def _(pool):
            pool.iota(iota_i[:], pattern=[[1, 128]], base=0, channel_multiplier=0).then_inc(made, 1)
            pool.iota(chunk_i[:], pattern=[[1, TILE_COLS]], base=0, channel_multiplier=TILE_COLS).then_inc(made, 1)
            pool.memset(K["ident"][:], 0.0).then_inc(made, 1)
            pool.memset(K["ones"][:], 1.0).then_inc(made, 1)
            pool.memset(K["eps"][:], LN_EPS).then_inc(made, 1)
            pool.wait_ge(made, 5)
            pool.affine_select(out=K["ident"][:], in_=K["ident"][:], compare_op=ALU.not_equal, fill=1.0,
                               base=0, pattern=[[-1, 128]], channel_multiplier=1).then_inc(made, 1)
            pool.affine_select(out=K["before"][:], in_=K["ones"][:], compare_op=ALU.is_gt, fill=0.0,
                               base=0, pattern=[[1, 128]], channel_multiplier=-1).then_inc(made, 1)

        @block.vector
        def _(dve):
            dve.wait_ge(made, 2)
            dve.tensor_copy(K["iota_row"][:], iota_i[:]).then_inc(cast, 1)
            dve.tensor_copy(K["chunk_no"][:], chunk_i[:]).then_inc(cast, 1)


def sort_edges(nc, K, T, scattered, src, dst, edge_attr, edge_type, edge_weight):
    with ExitStack() as c:
        def sb(name, shape, dt=F32):
            return c.enter_context(nc.sbuf_tensor(name, shape, dt))

        sem = semaphores(nc, c)
        L, C = LANES, EDGE_COLS
        PARTS = 4
        key_i = [sb("dst_i", [L, C], I32), sb("src_i", [L, C], I32)]
        type_i = sb("type_i", [L, C], I32)
        key = [sb("dst_f", [L, C]), sb("src_f", [L, C])]
        bucket = sb("bucket", [L, C])
        lane = [sb("dst_lane", [L, C]), sb("src_lane", [L, C])]
        row = [sb("dst_row", [L, C]), sb("src_row", [L, C])]
        tmp = sb("tmp", [L, C])
        tmp_i = sb("tmp_i", [L, C], I32)
        rank, slot_i = sb("rank", [L, C]), sb("slot_i", [L, C], I32)
        ones_c = sb("ones_c", [L, C])
        norm = sb("norm", [L, C])
        rel_row = sb("rel_row", [L, C])
        rec2 = sb("rec2", [L, C, REC2])
        attr = sb("attr", [L, C // PARTS, ATTR])
        rows2_i = sb("rows2_i", [L, C], I32)
        hist = sb("hist", [L, TILES])
        total = sb("total", [128, TILES])
        total_i = sb("total_i", [128, TILES], I32)
        chunks = sb("chunks", [128, TILES])
        chunks_end = sb("chunks_end", [128, TILES])
        base = sb("base", [L, TILES])
        over = sb("over", [128, TILE_COLS, TILES])
        tile_f = sb("tile_f", [128, TILE_COLS])
        tile_i = [sb("tile1_i", [128, TILE_COLS], I32), sb("tile2_i", [128, TILE_COLS], I32)]
        fill2 = sb("fill2", [128, CHUNKS // 8, REC2])
        row_stage = sb("row_stage", [L, RING], I32)
        rec1_stage = sb("rec1_stage", [L, RING, REC1])
        count_ps = c.enter_context(nc.psum_tensor("count_ps", [128, 2, 256], F32))

        keys_in, rest_in = sem("keys_in"), sem("rest_in")
        filled, filled_rows = sem("filled"), sem("filled_rows")
        step_s = sem("dve_step")
        hist_done, counted = sem("hist_done"), sem("counted")
        tile_done, tile_out = sem("tile_done"), sem("tile_out")
        rows_done = sem("rows_done")
        staged, stage_step = sem("staged"), sem("stage_step")
        issued, passed = sem("issued"), sem("passed")
        attr_in, attr_used, rec2_ok, rec2_out = sem("attr_in"), sem("attr_used"), sem("rec2_ok"), sem("rec2_out")
        block = c.enter_context(nc.Block())
        SC_TURNS = EDGE_COLS // RING

        @block.sync
        def _(sp):
            for t, a in ((key_i[0], dst), (key_i[1], src)):
                sp.dma_start(t[:], a.rearrange("(p c) -> p c", p=L)).then_inc(keys_in, 16)
            sp.dma_start(type_i[:], edge_type.rearrange("(p c) -> p c", p=L)).then_inc(rest_in, 16)
            sp.dma_start(norm[:], edge_weight.rearrange("(p c) o -> p (c o)", p=L)).then_inc(rest_in, 16)
            for q in range(PARTS):
                if q > 0:
                    sp.wait_ge(attr_used, q)
                sp.dma_start(attr[:], edge_attr.rearrange("(p c) k -> p c k", p=L)
                             [:, q * C // PARTS:(q + 1) * C // PARTS, :]).then_inc(attr_in, 16)
            sp.wait_ge(filled, 2)
            sp.dma_start(T["slots1"].rearrange("(p q) w -> p (q w)", p=128),
                         K["rec"][:, 0:CHUNKS, :].rearrange("p q w -> p (q w)")).then_inc(filled_rows, 16)
            sp.wait_ge(filled, 4)
            slots2 = T["slots2"].rearrange("(p e q) w -> p e (q w)", p=128, e=8)
            for e in range(8):
                sp.dma_start(slots2[:, e, :], fill2[:].rearrange("p q w -> p (q w)")).then_inc(filled_rows, 16)
            for k in range(2):
                sp.wait_ge(tile_done, k + 1)
                sp.dma_start(T[f"tile_of_chunk{k + 1}"].rearrange("(p j) -> p j", p=128), tile_i[k][:])\
                    .then_inc(tile_out, 16)
            sp.wait_ge(attr_used, PARTS)
            sp.wait_ge(rec2_ok, 3)
            sp.dma_start(T["edges2"].rearrange("(p c) w -> p c w", p=L), rec2[:]).then_inc(rec2_out, 16)
            sp.dma_start(T["rows2"].rearrange("(p c) -> p c", p=L), rows2_i[:]).then_inc(rec2_out, 16)
            sp.wait_ge(tile_out, 32)
            sp.wait_ge(rec2_out, 32)

        @block.gpsimd
        def _(pool):
            pool.memset(K["rec"][:], 0.0).then_inc(filled, 1)
            pool.wait_ge(filled, 1)
            pool.memset(K["rec"][:, :, 1:2], -1.0).then_inc(filled, 1)
            pool.memset(fill2[:], 0.0).then_inc(filled, 1)
            pool.wait_ge(filled, 3)
            pool.memset(fill2[:, :, 1:2], -1.0).then_inc(filled, 1)
            pool.wait_ge(filled_rows, 16 * 9)
            with pool.Fori(0, SC_TURNS) as i:
                for r in range(RING):
                    if r % HALF == 0:
                        pool.wait_ge(staged, i * 2 + (r // HALF + 1))
                        pool.sem_inc(issued, 1)
                    pool.indirect_dma_start(
                        out=T["slots1"], out_offset=bass.IndirectOffsetOnAxis(ap=row_stage[:, r:r + 1], axis=0),
                        in_=rec1_stage[:, r, :], in_offset=None).then_inc(scattered[r // HALF], 16)
            for h in range(2):
                pool.wait_ge(scattered[h], 16 * HALF * SC_TURNS)

        @block.scalar
        def _(act):
            def stage(i, h, first):
                s = slice(h * HALF, h * HALF + HALF)
                cols = bass.ds(i * RING + h * HALF, HALF)
                if not first:
                    act.wait_ge(scattered[h], i * (16 * HALF))
                act.copy(row_stage[:, s], row[0][:, cols]).then_inc(stage_step, 1)
                for w, t in enumerate((key[1], lane[0], rel_row)):
                    act.copy(rec1_stage[:, s, w], t[:, cols]).then_inc(stage_step, 1)
                act.copy(rec1_stage[:, s, 3], norm[:, cols]).then_inc(staged, 1)

            for q in range(PARTS):
                act.wait_ge(attr_in, 16 * (q + 1))
                act.copy(rec2[:, q * C // PARTS:(q + 1) * C // PARTS, 2:REC2], attr[:]).then_inc(attr_used, 1)
            act.wait_ge(rest_in, 32)
            act.wait_ge(rows_done, 1)
            for h in range(2):
                stage(0, h, True)
            for q in range(PARTS):
                act.wait_ge(rows_done, q + 1)
                act.sem_inc(passed, 1)
                with act.Fori(max(1, q * SC_TURNS // PARTS), (q + 1) * SC_TURNS // PARTS) as i:
                    for h in range(2):
                        stage(i, h, False)

        @block.tensor
        def _(pe):
            for k in range(2):
                pe.wait_ge(hist_done, k + 1)
                pe.matmul(count_ps[0:L, 0, 0:TILES], K["before"][0:L, 0:L], hist[:], start=True, stop=True)
                pe.matmul(count_ps[:, 1, 0:TILES], K["ones"][0:L, :], hist[:], start=True, stop=True)\
                    .then_inc(counted, 1)

        @block.vector
        def _(dve):
            step = Steps(dve, step_s)
            step(dve.memset(ones_c[:], 1.0))
            dve.wait_ge(keys_in, 32)
            step(dve.tensor_copy(key[0][:], key_i[0][:]))
            step(dve.tensor_copy(key[1][:], key_i[1][:]))
            dve.wait_ge(rest_in, 32)
            step(dve.tensor_copy(tmp[:], type_i[:]))
            step(dve.scalar_tensor_tensor(rel_row[:], key[1][:], float(RELS), tmp[:], ALU.mult, ALU.add))
            for k in range(2):
                step(dve.tensor_scalar(tmp_i[:], key[k][:], 1.0 / TILES, -0.49, ALU.mult, ALU.add))
                step(dve.tensor_copy(lane[k][:], tmp_i[:]))
                step(dve.scalar_tensor_tensor(bucket[:], lane[k][:], -float(TILES), key[k][:], ALU.mult, ALU.add))
                step(dve.tensor_single_scalar(tmp[:], bucket[:], 0.0, ALU.is_lt))
                step(dve.tensor_tensor(lane[k][:], lane[k][:], tmp[:], ALU.subtract))
                step(dve.scalar_tensor_tensor(bucket[:], tmp[:], float(TILES), bucket[:], ALU.mult, ALU.add))
                step(dve.tensor_single_scalar(tmp[:], bucket[:], float(TILES), ALU.is_ge))
                step(dve.tensor_tensor(lane[k][:], lane[k][:], tmp[:], ALU.add))
                step(dve.scalar_tensor_tensor(bucket[:], tmp[:], -float(TILES), bucket[:], ALU.mult, ALU.add))
                at = step.done
                with dve.Fori(0, TILES) as t:
                    step.done = at + t
                    step(dve.tensor_scalar(tmp[:], bucket[:], K["iota_row"][0:L, bass.ds(t, 1)], 0.0,
                                           ALU.is_equal, ALU.add, accum_out=hist[:, bass.ds(t, 1)]))
                step.done = at + TILES
                dve.sem_inc(hist_done, 1)
                dve.wait_ge(counted, k + 1)
                step(dve.tensor_scalar(total_i[:], count_ps[:, 1, 0:TILES], float(SLOT - 1), None, ALU.add))
                step(dve.tensor_scalar(total_i[:], total_i[:], 7, None, ALU.arith_shift_right))
                step(dve.tensor_copy(chunks[:], total_i[:]))
                step(dve.tensor_tensor_scan(chunks_end[:], K["ones"][:, 0:TILES], chunks[:], 0.0, ALU.mult, ALU.add))
                step(dve.tensor_tensor(total[:], chunks_end[:], chunks[:], ALU.subtract))
                step(dve.tensor_scalar(total[:], total[:], float(SLOT), -1.0, ALU.mult, ALU.add))
                step(dve.tensor_tensor(base[:], total[0:L, :], count_ps[0:L, 0, 0:TILES], ALU.add))
                step(dve.tensor_tensor(
                    over[:], chunks_end[:, None, :].to_broadcast([128, TILE_COLS, TILES]),
                    K["chunk_no"][:, :, None].to_broadcast([128, TILE_COLS, TILES]), ALU.is_le))
                step(dve.tensor_reduce(tile_f[:], over[:], AX.X, ALU.add))
                step(dve.tensor_single_scalar(tile_i[k][:], tile_f[:], float(TILES - 1), ALU.min))
                dve.sem_inc(tile_done, 1)
                parts = PARTS if k == 0 else 1
                for q in range(parts):
                    cols = slice(q * C // parts, (q + 1) * C // parts)
                    at = step.done
                    with dve.Fori(0, TILES) as t:
                        step.done = at + t * 4
                        step(dve.tensor_scalar(tmp[:, cols], bucket[:, cols], K["iota_row"][0:L, bass.ds(t, 1)],
                                               None, ALU.is_equal))
                        step(dve.tensor_tensor_scan(rank[:, cols], ones_c[:, cols], tmp[:, cols],
                                                    base[:, bass.ds(t, 1)], ALU.mult, ALU.add))
                        dve.sem_inc(passed, 1)
                        step(dve.copy_predicated(row[k][:, cols], tmp[:, cols].bitcast(I32), rank[:, cols]))
                        dve.sem_inc(passed, 1)
                        step(dve.tensor_copy(base[:, bass.ds(t, 1)], rank[:, cols.stop - 1:cols.stop]))
                    step.done = at + TILES * 4
                    step(dve.tensor_copy(tmp_i[:, cols], row[k][:, cols]))
                    step(dve.tensor_scalar(slot_i[:, cols], tmp_i[:, cols], 7, None, ALU.arith_shift_right))
                    step(dve.tensor_scalar(tmp_i[:, cols], tmp_i[:, cols], SLOT - 1, None, ALU.bitwise_and))
                    step(dve.tensor_copy(rank[:, cols], slot_i[:, cols]))
                    step(dve.tensor_copy(tmp[:, cols], tmp_i[:, cols]))
                    step(dve.scalar_tensor_tensor(row[k][:, cols], tmp[:, cols], float(CHUNKS), rank[:, cols],
                                                  ALU.mult, ALU.add))
                    dve.sem_inc(rows_done, 1)
            dve.tensor_copy(rec2[:, :, 0], key[0][:]).then_inc(rec2_ok, 1)
            dve.tensor_copy(rec2[:, :, 1], lane[1][:]).then_inc(rec2_ok, 1)
            dve.tensor_copy(rows2_i[:], row[1][:]).then_inc(rec2_ok, 1)


def load_slots(nc, K, T):
    with ExitStack() as c:
        loaded = semaphores(nc, c)("slots_loaded")
        block = c.enter_context(nc.Block())

        @block.sync
        def _(sp):
            sp.dma_start(K["rec"][:, 0:CHUNKS, :].rearrange("p q w -> p (q w)"),
                         T["slots1"].rearrange("(p q) w -> p (q w)", p=128)).then_inc(loaded, 16)
            for k in (1, 2):
                sp.dma_start(K[f"tile{k}"][:], T[f"tile_of_chunk{k}"][0:CHUNKS]
                             .rearrange("(a q) -> a q", a=1)).then_inc(loaded, 16)
            sp.wait_ge(loaded, 48)


class GatherSems:
    def __init__(self, make, row_in, name):
        self.name = name

        def sem(n):
            return make(f"{name}_{n}")
        self.idx_staged = sem("idx_staged")
        self.issued = sem("issued")
        self.row_in = row_in
        self.onehot = sem("onehot")
        self.summed = sem("summed")
        self.psum_free = sem("psum_free")
        self.zeroed = sem("zeroed")
        self.started = sem("started")


def tiles_of(nc, eng, table, half):
    _, tiles = nc.values_load_multi_w_load_instructions(
        table[0:1, bass.ds(half * HALF, HALF)], engines=[eng.engine], min_val=0, max_val=TILES - 1)
    return tiles


def gather_sum(nc, K, S, rnd, table, word, width, by_row=False, weighted=False, count=False):
    NPS = 4
    onehot, rows, idx = K["onehot"], K["rows"], K["idx"]
    agg, rec = K["agg"], K["rec"]
    halves = width // D
    agg_t = agg[:, 0:halves * NODES].rearrange("p (s n) -> p s n", s=halves)
    with ExitStack() as c:
        prod = [c.enter_context(nc.psum_tensor(f"{S.name}_prod{b}", [128, 512], F32)) for b in range(NPS)]
        block = c.enter_context(nc.Block())
        s_base = rnd * (CHUNKS + G_RING)
        f_base = rnd * (CHUNKS + NPS)

        @block.scalar
        def _(act):
            act.wait_ge(S.summed, s_base + G_RING)
            act.sem_inc(S.started, 1)
            with act.Fori(0, TURNS) as i:
                for h in range(G_HALVES):
                    act.wait_ge(S.summed, s_base + i * G_RING + (h * HALF + HALF))
                    act.copy(idx[:, h * HALF:h * HALF + HALF],
                             rec[:, bass.ds(i * G_RING + h * HALF, HALF), word]).then_inc(S.idx_staged, 1)

        @block.gpsimd
        def _(pool):
            with pool.Fori(0, TURNS) as i:
                for r in range(G_RING):
                    if r % HALF == 0:
                        pool.wait_ge(S.idx_staged, (rnd * TURNS + i) * G_HALVES + (r // HALF + 1))
                        pool.sem_inc(S.issued, 1)
                    pool.indirect_dma_start(
                        out=rows[:, r, 0:width], out_offset=None, in_=table,
                        in_offset=bass.IndirectOffsetOnAxis(ap=idx[:, r:r + 1], axis=0)).then_inc(S.row_in[r // HALF], 16)

        @block.tensor
        def _(pe):
            pe.sem_inc(S.summed, G_RING)
            with pe.Fori(0, TURNS) as i:
                for r in range(G_RING):
                    if r % HALF == 0:
                        pe.wait_ge(S.onehot, rnd * (TURNS * G_HALVES + 1) + i * G_HALVES + (r // HALF + 1))
                        pe.wait_ge(S.row_in[r // HALF], (rnd * TURNS + i) * (16 * HALF) + 16 * HALF)
                    pe.wait_ge(S.psum_free, f_base + i * G_RING + (r + 1))
                    p = prod[r % NPS]
                    oh = onehot[:, r // HALF, r % HALF, :]
                    if count:
                        pe.matmul(p[0:LANES, 2 * LANES:2 * LANES + 1], oh, K["ones"][:, 0:1], start=True, stop=True)
                    if by_row:
                        pe.matmul(p[0:LANES, 0:D], oh, rows[:, r, 0:D], start=True, stop=True)\
                            .then_inc(S.summed, 1)
                    else:
                        for s in range(halves):
                            last = pe.matmul(p[:, s * LANES:(s + 1) * LANES], rows[:, r, s * D:(s + 1) * D], oh,
                                             start=True, stop=True)
                        last.then_inc(S.summed, 1)

        @block.vector
        def _(dve):
            def build(chunk, h):
                if weighted:
                    for k in range(HALF):
                        slot = rec[:, bass.ds(chunk + k, 1), :].rearrange("p a w -> p (a w)")
                        ins = dve.tensor_scalar(onehot[:, h, k, :], K["iota_row"][:, 0:LANES], slot[:, 1:2],
                                                slot[:, 3:4], ALU.is_equal, ALU.mult)
                else:
                    ins = dve.tensor_tensor(onehot[:, h], K["iota_row"][:, None, 0:LANES].to_broadcast([128, HALF, LANES]),
                                            rec[:, bass.ds(chunk, HALF), 1:2].to_broadcast([128, HALF, LANES]),
                                            ALU.is_equal)
                ins.then_inc(S.onehot, 1)

            dve.memset(agg[:], 0.0).then_inc(S.zeroed, 1)
            if count:
                dve.memset(K["cnt"][:], 0.0).then_inc(S.zeroed, 1)
            dve.sem_inc(S.psum_free, NPS)
            build(0, 0)
            dve.wait_ge(S.zeroed, rnd + (2 if count else 1))
            dve.sem_inc(S.started, 1)
            with dve.Fori(0, TURNS) as i:
                for h in range(G_HALVES):
                    tiles = tiles_of(nc, dve, K["tile1"], i * G_HALVES + h)
                    dve.wait_ge(S.summed, s_base + i * G_RING + ((h + 1) * HALF))
                    build(i * G_RING + (h * HALF + HALF), (h + 1) % G_HALVES)
                    for r in range(h * HALF, h * HALF + HALF):
                        tile = tiles[r % HALF]
                        dve.wait_ge(S.summed, s_base + i * G_RING + (r + G_RING + 1))
                        dve.wait_ge(S.psum_free, f_base + i * G_RING + (r + NPS))
                        p = prod[r % NPS]
                        if count:
                            dve.tensor_tensor(K["cnt"][:, bass.ds(tile, 1)], K["cnt"][:, bass.ds(tile, 1)],
                                              p[0:LANES, 2 * LANES:2 * LANES + 1], ALU.add)
                        if by_row:
                            a = agg[0:LANES, bass.ds(tile * D, D)]
                            dve.tensor_tensor(a, a, p[0:LANES, 0:D], ALU.add).then_inc(S.psum_free, 1)
                        else:
                            a = agg_t[:, :, bass.ds(tile * LANES, LANES)]
                            dve.tensor_tensor(a, a, p[:, 0:halves * LANES]
                                              .rearrange("p (s n) -> p s n", s=halves), ALU.add)\
                                .then_inc(S.psum_free, 1)


def rows_of(area, at):
    return area[0:LANES, at:at + TILES * D].rearrange("p (t f) -> p t f", t=TILES)


def transposed(area, halves):
    return area[:, 0:halves * NODES].rearrange("p (s n) -> p s n", s=halves)


ROWS_A, ROWS_B = 0, TILES * D


class Norm:

    def __init__(self, sb, sem):
        self.stats, self.mean_var, self.rstd = sb("stats", [LANES, 2, 6]), sb("mv", [LANES, 2, 2]), sb("rstd", [LANES, 2])
        self.std = sb("std", [LANES, 2])
        self.var_ok, self.std_ok, self.dve_passed = sem("var_ok"), sem("std_ok"), sem("dve_passed")


def layer_norm(dve, step, g, out, y, norm):
    for j in range(2):
        ins = dve.bn_stats(norm.stats[:, j, :], y[:, j, :])
    step(ins)
    dve.sem_inc(norm.dve_passed, 1)
    for j in range(2):
        ins = dve.bn_aggr(norm.mean_var[:, j, :], norm.stats[:, j, :])
    ins.then_inc(norm.var_ok, 1)
    dve.wait_ge(norm.std_ok, g + 1)
    step(dve.reciprocal(norm.rstd[:], norm.std[:]))
    for j in range(2):
        ins = dve.tensor_scalar(out[:, j, :], y[:, j, :], norm.mean_var[:, j, 0:1], norm.rstd[:, j:j + 1],
                                ALU.subtract, ALU.mult)
    step(ins)


def deviation(act, K, g, norm):
    act.wait_ge(norm.var_ok, g + 1)
    act.activation(norm.std[:], norm.mean_var[:, :, 1], ACT.Sqrt, bias=K["eps"][0:LANES, :]).then_inc(norm.std_ok, 1)


LN_STEPS = 3


def phase(nc, name):
    c = ExitStack()

    def sb(n, shape, dt=F32):
        return c.enter_context(nc.sbuf_tensor(f"{name}_{n}", shape, dt))

    make = semaphores(nc, c)

    def sem(n):
        return make(f"{name}_{n}")

    def bank(n):
        return c.enter_context(nc.psum_tensor(f"{name}_{n}", [128, 512], F32))
    return c, sb, sem, bank


def layer0_nodes(nc, K, T, x, w_l, b_l, w_r, rel_weight):
    c, sb, sem, bank = phase(nc, "l0")
    with c:
        wl, wr, bl = sb("wl", [D, D]), sb("wr", [D, D]), sb("bl", [1, D])
        relw = sb("relw", [D, RELS * D])
        xs, aggs = sb("xs", [LANES, 2, D]), sb("aggs", [D, PAIR])
        xt, x1t = sb("xt", [D, PAIR]), sb("x1t", [D, PAIR])
        inv = sb("inv", [LANES, TILES])
        o, sq, y, x1 = (sb(n, [LANES, 2, D]) for n in ("o", "sq", "y", "x1"))
        ss, l2, inv_norm = sb("ss", [LANES, 2]), sb("norm", [LANES, 2]), sb("inv_norm", [LANES, 2])
        norm = Norm(sb, sem)
        relrow = sb("relrow", [LANES, 2, RELS * D])
        xt_ps, mean_ps, self_ps, x1t_ps = bank("xt_ps"), bank("mean_ps"), bank("self_ps"), bank("x1t_ps")
        rel_ps = [bank(f"rel_ps{i}") for i in range(4)]
        loaded, step_s, ss_ok, norm_ok = sem("loaded"), sem("step"), sem("ss_ok"), sem("norm_ok")
        staged = sem("staged")
        xt_ps_ok, xt_ok = sem("xt_ps_ok"), sem("xt_ok")
        sums_ok, sums_used = sem("sums_ok"), sem("sums_used")
        x1_ok, x1_kept = sem("x1_ok"), sem("x1_kept")
        x1t_ps_ok, x1t_ok = sem("x1t_ps_ok"), sem("x1t_ok")
        rel_ps_ok, rel_ok = sem("rel_ps_ok"), sem("rel_ok")
        relrow_free, stored = sem("relrow_free"), sem("stored")
        block = c.enter_context(nc.Block())
        xrows, x1rows = rows_of(K["state"], ROWS_A), rows_of(K["state"], ROWS_B)
        agg = K["agg"]

        @block.sync
        def _(sp):
            sp.dma_start(K["state"][0:LANES, 0:TILES * D], x.rearrange("(p t) f -> p (t f)", p=LANES))\
                .then_inc(loaded, 16)
            sp.dma_start(wl[:], w_l).then_inc(loaded, 16)
            sp.dma_start(wr[:], w_r).then_inc(loaded, 16)
            sp.dma_start(bl[:], b_l.rearrange("(a f) -> a f", a=1)).then_inc(loaded, 16)
            for r in range(RELS):
                sp.dma_start(relw[:, r * D:(r + 1) * D], rel_weight[r]).then_inc(loaded, 16)
            sp.sem_inc(relrow_free, 1)
            with sp.Fori(0, PAIRS) as g:
                sp.wait_ge(rel_ok, g + 2)
                sp.dma_start(T["rel"].rearrange("(p t r) f -> p t (r f)", p=LANES, r=RELS)[:, bass.ds(g * 2, 2), :],
                             relrow[:]).then_inc(stored, 16)
                sp.wait_ge(stored, g * 16 + 16)
                sp.sem_inc(relrow_free, 1)

        @block.gpsimd
        def _(pool):
            def stage(g):
                pool.tensor_copy(xs[:], xrows[:, bass.ds(g * 2, 2), :]).then_inc(staged, 1)
                pool.tensor_copy(aggs[:], agg[:, bass.ds(g * PAIR, PAIR)]).then_inc(staged, 1)

            pool.wait_ge(loaded, 16 * 12)
            pool.sem_inc(x1_kept, 1)
            stage(0)
            with pool.Fori(0, PAIRS - 1) as g:
                pool.wait_ge(sums_ok, g + 1)
                pool.wait_ge(x1_ok, g + 1)
                pool.tensor_copy(x1rows[:, bass.ds(g * 2, 2), :], x1[:]).then_inc(x1_kept, 1)
                stage(g + 1)
            pool.wait_ge(x1_ok, PAIRS)
            pool.tensor_copy(x1rows[:, TILES - 2:TILES, :], x1[:]).then_inc(x1_kept, 1)

        @block.tensor
        def _(pe):
            def front(g, first):
                pe.wait_ge(staged, g * 2 + 2)
                for j in range(2):
                    last = pe.transpose(xt_ps[:, j * LANES:(j + 1) * LANES], xs[:, j, :],
                                        K["ident"][0:LANES, 0:LANES])
                last.then_inc(xt_ps_ok, 1)
                if not first:
                    pe.wait_ge(sums_used, g)
                for j in range(2):
                    pe.matmul(mean_ps[0:LANES, j * D:(j + 1) * D], aggs[:, j * LANES:(j + 1) * LANES], wl[:],
                              start=True, stop=True)
                pe.wait_ge(xt_ok, g + 1)
                for j in range(2):
                    out = self_ps[0:LANES, j * D:(j + 1) * D]
                    pe.matmul(out, xt[:, j * LANES:(j + 1) * LANES], wr[:], start=True, stop=False)
                    last = pe.matmul(out, K["ones"][0:1, 0:LANES], bl[:], start=False, stop=True)
                last.then_inc(sums_ok, 1)

            def back(g):
                pe.wait_ge(x1_ok, g + 1)
                for j in range(2):
                    last = pe.transpose(x1t_ps[:, j * LANES:(j + 1) * LANES], x1[:, j, :],
                                        K["ident"][0:LANES, 0:LANES])
                last.then_inc(x1t_ps_ok, 1)
                pe.wait_ge(x1t_ok, g + 1)
                pe.wait_ge(rel_ok, g + 1)
                for j in range(2):
                    for h in range(2):
                        last = pe.matmul(rel_ps[2 * j + h][0:LANES, :], x1t[:, j * LANES:(j + 1) * LANES],
                                         relw[:, h * 512:(h + 1) * 512], start=True, stop=True)
                last.then_inc(rel_ps_ok, 1)

            pe.wait_ge(loaded, 16 * 12)
            pe.sem_inc(x1t_ps_ok, 1)
            front(0, True)
            with pe.Fori(0, PAIRS - 1) as g:
                front(g + 1, False)
                back(g)
            back(PAIRS - 1)

        @block.scalar
        def _(act):
            def copy_xt(g):
                act.wait_ge(xt_ps_ok, g + 1)
                act.copy(xt[:], xt_ps[:, 0:PAIR]).then_inc(xt_ok, 1)

            def norms(g):
                act.wait_ge(ss_ok, g + 1)
                act.activation(l2[:], ss[:], ACT.Sqrt).then_inc(norm_ok, 1)
                deviation(act, K, g, norm)

            def copy_rel(g):
                act.wait_ge(x1t_ps_ok, g + 2)
                act.copy(x1t[:], x1t_ps[:, 0:PAIR]).then_inc(x1t_ok, 1)
                act.wait_ge(rel_ps_ok, g + 1)
                act.wait_ge(relrow_free, g + 1)
                for q in range(4):
                    last = act.copy(relrow[:, q // 2, (q % 2) * 512:(q % 2 + 1) * 512], rel_ps[q][0:LANES, :])
                last.then_inc(rel_ok, 1)

            act.sem_inc(rel_ok, 1)
            copy_xt(0)
            with act.Fori(0, PAIRS - 1) as g:
                norms(g)
                copy_xt(g + 1)
                copy_rel(g)
            norms(PAIRS - 1)
            copy_rel(PAIRS - 1)

        @block.vector
        def _(dve):
            step = Steps(dve, step_s)
            step(dve.tensor_single_scalar(inv[:], K["cnt"][:], 1.0, ALU.max))
            step(dve.reciprocal(inv[:], inv[:]))
            at = step.done
            per_pair = 6 + LN_STEPS
            with dve.Fori(0, PAIRS) as g:
                step.done = at + g * per_pair
                dve.wait_ge(sums_ok, g + 1)
                for j in range(2):
                    ins = dve.tensor_scalar(o[:, j, :], mean_ps[0:LANES, j * D:(j + 1) * D],
                                            inv[:, bass.ds(g * 2 + j, 1)], None, ALU.mult)
                step(ins)
                step(dve.tensor_tensor(o[:], o[:], self_ps[0:LANES, 0:2 * D].rearrange("p (j f) -> p j f", j=2),
                                       ALU.add))
                dve.sem_inc(sums_used, 1)
                step(dve.tensor_tensor(sq[:], o[:], o[:], ALU.mult))
                step(dve.tensor_reduce(ss[:], sq[:], AX.X, ALU.add))
                dve.tensor_single_scalar(ss[:], ss[:], NORM_EPS * NORM_EPS, ALU.max).then_inc(ss_ok, 1)
                dve.wait_ge(norm_ok, g + 1)
                step(dve.reciprocal(inv_norm[:], l2[:]))
                for j in range(2):
                    ins = dve.scalar_tensor_tensor(y[:, j, :], o[:, j, :], inv_norm[:, j:j + 1],
                                                   xrows[:, bass.ds(g * 2 + j, 1), :].rearrange("p a f -> p (a f)"),
                                                   ALU.mult, ALU.add)
                step(ins)
                dve.wait_ge(x1_kept, g + 1)
                dve.wait_ge(x1t_ps_ok, g + 1)
                layer_norm(dve, step, g, x1, y, norm)
                dve.sem_inc(x1_ok, 1)


def layer1_nodes(nc, K, T, bias):
    c, sb, sem, bank = phase(nc, "l1")
    with c:
        bias_all = sb("bias_all", [LANES, D])
        y, x2 = sb("y", [LANES, 2, D]), sb("x2", [LANES, 2, D])
        norm = Norm(sb, sem)
        tr = bank("tr")
        loaded, step_s = sem("loaded"), sem("step")
        x2_ok, x2_kept = sem("x2_ok"), sem("x2_kept")
        tr_ok, tr_free = sem("tr_ok"), sem("tr_free")
        block = c.enter_context(nc.Block())
        sums = rows_of(K["agg"], ROWS_A)
        rows = rows_of(K["state"], ROWS_B)

        @block.sync
        def _(sp):
            sp.dma_start(bias_all[:], bias.rearrange("(a f) -> a f", a=1).to_broadcast([LANES, D]))\
                .then_inc(loaded, 16)

        @block.gpsimd
        def _(pool):
            pool.sem_inc(x2_kept, 1)
            with pool.Fori(0, PAIRS) as g:
                pool.wait_ge(x2_ok, g + 1)
                pool.tensor_copy(rows[:, bass.ds(g * 2, 2), :], x2[:]).then_inc(x2_kept, 1)

        @block.tensor
        def _(pe):
            pe.sem_inc(tr_ok, 1)
            with pe.Fori(0, PAIRS) as g:
                pe.wait_ge(x2_ok, g + 1)
                pe.wait_ge(tr_free, g + 1)
                for j in range(2):
                    last = pe.transpose(tr[:, j * LANES:(j + 1) * LANES], x2[:, j, :], K["ident"][0:LANES, 0:LANES])
                last.then_inc(tr_ok, 1)

        @block.scalar
        def _(act):
            act.sem_inc(tr_free, 1)
            with act.Fori(0, PAIRS) as g:
                deviation(act, K, g, norm)
                act.wait_ge(tr_ok, g + 2)
                act.copy(K["state"][:, bass.ds(g * PAIR, PAIR)], tr[:, 0:PAIR]).then_inc(tr_free, 1)

        @block.vector
        def _(dve):
            step = Steps(dve, step_s)
            dve.wait_ge(loaded, 16)
            dve.sem_inc(step_s, 1)
            with dve.Fori(0, PAIRS) as g:
                step.done = g * (2 + LN_STEPS) + 1
                pair = bass.ds(g * 2, 2)
                step(dve.tensor_tensor(y[:], sums[:, pair, :], bias_all[:, None, :].to_broadcast([LANES, 2, D]),
                                       ALU.add))
                step(dve.scalar_tensor_tensor(y[:], y[:], 0.0, rows[:, pair, :], ALU.max, ALU.add))
                dve.wait_ge(x2_kept, g + 1)
                dve.wait_ge(tr_ok, g + 1)
                layer_norm(dve, step, g, x2, y, norm)
                dve.sem_inc(x2_ok, 1)


def first_state(nc, K, T):
    c, sb, sem, bank = phase(nc, "fs")
    with c:
        stored, cleared = sem("stored"), sem("cleared")
        zeros = sb("zeros", [LANES, 10 * D])
        block = c.enter_context(nc.Block())
        rows = rows_of(K["state"], ROWS_B)

        @block.sync
        def _(sp):
            state = T["state"].rearrange("(p t) w -> p t w", p=LANES)
            sp.dma_start(T["x2"].rearrange("(p t) f -> p t f", p=LANES), rows).then_inc(stored, 16)
            sp.dma_start(state[:, :, 0:D], rows).then_inc(stored, 16)
            sp.wait_ge(cleared, 1)
            for q in range(5):
                sp.dma_start(state[:, q * 10:(q + 1) * 10, D:STATE], zeros[:].rearrange("p (t f) -> p t f", t=10))\
                    .then_inc(stored, 16)
            sp.wait_ge(stored, 16 * 7)

        @block.vector
        def _(dve):
            dve.memset(zeros[:], 0.0).then_inc(cleared, 1)
            dve.wait_ge(stored, 16 * 7)
            dve.memset(K["state"][:, NODES:2 * NODES], 0.0).then_inc(cleared, 1)


def gated_weights(nc, K, w_ih, w_hh, b_ih, b_hh, l0_w, l1_w):
    c, sb, sem, bank = phase(nc, "gw")
    with c:
        jobs = []
        plan = (("w_ih", w_ih, K["w_ih_t"]), ("w_hh", w_hh, K["w_hh_t"]), ("l0_w", l0_w, K["l0_t"]),
                ("l1_w", l1_w, K["l1_t"]))
        raw = []
        for name, w, t in plan:
            raw.append(sb(name, [128, w.shape[0] // 128, w.shape[1]]))
            for q in range(w.shape[0] // 128):
                for k in range(w.shape[1] // 128):
                    jobs.append((raw[-1][:, q, k * 128:(k + 1) * 128], t[:, k, q * 128:(q + 1) * 128]))
        b_raw = [sb("b_ih", [128, 6]), sb("b_hh", [128, 6])]
        tr = [bank("tr0"), bank("tr1")]
        loaded, tr_ok, tr_used = sem("loaded"), sem("tr_ok"), sem("tr_used")
        block = c.enter_context(nc.Block())

        @block.sync
        def _(sp):
            for (name, w, t), r in zip(plan, raw):
                sp.dma_start(r[:], w.rearrange("(q p) k -> p q k", p=128)).then_inc(loaded, 16)
            with nc.allow_non_contiguous_dma(reason="a few biases by partition"):
                for b, r in zip((b_ih, b_hh), b_raw):
                    sp.dma_start(r[:], b.rearrange("(q p) -> p q", p=128)).then_inc(loaded, 16)

        @block.tensor
        def _(pe):
            pe.wait_ge(loaded, 16 * 6)
            for n, (src, _) in enumerate(jobs):
                if n >= 2:
                    pe.wait_ge(tr_used, n - 1)
                pe.transpose(tr[n % 2][:, 0:128], src, K["ident"][:]).then_inc(tr_ok, 1)

        @block.scalar
        def _(act):
            for n, (_, dst) in enumerate(jobs):
                act.wait_ge(tr_ok, n + 1)
                act.copy(dst, tr[n % 2][:, 0:128]).then_inc(tr_used, 1)

        @block.vector
        def _(dve):
            dve.wait_ge(loaded, 16 * 6)
            dve.tensor_tensor(K["b_rz"][:], b_raw[0][:, 0:4], b_raw[1][:, 0:4], ALU.add)
            dve.tensor_copy(K["b_n"][:, 0, :], b_raw[0][:, 4:6])
            dve.tensor_copy(K["b_n"][:, 1, :], b_raw[1][:, 4:6])


class WeightSems:
    def __init__(self, make):
        def sem(n):
            return make(f"cw_{n}")
        self.loaded, self.tr_ok, self.wt_ok, self.prod_ok = sem("loaded"), sem("tr_ok"), sem("wt_ok"), sem("prod_ok")


def combined_weight(nc, K, S, rnd, w):
    c, sb, sem, bank = phase(nc, "cw")
    with c:
        raw = sb("raw", [128, 2, STATE])
        wt = sb("wt", [128, 2, STATE])
        tr = bank("tr")
        prod = [bank(f"prod{i}") for i in range(4)]
        block = c.enter_context(nc.Block())
        N3 = GATES // 2

        @block.sync
        def _(sp):
            sp.dma_start(raw[:], w[bass.ds(rnd, 1), :, :].rearrange("a (s p) m -> p (a s) m", p=128))\
                .then_inc(S.loaded, 16)

        @block.tensor
        def _(pe):
            pe.wait_ge(S.loaded, rnd * 16 + 16)
            for s in range(2):
                for m in range(2):
                    last = pe.transpose(tr[:, (m * 2 + s) * 128:(m * 2 + s + 1) * 128],
                                        raw[:, s, m * 128:(m + 1) * 128], K["ident"][:])
            last.then_inc(S.tr_ok, 1)
            pe.wait_ge(S.wt_ok, rnd + 1)
            for s in range(2):
                for h in range(2):
                    for m in range(2):
                        last = pe.matmul(prod[2 * s + h][:, 0:N3], wt[:, m, s * 128:(s + 1) * 128],
                                         K["w_ih_t"][:, m, h * N3:(h + 1) * N3], start=(m == 0), stop=(m == 1))
            last.then_inc(S.prod_ok, 1)

        @block.scalar
        def _(act):
            act.wait_ge(S.tr_ok, rnd + 1)
            act.copy(wt[:].rearrange("p m s -> p (m s)"), tr[:]).then_inc(S.wt_ok, 1)
            act.wait_ge(S.prod_ok, rnd + 1)
            for s in range(2):
                act.copy(K["w_comb"][:, s, 0:N3], prod[2 * s][:, 0:N3])

        @block.vector
        def _(dve):
            dve.wait_ge(S.prod_ok, rnd + 1)
            for s in range(2):
                dve.tensor_copy(K["w_comb"][:, s, N3:GATES], prod[2 * s + 1][:, 0:N3])


class GateSems:
    def __init__(self, make):
        def sem(n):
            return make(f"gru_{n}")
        self.r_ps, self.z_ps, self.n_ps, self.h_ps = sem("r_ps"), sem("z_ps"), sem("n_ps"), sem("h_ps")
        self.r_ok, self.z_ok = sem("r_ok"), sem("z_ok")
        self.t_ok, self.u_ok, self.n_ok = sem("t_ok"), sem("u_ok"), sem("n_ok")
        self.step, self.new_ok = sem("step"), sem("new_ok")
        self.tr_ok, self.row_ok = sem("tr_ok"), sem("row_ok")
        self.row_free, self.stored = sem("row_free"), sem("stored")
        self.edges_in, self.staged, self.issued = sem("edges_in"), sem("staged"), sem("issued")


def gated_update(nc, K, T, S, scattered, rnd, rounds):
    cols = EDGE_COLS // rounds
    turns = cols // RING
    assert cols * rounds == EDGE_COLS and turns * RING == cols
    c, sb, sem, bank = phase(nc, "gru")
    with c:
        gr, gz, u, ng, dd, new = (sb(n, [128, 2, PAIR]) for n in ("gr", "gz", "u", "ng", "dd", "new"))
        row = sb("row", [LANES, 2, STATE])
        targets = sb("targets", [LANES, cols], I32)
        target_stage, edge_stage = sb("target_stage", [LANES, RING], I32), sb("edge_stage", [LANES, RING, REC2])
        edges = K["rows"][0:LANES].rearrange("p r w -> p (r w)")[:, 0:cols * REC2]\
            .rearrange("p (c w) -> p c w", w=REC2)
        r_b, z_b, n_b, h_b, tr = (bank(n) for n in ("r", "z", "n", "h", "tr"))
        block = c.enter_context(nc.Block())
        state, agg = transposed(K["state"], 2), transposed(K["agg"], 2)
        w_comb, w_hh = K["w_comb"], K["w_hh_t"]
        base = rnd * PAIRS
        credit = rnd * (PAIRS + 1)

        def half(b, s):
            return b[:, s * PAIR:(s + 1) * PAIR]

        @block.tensor
        def _(pe):
            def gates(g, first):
                cols = bass.ds(g * PAIR, PAIR)

                def product(b, gate, sums, states):
                    for s in range(2):
                        terms = [(w_comb, agg, k) for k in range(2) if sums] + \
                                [(w_hh, state, k) for k in range(2) if states]
                        out = slice(gate * STATE + s * 128, gate * STATE + (s + 1) * 128)
                        for n, (w, v, k) in enumerate(terms):
                            last = pe.matmul(half(b, s), w[:, k, out], v[:, k, cols],
                                             start=(n == 0), stop=(n == len(terms) - 1))
                    return last

                if not first:
                    pe.wait_ge(S.r_ok, base + g)
                product(r_b, 0, True, True).then_inc(S.r_ps, 1)
                if not first:
                    pe.wait_ge(S.t_ok, base + g)
                product(h_b, 2, False, True).then_inc(S.h_ps, 1)
                if not first:
                    pe.wait_ge(S.u_ok, base + g)
                product(n_b, 2, True, False).then_inc(S.n_ps, 1)
                if not first:
                    pe.wait_ge(S.z_ok, base + g)
                product(z_b, 1, True, True).then_inc(S.z_ps, 1)

            def rows(g):
                pe.wait_ge(S.new_ok, base + g + 1)
                pe.wait_ge(S.row_ok, credit + g + 1)
                for j in range(2):
                    for s in range(2):
                        last = pe.transpose(tr[0:LANES, (j * 2 + s) * 128:(j * 2 + s + 1) * 128],
                                            new[:, s, j * LANES:(j + 1) * LANES], K["ident"][:])
                last.then_inc(S.tr_ok, 1)

            pe.sem_inc(S.tr_ok, 1)
            gates(0, True)
            with pe.Fori(0, PAIRS - 1) as g:
                gates(g + 1, False)
                rows(g)
            rows(PAIRS - 1)

        @block.scalar
        def _(act):
            def gate(g):
                act.wait_ge(S.r_ps, base + g + 1)
                act.activation(gr[:, 0, :], half(r_b, 0), ACT.Sigmoid, bias=K["b_rz"][:, 0:1])
                act.activation(gr[:, 1, :], half(r_b, 1), ACT.Sigmoid, bias=K["b_rz"][:, 1:2]).then_inc(S.r_ok, 1)
                act.wait_ge(S.z_ps, base + g + 1)
                act.activation(gz[:, 0, :], half(z_b, 0), ACT.Sigmoid, bias=K["b_rz"][:, 2:3])
                act.activation(gz[:, 1, :], half(z_b, 1), ACT.Sigmoid, bias=K["b_rz"][:, 3:4]).then_inc(S.z_ok, 1)
                act.wait_ge(S.u_ok, base + g + 1)
                act.activation(ng[:, 0, :], u[:, 0, :], ACT.Tanh, bias=K["b_n"][:, 0, 0:1])
                act.activation(ng[:, 1, :], u[:, 1, :], ACT.Tanh, bias=K["b_n"][:, 0, 1:2]).then_inc(S.n_ok, 1)

            def rows(g):
                act.wait_ge(S.tr_ok, credit + g + 2)
                act.wait_ge(S.row_free, credit + g + 1)
                act.copy(row[:].rearrange("p j w -> p (j w)"), tr[0:LANES, :]).then_inc(S.row_ok, 1)

            act.sem_inc(S.row_ok, 1)
            gate(0)
            with act.Fori(0, PAIRS - 1) as g:
                act.wait_ge(S.new_ok, base + g + 1)
                gate(g + 1)
                rows(g)
            rows(PAIRS - 1)

        @block.vector
        def _(dve):
            step = Steps(dve, S.step)
            with dve.Fori(0, PAIRS) as g:
                step.done = (base + g) * 6
                pair = bass.ds(g * PAIR, PAIR)
                dve.wait_ge(S.r_ok, base + g + 1)
                dve.wait_ge(S.h_ps, base + g + 1)
                for s in range(2):
                    last = dve.scalar_tensor_tensor(u[:, s, :], half(h_b, s), K["b_n"][:, 1, s:s + 1], gr[:, s, :],
                                                    ALU.add, ALU.mult)
                step(last)
                dve.sem_inc(S.t_ok, 1)
                dve.wait_ge(S.n_ps, base + g + 1)
                step(dve.tensor_tensor(u[:], u[:], n_b[:, 0:2 * PAIR].rearrange("p (s n) -> p s n", s=2), ALU.add))
                dve.sem_inc(S.u_ok, 1)
                dve.wait_ge(S.n_ok, base + g + 1)
                dve.wait_ge(S.z_ok, base + g + 1)
                step(dve.tensor_tensor(dd[:], state[:, :, pair], ng[:], ALU.subtract))
                step(dve.tensor_tensor(dd[:], dd[:], gz[:], ALU.mult))
                dve.wait_ge(S.tr_ok, credit + g + 1)
                step(dve.tensor_tensor(new[:], dd[:], ng[:], ALU.add))
                dve.sem_inc(S.new_ok, 1)
                step(dve.tensor_copy(state[:, :, pair], new[:]))

        @block.gpsimd
        def _(pool):
            def turn(i, first):
                for h in range(2):
                    stage = slice(h * HALF, h * HALF + HALF)
                    at = bass.ds(i * RING + h * HALF, HALF)
                    if not first:
                        pool.wait_ge(scattered[h], (rnd * turns + i) * (16 * HALF))
                    pool.tensor_copy(target_stage[:, stage], targets[:, at]).then_inc(S.staged, 1)
                    pool.tensor_copy(edge_stage[:, stage, :], edges[:, at, :]).then_inc(S.staged, 1)
                    pool.wait_ge(S.staged, (rnd * turns + i) * 4 + (2 * h + 2))
                    pool.sem_inc(S.issued, 1)
                    for r in range(h * HALF, h * HALF + HALF):
                        pool.indirect_dma_start(
                            out=T["slots2"],
                            out_offset=bass.IndirectOffsetOnAxis(ap=target_stage[:, r:r + 1], axis=0),
                            in_=edge_stage[:, r, :], in_offset=None).then_inc(scattered[h], 16)

            pool.wait_ge(S.edges_in, rnd * 32 + 32)
            pool.sem_inc(S.issued, 1)
            turn(0, True)
            with pool.Fori(1, turns) as i:
                turn(i, False)
            for h in range(2):
                pool.wait_ge(scattered[h], (rnd + 1) * (turns * 16 * HALF))
            pool.sem_inc(S.issued, 1)

        @block.sync
        def _(sp):
            part = bass.ds(rnd * cols, cols)
            sp.dma_start(targets[:], T["rows2"].rearrange("(p c) -> p c", p=LANES)[:, part]).then_inc(S.edges_in, 16)
            sp.dma_start(edges, T["edges2"].rearrange("(p c) w -> p c w", p=LANES)[:, part, :])\
                .then_inc(S.edges_in, 16)
            table = T["state"].rearrange("(p t) w -> p t w", p=LANES)
            sp.sem_inc(S.row_free, 1)
            with sp.Fori(0, PAIRS) as g:
                sp.wait_ge(S.row_ok, credit + g + 2)
                sp.dma_start(table[:, bass.ds(g * 2, 2), :], row[:]).then_inc(S.stored, 16)
                sp.wait_ge(S.stored, (base + g) * 16 + 16)
                sp.sem_inc(S.row_free, 1)


def layer2_nodes(nc, K, T, l0_b, l1_b, e_w1, e_b1):
    c, sb, sem, bank = phase(nc, "l2")
    with c:
        b0, b1 = sb("b0", [128, 2]), sb("b1", [LANES, D])
        w_edge = sb("w_edge", [D, 2, D])
        b_edge = sb("b_edge", [1, D])
        xs, xt = sb("xs", [LANES, 2, D]), sb("xt", [D, PAIR])
        hid = sb("hid", [D, 2, PAIR])
        y, x3, x3t = sb("y", [LANES, 2, D]), sb("x3", [LANES, 2, D]), sb("x3t", [D, PAIR])
        colrow = sb("colrow", [LANES, 2, D])
        norm = Norm(sb, sem)
        xt_ps, hid_ps, y_ps, x3t_ps, proj_ps = (bank(n) for n in ("xt_ps", "hid_ps", "y_ps", "x3t_ps", "proj_ps"))
        loaded, staged, step_s = sem("loaded"), sem("staged"), sem("step")
        xt_ps_ok, xt_ok, hid_ps_ok, hid_ok, y_ps_ok, y_used = (
            sem("xt_ps_ok"), sem("xt_ok"), sem("hid_ps_ok"), sem("hid_ok"), sem("y_ps_ok"), sem("y_used"))
        x3_ok, x3_kept, x3t_ps_ok, x3t_ok = sem("x3_ok"), sem("x3_kept"), sem("x3t_ps_ok"), sem("x3t_ok")
        proj_ps_ok, proj_ok, col_free, stored = sem("proj_ps_ok"), sem("proj_ok"), sem("col_free"), sem("stored")
        block = c.enter_context(nc.Block())
        rows, source_rows = rows_of(K["agg"], ROWS_A), rows_of(K["agg"], ROWS_B)
        state = transposed(K["state"], 2)
        LOADED = 16 * 6

        @block.sync
        def _(sp):
            sp.dma_start(rows, T["x2"].rearrange("(p t) f -> p t f", p=LANES)).then_inc(loaded, 16)
            with nc.allow_non_contiguous_dma(reason="a few biases by partition"):
                sp.dma_start(b0[:], l0_b.rearrange("(q p) -> p q", p=128)).then_inc(loaded, 16)
            sp.dma_start(b1[:], l1_b.rearrange("(a f) -> a f", a=1).to_broadcast([LANES, D])).then_inc(loaded, 16)
            for k in range(2):
                sp.dma_start(w_edge[:, k, :], e_w1[k * D:(k + 1) * D, :]).then_inc(loaded, 16)
            sp.dma_start(b_edge[:], e_b1.rearrange("(a f) -> a f", a=1)).then_inc(loaded, 16)
            sp.sem_inc(col_free, 1)
            with sp.Fori(0, PAIRS) as g:
                sp.wait_ge(proj_ok, g + 2)
                sp.dma_start(T["xcol"].rearrange("(p t) f -> p t f", p=LANES)[:, bass.ds(g * 2, 2), :], colrow[:])\
                    .then_inc(stored, 16)
                sp.wait_ge(stored, g * 16 + 16)
                sp.sem_inc(col_free, 1)

        @block.gpsimd
        def _(pool):
            def stage(g):
                pool.tensor_copy(xs[:], rows[:, bass.ds(g * 2, 2), :]).then_inc(staged, 1)

            pool.wait_ge(loaded, LOADED)
            pool.sem_inc(x3_kept, 1)
            stage(0)
            with pool.Fori(0, PAIRS - 1) as g:
                pool.wait_ge(y_ps_ok, g + 1)
                pool.wait_ge(x3_ok, g + 1)
                stage(g + 1)
                pool.tensor_copy(rows[:, bass.ds(g * 2, 2), :], x3[:]).then_inc(x3_kept, 1)
            pool.wait_ge(x3_ok, PAIRS)
            pool.tensor_copy(rows[:, TILES - 2:TILES, :], x3[:]).then_inc(x3_kept, 1)

        @block.tensor
        def _(pe):
            def front(g):
                pe.wait_ge(staged, g + 1)
                for j in range(2):
                    last = pe.transpose(xt_ps[:, j * LANES:(j + 1) * LANES], xs[:, j, :],
                                        K["ident"][0:LANES, 0:LANES])
                last.then_inc(xt_ps_ok, 1)
                pe.wait_ge(xt_ok, g + 1)
                pe.wait_ge(hid_ok, g + 1)
                for s in range(2):
                    for k in range(3):
                        v = xt[:] if k == 2 else state[:, k, bass.ds(g * PAIR, PAIR)]
                        last = pe.matmul(hid_ps[:, s * PAIR:(s + 1) * PAIR], K["l0_t"][:, k, s * 128:(s + 1) * 128],
                                         v, start=(k == 0), stop=(k == 2))
                last.then_inc(hid_ps_ok, 1)

            def middle(g):
                pe.wait_ge(hid_ok, g + 2)
                pe.wait_ge(y_used, g + 1)
                for j in range(2):
                    for k in range(2):
                        last = pe.matmul(y_ps[0:LANES, j * D:(j + 1) * D], hid[:, k, j * LANES:(j + 1) * LANES],
                                         K["l1_t"][:, k, :], start=(k == 0), stop=(k == 1))
                last.then_inc(y_ps_ok, 1)

            def back(g):
                pe.wait_ge(x3_ok, g + 1)
                for j in range(2):
                    last = pe.transpose(x3t_ps[:, j * LANES:(j + 1) * LANES], x3[:, j, :],
                                        K["ident"][0:LANES, 0:LANES])
                last.then_inc(x3t_ps_ok, 1)
                pe.wait_ge(x3t_ok, g + 1)
                pe.wait_ge(proj_ok, g + 1)
                for j in range(2):
                    v = x3t[:, j * LANES:(j + 1) * LANES]
                    at_source, at_dest = (proj_ps[0:LANES, (2 * j + k) * D:(2 * j + k + 1) * D] for k in range(2))
                    pe.matmul(at_source, v, w_edge[:, 0, :], start=True, stop=False)
                    pe.matmul(at_source, K["ones"][0:1, 0:LANES], b_edge[:], start=False, stop=True)
                    last = pe.matmul(at_dest, v, w_edge[:, 1, :], start=True, stop=True)
                last.then_inc(proj_ps_ok, 1)

            pe.wait_ge(loaded, LOADED)
            pe.sem_inc(x3t_ps_ok, 1)
            front(0)
            middle(0)
            with pe.Fori(0, PAIRS - 1) as g:
                front(g + 1)
                back(g)
                middle(g + 1)
            back(PAIRS - 1)

        @block.scalar
        def _(act):
            def front(g):
                act.wait_ge(xt_ps_ok, g + 1)
                act.copy(xt[:], xt_ps[:, 0:PAIR]).then_inc(xt_ok, 1)
                act.wait_ge(hid_ps_ok, g + 1)
                for s in range(2):
                    last = act.activation(hid[:, s, :], hid_ps[:, s * PAIR:(s + 1) * PAIR], ACT.Relu,
                                          bias=b0[:, s:s + 1])
                last.then_inc(hid_ok, 1)

            def back(g):
                act.wait_ge(x3t_ps_ok, g + 2)
                act.copy(x3t[:], x3t_ps[:, 0:PAIR]).then_inc(x3t_ok, 1)
                act.wait_ge(proj_ps_ok, g + 1)
                act.wait_ge(col_free, g + 1)
                proj = proj_ps[0:LANES, :].rearrange("p (j k f) -> p j k f", j=2, k=2)
                act.copy(source_rows[:, bass.ds(g * 2, 2), :], proj[:, :, 0, :])
                act.copy(colrow[:], proj[:, :, 1, :]).then_inc(proj_ok, 1)

            act.wait_ge(loaded, LOADED)
            act.sem_inc(hid_ok, 1)
            act.sem_inc(proj_ok, 1)
            front(0)
            with act.Fori(0, PAIRS - 1) as g:
                deviation(act, K, g, norm)
                act.wait_ge(y_ps_ok, g + 1)
                front(g + 1)
                back(g)
            deviation(act, K, PAIRS - 1, norm)
            back(PAIRS - 1)

        @block.vector
        def _(dve):
            step = Steps(dve, step_s)
            dve.wait_ge(loaded, LOADED)
            dve.sem_inc(y_used, 1)
            with dve.Fori(0, PAIRS) as g:
                step.done = g * (2 + LN_STEPS)
                dve.wait_ge(y_ps_ok, g + 1)
                step(dve.tensor_tensor(y[:], y_ps[0:LANES, 0:2 * D].rearrange("p (j f) -> p j f", j=2),
                                       b1[:, None, :].to_broadcast([LANES, 2, D]), ALU.add))
                dve.sem_inc(y_used, 1)
                step(dve.scalar_tensor_tensor(y[:], y[:], 0.0, rows[:, bass.ds(g * 2, 2), :], ALU.max, ALU.add))
                dve.wait_ge(x3_kept, g + 1)
                dve.wait_ge(x3t_ps_ok, g + 1)
                layer_norm(dve, step, g, x3, y, norm)
                dve.sem_inc(x3_ok, 1)


def edge_mlp(nc, K, T, row_in, e_w1, e_w2, e_b2):
    c, sb, sem, bank = phase(nc, "l3")
    with c:
        HALVES = CHUNKS // HALF
        W = HALF * D
        LEAD = 3
        w_attr = sb("w_attr", [HALF * REC2, W])
        w2, b2 = sb("w2", [D, D]), sb("b2", [128, D])
        slots = sb("slots", [128, DEEP, HALF, REC2])
        idx = sb("idx", [128, FETCH * HALF], I32)
        gathered = sb("gathered", [128, FETCH, W])
        onehot = sb("onehot", [128, DEEP, HALF, LANES])
        onehot_t, slots_t = sb("onehot_t", [LANES, 2, HALF * SLOT]), sb("slots_t", [HALF * REC2, 2, SLOT])
        pre1, hid, hid_t = sb("pre1", [128, W]), sb("hid", [128, 2, W]), sb("hid_t", [D, 2, HALF * SLOT])
        pre2, msg = sb("pre2", [128, W]), sb("msg", [128, 2, W])
        onehot_ps, slots_ps, hid_ps, hid_t_ps, msg_ps, sum_ps = (
            bank(n) for n in ("onehot_ps", "slots_ps", "hid_ps", "hid_t_ps", "msg_ps", "sum_ps"))
        loaded, zeroed = sem("loaded"), sem("zeroed")
        slots_in = [sem(f"slots_in{q}") for q in range(DEEP)]
        idx_ok, issued, onehot_ok = sem("idx_ok"), sem("issued"), sem("onehot_ok")
        tr_ps_ok, tr_ok = sem("tr_ps_ok"), sem("tr_ok")
        hid_ps_ok, pre1_ok, hid_ok = sem("hid_ps_ok"), sem("pre1_ok"), sem("hid_ok")
        hid_t_ps_ok, hid_t_ok = sem("hid_t_ps_ok"), sem("hid_t_ok")
        msg_ps_ok, pre2_ok, msg_ok = sem("msg_ps_ok"), sem("pre2_ok"), sem("msg_ok")
        sum_ok, added = sem("sum_ok"), sem("added")
        block = c.enter_context(nc.Block())
        source_rows = rows_of(K["agg"], ROWS_B)
        sums = K["state"]

        def number(i, off):
            return off if i is None else i * DEEP + off

        def run(eng, step):
            for j in range(-LEAD, DEEP):
                step(None, j)
            with eng.Fori(0, HALVES // DEEP - 2) as i:
                for q in range(DEEP):
                    step(i, DEEP + q)
            for j in range(HALVES - DEEP, HALVES + LEAD):
                step(None, j)

        def exists(i, off):
            return i is not None or 0 <= off < HALVES

        def wait_half(eng, s, i, off):
            if i is not None or off >= 0:
                eng.wait_ge(s, number(i, off) + 1)

        def wait_slots(eng, i, off):
            turn = off // DEEP if i is None else i + off // DEEP
            eng.wait_ge(slots_in[off % DEEP], turn * 16 + 16)

        @block.sync
        def _(sp):
            sp.wait_ge(zeroed, 2)
            for k in range(HALF):
                sp.dma_start(w_attr[k * REC2 + 2:(k + 1) * REC2, k * D:(k + 1) * D], e_w1[2 * D:2 * D + ATTR, :])\
                    .then_inc(loaded, 16)
            sp.dma_start(w2[:], e_w2).then_inc(loaded, 16)
            sp.dma_start(b2[:], e_b2.rearrange("(a f) -> a f", a=1).to_broadcast([128, D])).then_inc(loaded, 16)
            table = T["slots2"].rearrange("(p q) w -> p q w", p=128)

            def load(i, off):
                wait_half(sp, tr_ps_ok, i, off - DEEP)
                wait_half(sp, idx_ok, i, off - DEEP)
                sp.dma_start(slots[:, off % DEEP], table[:, bass.ds(number(i, off) * HALF, HALF), :])\
                    .then_inc(slots_in[off % DEEP], 16)
            for j in range(DEEP):
                load(None, j)
            with sp.Fori(0, HALVES // DEEP - 1) as i:
                for q in range(DEEP):
                    load(i, DEEP + q)

        @block.gpsimd
        def _(pool):
            with pool.Fori(0, HALVES // FETCH) as i:
                for q in range(FETCH):
                    pool.wait_ge(idx_ok, i * FETCH + (q + 1))
                    pool.sem_inc(issued, 1)
                    for k in range(HALF):
                        r = q * HALF + k
                        pool.indirect_dma_start(
                            out=gathered[:, q, k * D:(k + 1) * D], out_offset=None, in_=T["xcol"],
                            in_offset=bass.IndirectOffsetOnAxis(ap=idx[:, r:r + 1], axis=0)).then_inc(row_in[q], 16)

        @block.tensor
        def _(pe):
            def step(i, off):
                if exists(i, off + 1):
                    q = (off + 1) % DEEP
                    wait_half(pe, onehot_ok, i, off + 1)
                    wait_half(pe, tr_ok, i, off)
                    for k in range(HALF):
                        pe.transpose(onehot_ps[0:LANES, k * SLOT:(k + 1) * SLOT], onehot[:, q, k, :], K["ident"][:])
                    pe.transpose(slots_ps[0:HALF * REC2, 0:SLOT], slots[:, q].rearrange("p k w -> p (k w)"), K["ident"][:])\
                        .then_inc(tr_ps_ok, 1)
                if exists(i, off):
                    tiles = tiles_of(nc, pe, K["tile2"], number(i, off))
                    wait_half(pe, tr_ok, i, off)
                    wait_half(pe, pre1_ok, i, off - 1)
                    pe.matmul(hid_ps[:], slots_t[:, off % 2, :], w_attr[:], start=True, stop=False)
                    for k, tile in enumerate(tiles):
                        last = pe.matmul(hid_ps[:, k * D:(k + 1) * D],
                                         onehot_t[:, off % 2, k * SLOT:(k + 1) * SLOT],
                                         source_rows[:, bass.ds(tile, 1), :].rearrange("p a f -> p (a f)"),
                                         start=False, stop=(k == HALF - 1))
                    last.then_inc(hid_ps_ok, 1)
                if exists(i, off - 1):
                    wait_half(pe, hid_ok, i, off - 1)
                    wait_half(pe, hid_t_ok, i, off - 2)
                    for k in range(HALF):
                        last = pe.transpose(hid_t_ps[:, k * SLOT:(k + 1) * SLOT],
                                            hid[:, (off - 1) % 2, k * D:(k + 1) * D], K["ident"][:])
                    last.then_inc(hid_t_ps_ok, 1)
                if exists(i, off - 2):
                    wait_half(pe, hid_t_ok, i, off - 2)
                    wait_half(pe, pre2_ok, i, off - 3)
                    for k in range(HALF):
                        last = pe.matmul(msg_ps[:, k * D:(k + 1) * D],
                                         hid_t[:, off % 2, k * SLOT:(k + 1) * SLOT], w2[:], start=True, stop=True)
                    last.then_inc(msg_ps_ok, 1)
                if exists(i, off - 3):
                    wait_half(pe, msg_ok, i, off - 3)
                    if i is not None or off - 4 >= 0:
                        pe.wait_ge(added, number(i, off - 3) * HALF)
                    for k in range(HALF):
                        last = pe.matmul(sum_ps[:, k * LANES:(k + 1) * LANES],
                                         msg[:, (off - 3) % 2, k * D:(k + 1) * D], onehot[:, (off - 3) % DEEP, k, :],
                                         start=True, stop=True)
                    last.then_inc(sum_ok, 1)

            pe.wait_ge(loaded, 96)
            run(pe, step)

        @block.scalar
        def _(act):
            def step(i, off):
                if exists(i, off + 1):
                    b = (off + 1) % 2
                    wait_half(act, tr_ps_ok, i, off + 1)
                    wait_half(act, hid_ps_ok, i, off - 1)
                    act.copy(onehot_t[:, b, :], onehot_ps[0:LANES, :])
                    act.copy(slots_t[:, b, :], slots_ps[0:HALF * REC2, 0:SLOT]).then_inc(tr_ok, 1)
                if exists(i, off - 1):
                    wait_half(act, hid_t_ps_ok, i, off - 1)
                    wait_half(act, msg_ps_ok, i, off - 3)
                    act.copy(hid_t[:, (off - 1) % 2, :], hid_t_ps[:]).then_inc(hid_t_ok, 1)
                if exists(i, off):
                    wait_half(act, pre1_ok, i, off)
                    wait_half(act, hid_t_ps_ok, i, off - 2)
                    act.activation(hid[:, off % 2, :], pre1[:], ACT.Silu).then_inc(hid_ok, 1)
                if exists(i, off + 3):
                    q = (off + 3) % FETCH
                    wait_slots(act, i, off + 3)
                    wait_half(act, pre1_ok, i, off - 1)
                    act.copy(idx[:, q * HALF:(q + 1) * HALF], slots[:, (off + 3) % DEEP, :, 0]).then_inc(idx_ok, 1)
                if exists(i, off - 2):
                    wait_half(act, pre2_ok, i, off - 2)
                    wait_half(act, sum_ok, i, off - 4)
                    act.activation(msg[:, off % 2, :], pre2[:], ACT.Silu).then_inc(msg_ok, 1)

            run(act, step)

        @block.vector
        def _(dve):
            def step(i, off):
                tiles = tiles_of(nc, dve, K["tile2"], number(i, off - 3)) if exists(i, off - 3) else []
                if exists(i, off + 2):
                    q = (off + 2) % DEEP
                    wait_slots(dve, i, off + 2)
                    wait_half(dve, sum_ok, i, off + 2 - DEEP)
                    dve.tensor_tensor(onehot[:, q], K["iota_row"][:, None, 0:LANES].to_broadcast([128, HALF, LANES]),
                                      slots[:, q, :, 1:2].to_broadcast([128, HALF, LANES]), ALU.is_equal)\
                        .then_inc(onehot_ok, 1)
                if exists(i, off):
                    wait_half(dve, hid_ps_ok, i, off)
                    turn = off // FETCH if i is None else i * (DEEP // FETCH) + off // FETCH
                    dve.wait_ge(row_in[off % FETCH], turn * (16 * HALF) + 16 * HALF)
                    wait_half(dve, hid_ok, i, off - 1)
                    dve.tensor_tensor(pre1[:], hid_ps[:], gathered[:, off % FETCH, :], ALU.add).then_inc(pre1_ok, 1)
                if exists(i, off - 2):
                    wait_half(dve, msg_ps_ok, i, off - 2)
                    wait_half(dve, msg_ok, i, off - 3)
                    dve.tensor_tensor(pre2[:].rearrange("p (k f) -> p k f", k=HALF),
                                      msg_ps[:].rearrange("p (k f) -> p k f", k=HALF),
                                      b2[:, None, :].to_broadcast([128, HALF, D]), ALU.add).then_inc(pre2_ok, 1)
                if exists(i, off - 3):
                    wait_half(dve, sum_ok, i, off - 3)
                    for k, tile in enumerate(tiles):
                        if i is not None or (off - 3) * HALF + k > 0:
                            dve.wait_ge(added, number(i, off - 3) * HALF + k)
                        a = sums[:, bass.ds(tile * LANES, LANES)]
                        dve.tensor_tensor(a, a, sum_ps[:, k * LANES:(k + 1) * LANES], ALU.add).then_inc(added, 1)

            dve.memset(w_attr[:], 0.0).then_inc(zeroed, 1)
            dve.memset(sums[:, 0:NODES], 0.0).then_inc(zeroed, 1)
            dve.wait_ge(zeroed, 2)
            dve.wait_ge(loaded, 96)
            run(dve, step)


def layer3_nodes(nc, K, T, n_w1, n_b1, n_w2, n_b2, out):
    c, sb, sem, bank = phase(nc, "l4")
    with c:
        w1, w2 = sb("w1", [D, 2, D]), sb("w2", [D, D])
        b1, b2 = sb("b1", [D, 1]), sb("b2", [LANES, D])
        xs, xt, hid = sb("xs", [LANES, 2, D]), sb("xt", [D, PAIR]), sb("hid", [D, PAIR])
        y = sb("y", [LANES, 2, D])
        stats, mean_var = sb("stats", [LANES, 2, 6]), sb("mv", [LANES, TILES, 2])
        pair_var = sb("pair_mv", [LANES, 2, 2])
        y_ok, y_kept, var_kept = sem("y_ok"), sem("y_kept"), sem("var_kept")
        std, rstd = sb("std", [LANES, TILES]), sb("rstd", [LANES, TILES])
        PARTS = 5
        xt_ps, hid_ps, y_ps = bank("xt_ps"), bank("hid_ps"), bank("y_ps")
        loaded, staged, step_s = sem("loaded"), sem("staged"), sem("step")
        xt_ps_ok, xt_ok, hid_ps_ok, hid_ok, y_ps_ok, y_used = (
            sem("xt_ps_ok"), sem("xt_ok"), sem("hid_ps_ok"), sem("hid_ok"), sem("y_ps_ok"), sem("y_used"))
        var_ok, std_ok, part_ok, stored, passed = (sem("var_ok"), sem("std_ok"), sem("part_ok"), sem("stored"),
                                                   sem("passed"))
        block = c.enter_context(nc.Block())
        rows = rows_of(K["agg"], ROWS_A)
        sums = K["state"]

        @block.sync
        def _(sp):
            for k in range(2):
                sp.dma_start(w1[:, k, :], n_w1[k * D:(k + 1) * D, :]).then_inc(loaded, 16)
            sp.dma_start(w2[:], n_w2).then_inc(loaded, 16)
            sp.dma_start(b1[:], n_b1.rearrange("(p a) -> p a", a=1)).then_inc(loaded, 16)
            sp.dma_start(b2[:], n_b2.rearrange("(a f) -> a f", a=1).to_broadcast([LANES, D])).then_inc(loaded, 16)
            for q in range(PARTS):
                t = slice(q * TILES // PARTS, (q + 1) * TILES // PARTS)
                sp.wait_ge(part_ok, q + 1)
                sp.dma_start(out.rearrange("(p t) f -> p t f", p=LANES)[:, t, :], rows[:, t, :]).then_inc(stored, 16)
            sp.wait_ge(stored, 16 * PARTS)

        @block.gpsimd
        def _(pool):
            pool.sem_inc(y_kept, 1)
            pool.tensor_copy(xs[:], rows[:, 0:2, :]).then_inc(staged, 1)
            with pool.Fori(0, PAIRS - 1) as g:
                pool.wait_ge(hid_ps_ok, g + 1)
                pool.tensor_copy(xs[:], rows[:, bass.ds(g * 2 + 2, 2), :]).then_inc(staged, 1)
                pool.wait_ge(y_ok, g + 1)
                pool.tensor_copy(rows[:, bass.ds(g * 2, 2), :], y[:]).then_inc(y_kept, 1)
            pool.wait_ge(y_ok, PAIRS)
            pool.tensor_copy(rows[:, TILES - 2:TILES, :], y[:]).then_inc(y_kept, 1)

        @block.tensor
        def _(pe):
            def front(g):
                pe.wait_ge(staged, g + 1)
                for j in range(2):
                    last = pe.transpose(xt_ps[:, j * LANES:(j + 1) * LANES], xs[:, j, :],
                                        K["ident"][0:LANES, 0:LANES])
                last.then_inc(xt_ps_ok, 1)
                pe.wait_ge(xt_ok, g + 1)
                pe.wait_ge(hid_ok, g + 1)
                pe.matmul(hid_ps[:, 0:PAIR], w1[:, 0, :], xt[:], start=True, stop=False)
                pe.matmul(hid_ps[:, 0:PAIR], w1[:, 1, :], sums[:, bass.ds(g * PAIR, PAIR)],
                          start=False, stop=True).then_inc(hid_ps_ok, 1)

            def back(g):
                pe.wait_ge(hid_ok, g + 2)
                pe.wait_ge(y_used, g + 1)
                for j in range(2):
                    last = pe.matmul(y_ps[0:LANES, j * D:(j + 1) * D], hid[:, j * LANES:(j + 1) * LANES], w2[:],
                                     start=True, stop=True)
                last.then_inc(y_ps_ok, 1)

            pe.wait_ge(loaded, 80)
            pe.sem_inc(y_ps_ok, 1)
            with pe.Fori(0, PAIRS) as g:
                front(g)
                back(g)

        @block.scalar
        def _(act):
            act.wait_ge(loaded, 80)
            act.sem_inc(hid_ok, 1)
            with act.Fori(0, PAIRS) as g:
                act.wait_ge(xt_ps_ok, g + 1)
                act.copy(xt[:], xt_ps[:, 0:PAIR]).then_inc(xt_ok, 1)
                act.wait_ge(hid_ps_ok, g + 1)
                act.wait_ge(y_ps_ok, g + 1)
                act.activation(hid[:], hid_ps[:, 0:PAIR], ACT.Silu, bias=b1[:]).then_inc(hid_ok, 1)
            act.wait_ge(var_ok, 1)
            act.activation(std[:], mean_var[:, :, 1], ACT.Sqrt, bias=K["eps"][0:LANES, :]).then_inc(std_ok, 1)

        @block.vector
        def _(dve):
            step = Steps(dve, step_s)
            dve.wait_ge(loaded, 80)
            dve.sem_inc(y_used, 1)
            with dve.Fori(0, PAIRS) as g:
                step.done = g * 4
                dve.wait_ge(y_kept, g + 1)
                dve.wait_ge(y_ps_ok, g + 2)
                step(dve.tensor_tensor(y[:], y_ps[0:LANES, 0:2 * D].rearrange("p (j f) -> p j f", j=2),
                                       b2[:, None, :].to_broadcast([LANES, 2, D]), ALU.add))
                dve.sem_inc(y_used, 1)
                step(dve.scalar_tensor_tensor(y[:], rows[:, bass.ds(g * 2, 2), :], 2.0, y[:], ALU.mult, ALU.add))
                dve.sem_inc(y_ok, 1)
                for j in range(2):
                    ins = dve.bn_stats(stats[:, j, :], y[:, j, :])
                step(ins)
                dve.sem_inc(passed, 1)
                for j in range(2):
                    ins = dve.bn_aggr(pair_var[:, j, :], stats[:, j, :])
                step(ins)
                dve.tensor_copy(mean_var[:, bass.ds(g * 2, 2), :], pair_var[:]).then_inc(var_kept, 1)
            dve.wait_ge(var_kept, PAIRS)
            dve.wait_ge(y_kept, PAIRS + 1)
            step.done = PAIRS * 4
            dve.sem_inc(var_ok, 1)
            dve.wait_ge(std_ok, 1)
            step(dve.reciprocal(rstd[:], std[:]))
            for q in range(PARTS):
                for t in range(q * TILES // PARTS, (q + 1) * TILES // PARTS):
                    ins = dve.tensor_scalar(rows[:, t, :], rows[:, t, :], mean_var[:, t, 0:1], rstd[:, t:t + 1],
                                            ALU.subtract, ALU.mult)
                ins.then_inc(part_ok, 1)


def gnn(nc, x, src, dst, edge_attr_16, edge_type_8, edge_weight1, L0_gnn_W_l, L0_gnn_b_l, L0_gnn_W_r,
        L1_gnn_weight, L1_gnn_bias, L2_gnn_W, L2_gnn_w_ih, L2_gnn_w_hh, L2_gnn_b_ih, L2_gnn_b_hh,
        L2_gnn_l0_w, L2_gnn_l0_b, L2_gnn_l1_w, L2_gnn_l1_b, L3_gnn_eW1, L3_gnn_eb1, L3_gnn_eW2, L3_gnn_eb2,
        L3_gnn_nW1, L3_gnn_nb1, L3_gnn_nW2, L3_gnn_nb2, out):
    with ExitStack() as c:
        K = {}

        def buffers(*specs):
            for name, shape, *dt in specs:
                K[name] = c.enter_context(nc.sbuf_tensor(name, shape, *(dt or [F32])))

        T = tables(nc, c)
        buffers(("ident", [128, 128]), ("iota_row", [128, 128]), ("ones", [128, 128]), ("before", [128, 128]),
                ("chunk_no", [128, TILE_COLS]), ("eps", [128, 1]), ("rec", [128, PAD_CHUNKS, REC1]),
                ("tile1", [1, CHUNKS], I32), ("tile2", [1, CHUNKS], I32))
        constants(nc, K)

        def sems(name, n):
            return [c.enter_context(nc.semaphore(f"{name}{r}")) for r in range(n)]

        sort_edges(nc, K, T, sems("scattered1_", 2), src, dst, edge_attr_16, edge_type_8, edge_weight1)
        load_slots(nc, K, T)
        buffers(("agg", [128, 2 * TILES * D]), ("state", [128, 2 * TILES * D]))
        with ExitStack() as g:
            def scoped(*specs):
                for name, shape, *dt in specs:
                    K[name] = g.enter_context(nc.sbuf_tensor(name, shape, *(dt or [F32])))

            scoped(("onehot", [128, G_HALVES, HALF, LANES]), ("rows", [128, G_RING, STATE]),
                   ("idx", [128, G_RING], I32))
            with ExitStack() as q:
                K["cnt"] = q.enter_context(nc.sbuf_tensor("cnt", [LANES, TILES], F32))
                gather_sum(nc, K, GatherSems(semaphores(nc, q), sems("g0_row_in", G_HALVES), "g0"), 0, x, 0, D, count=True)
                layer0_nodes(nc, K, T, x, L0_gnn_W_l, L0_gnn_b_l, L0_gnn_W_r, L1_gnn_weight)
            with ExitStack() as q:
                gather_sum(nc, K, GatherSems(semaphores(nc, q), sems("g1_row_in", G_HALVES), "g1"), 0, T["rel"], 2, D, by_row=True, weighted=True)
                layer1_nodes(nc, K, T, L1_gnn_bias)
                first_state(nc, K, T)
            scoped(("w_ih_t", [128, 2, GATES]), ("w_hh_t", [128, 2, GATES]), ("w_comb", [128, 2, GATES]),
                   ("l0_t", [128, 3, 256]), ("l1_t", [128, 2, D]), ("b_rz", [128, 4]), ("b_n", [128, 2, 2]))
            gated_weights(nc, K, L2_gnn_w_ih, L2_gnn_w_hh, L2_gnn_b_ih, L2_gnn_b_hh, L2_gnn_l0_w, L2_gnn_l1_w)
            with ExitStack() as q:
                rounds = L2_gnn_W.shape[0]
                scattered = sems("scattered2_", 2)
                gather_s, weight_s, gate_s = GatherSems(semaphores(nc, q), sems("g2_row_in", G_HALVES), "g2"), WeightSems(semaphores(nc, q)), GateSems(semaphores(nc, q))
                with nc.Fori(0, rounds) as rnd:
                    combined_weight(nc, K, weight_s, rnd, L2_gnn_W)
                    gather_sum(nc, K, gather_s, rnd, T["state"], 0, STATE)
                    gated_update(nc, K, T, gate_s, scattered, rnd, rounds)
            layer2_nodes(nc, K, T, L2_gnn_l0_b, L2_gnn_l1_b, L3_gnn_eW1, L3_gnn_eb1)
        edge_mlp(nc, K, T, sems("edge_row_in", FETCH), L3_gnn_eW1, L3_gnn_eW2, L3_gnn_eb2)
        layer3_nodes(nc, K, T, L3_gnn_nW1, L3_gnn_nb1, L3_gnn_nW2, L3_gnn_nb2, out)


_INS = ["x", "src", "dst", "edge_attr_16", "edge_type_8", "edge_weight1", "L0_gnn_W_l", "L0_gnn_b_l", "L0_gnn_W_r",
        "L1_gnn_weight", "L1_gnn_bias", "L2_gnn_W", "L2_gnn_w_ih", "L2_gnn_w_hh", "L2_gnn_b_ih", "L2_gnn_b_hh",
        "L2_gnn_l0_w", "L2_gnn_l0_b", "L2_gnn_l1_w", "L2_gnn_l1_b", "L3_gnn_eW1", "L3_gnn_eb1", "L3_gnn_eW2",
        "L3_gnn_eb2", "L3_gnn_nW1", "L3_gnn_nb1", "L3_gnn_nW2", "L3_gnn_nb2"]
_OUTS = [((NODES, D), "float32")]


def kernel(**inputs):
    import numpy as _np
    import concourse.bacc as _bacc
    from concourse import mybir as _mybir
    from concourse.bass_utils import run_bass_kernel_spmd as _run

    nc = _bacc.Bacc("TRN2", target_bir_lowering=False, num_devices=1)
    arrays, args = {}, []
    for name in _INS:
        a = _np.ascontiguousarray(inputs[name])
        arrays[f"in_{name}_dram"] = a
        args.append(nc.dram_tensor(f"in_{name}_dram", a.shape, _mybir.dt.from_np(a.dtype), kind="ExternalInput").ap())
    for i, (shape, dtype) in enumerate(_OUTS):
        dt = _mybir.dt.from_np(_np.dtype(dtype))
        args.append(nc.dram_tensor(f"out_{i}_dram", shape, dt, kind="ExternalOutput").ap())
    gnn(nc, *args)
    r = _run(nc, [arrays], core_ids=[0])
    got = tuple(r.results[0][f"out_{i}_dram"] for i in range(len(_OUTS)))
    return got[0]
```

```python
from contextlib import ExitStack

import concourse.bass as bass
from concourse import mybir

F32 = mybir.dt.float32
I32 = mybir.dt.int32
ALU = mybir.AluOpType
ACT = mybir.ActivationFunctionType
AX = mybir.AxisListType

D = 128
LANES = 125
TILES = 50
NODES = LANES * TILES
PAIRS = TILES // 2
PAIR = 2 * LANES
EDGE_COLS = 800
RELS = 8
ATTR = 16
HALF = 4
RING = 8
G_HALVES = 4
G_RING = G_HALVES * HALF
SLOT = 128
CHUNKS = -(-((LANES * EDGE_COLS + TILES * (SLOT - 1)) // SLOT) // (8 * HALF)) * 8 * HALF
TURNS = CHUNKS // G_RING
DEEP = 8
FETCH = 4
PAD_CHUNKS = CHUNKS + HALF
TILE_COLS = 8
TILE_BITS = 6
REC1 = 4
REC2 = 2 + ATTR
STATE = 2 * D
GATES = 3 * STATE
LN_EPS = 1e-5
NORM_EPS = 1e-12


class Steps:

    def __init__(self, eng, sem, start=0):
        self.eng, self.sem, self.done = eng, sem, start

    def __call__(self, ins):
        ins.then_inc(self.sem, 1)
        self.done = self.done + 1
        self.eng.wait_ge(self.sem, self.done)


class Pipeline:

    def __init__(self, count, unroll, before, after):
        self.count, self.unroll, self.before, self.after = count, unroll, before, after
        self.start = -(-(after + 2) // unroll) * unroll
        self.turns = (count - before - self.start) // unroll

    def run(self, eng, step):
        for j in range(-self.before, self.start):
            step(None, j)
        with eng.Fori(0, self.turns) as i:
            for q in range(self.unroll):
                step(i, self.start + q)
        for j in range(self.start + self.turns * self.unroll, self.count + self.after):
            step(None, j)

    def exists(self, i, off):
        return i is not None or 0 <= off < self.count

    def number(self, i, off):
        return off if i is None else i * self.unroll + off

    def wait(self, eng, sem, i, off, per=1):
        if i is not None or off >= 0:
            eng.wait_ge(sem, self.number(i, off) * per + per)


def semaphores(nc, c):
    made = []

    def clear():
        nc.clear_and_free_semaphores(made)
        nc.all_engine_barrier()

    def sem(name):
        made.append(nc.alloc_semaphore(name))
        return made[-1]
    c.callback(clear)
    return sem


def tables(nc, c):
    def dram(name, shape, dt=F32):
        return nc.dram_tensor(f"{name}_table", shape, dt, kind="Internal").ap()
    return dict(
        slots1=dram("slots1", (SLOT * CHUNKS, REC1)),
        slots2=dram("slots2", (SLOT * CHUNKS, REC2)),
        edges2=dram("edges2", (LANES * EDGE_COLS, REC2)),
        rows2=dram("rows2", (LANES * EDGE_COLS,), I32),
        tiles_of_half1=dram("tiles_of_half1", (SLOT * TILE_COLS // HALF,), I32),
        tiles_of_half2=dram("tiles_of_half2", (SLOT * TILE_COLS // HALF,), I32),
        x2=dram("x2", (NODES, D)),
        rel=dram("rel", (NODES * RELS, D)),
        state=dram("state", (NODES, STATE)),
        xcol=dram("xcol", (NODES, D)),
    )


def constants(nc, K):
    with ExitStack() as c:
        sem = semaphores(nc, c)
        made, cast = sem("const_made"), sem("const_cast")
        iota_i = c.enter_context(nc.sbuf_tensor("iota_i", [128, 128], I32))
        chunk_i = c.enter_context(nc.sbuf_tensor("chunk_i", [128, TILE_COLS], I32))
        block = c.enter_context(nc.Block())

        @block.gpsimd
        def _(pool):
            pool.iota(iota_i[:], pattern=[[1, 128]], base=0, channel_multiplier=0).then_inc(made, 1)
            pool.iota(chunk_i[:], pattern=[[1, TILE_COLS]], base=0, channel_multiplier=TILE_COLS).then_inc(made, 1)
            pool.memset(K["ident"][:], 0.0).then_inc(made, 1)
            pool.memset(K["ones"][:], 1.0).then_inc(made, 1)
            pool.memset(K["eps"][:], LN_EPS).then_inc(made, 1)
            pool.wait_ge(made, 5)
            pool.affine_select(out=K["ident"][:], in_=K["ident"][:], compare_op=ALU.not_equal, fill=1.0,
                               base=0, pattern=[[-1, 128]], channel_multiplier=1).then_inc(made, 1)
            pool.affine_select(out=K["before"][:], in_=K["ones"][:], compare_op=ALU.is_gt, fill=0.0,
                               base=0, pattern=[[1, 128]], channel_multiplier=-1).then_inc(made, 1)

        @block.vector
        def _(dve):
            dve.wait_ge(made, 2)
            dve.tensor_copy(K["iota_row"][:], iota_i[:]).then_inc(cast, 1)
            dve.tensor_copy(K["chunk_no"][:], chunk_i[:]).then_inc(cast, 1)


def sort_edges(nc, K, T, scattered, src, dst, edge_attr, edge_type, edge_weight):
    with ExitStack() as c:
        def sb(name, shape, dt=F32):
            return c.enter_context(nc.sbuf_tensor(name, shape, dt))

        sem = semaphores(nc, c)
        L, C = LANES, EDGE_COLS
        PARTS = 5
        GROUP = 5
        key_i = [sb("dst_i", [L, C], I32), sb("src_i", [L, C], I32)]
        type_i = sb("type_i", [L, C], I32)
        key = [sb("dst_f", [L, C]), sb("src_f", [L, C])]
        bucket = sb("bucket", [L, C])
        lane = [sb("dst_lane", [L, C]), sb("src_lane", [L, C])]
        row = [sb("dst_row", [L, C]), sb("src_row", [L, C])]
        tmp = sb("tmp", [L, C])
        tmp_i = sb("tmp_i", [L, C], I32)
        is_tile, rank = sb("is_tile", [L, GROUP, C // PARTS]), sb("rank", [L, GROUP, C // PARTS])
        found, slot_i = sb("found", [L, C // PARTS]), sb("slot_i", [L, C // PARTS], I32)
        slot_f, unused = sb("slot_f", [L, C // PARTS]), sb("unused", [L, GROUP, C])
        ones_c = sb("ones_c", [L, C])
        norm = sb("norm", [L, C])
        rel_row = sb("rel_row", [L, C])
        rec2 = sb("rec2", [L, C, REC2])
        attr = sb("attr", [L, C // PARTS, ATTR])
        rows2_i = sb("rows2_i", [L, C], I32)
        hist = sb("hist", [L, TILES])
        total = sb("total", [128, TILES])
        total_i = sb("total_i", [128, TILES], I32)
        chunks = sb("chunks", [128, TILES])
        chunks_end = sb("chunks_end", [128, TILES])
        base = sb("base", [L, TILES])
        over = sb("over", [128, TILE_COLS, TILES])
        tile_f = sb("tile_f", [128, TILE_COLS // HALF, HALF])
        packed = sb("packed", [128, TILE_COLS // HALF])
        tile_i = [sb("tiles1_i", [128, TILE_COLS // HALF], I32), sb("tiles2_i", [128, TILE_COLS // HALF], I32)]
        fill2 = sb("fill2", [128, CHUNKS // 8, REC2])
        row_stage = sb("row_stage", [L, RING], I32)
        rec1_stage = sb("rec1_stage", [L, RING, REC1])
        count_ps = c.enter_context(nc.psum_tensor("count_ps", [128, 2, 256], F32))

        keys_in, rest_in = sem("keys_in"), sem("rest_in")
        filled, filled_rows = sem("filled"), sem("filled_rows")
        step_s = sem("dve_step")
        hist_done, counted = sem("hist_done"), sem("counted")
        tile_done, tile_out = sem("tile_done"), sem("tile_out")
        rows_done = sem("rows_done")
        staged, stage_step = sem("staged"), sem("stage_step")
        issued, passed = sem("issued"), sem("passed")
        attr_in, attr_used, rec2_ok, rec2_out = sem("attr_in"), sem("attr_used"), sem("rec2_ok"), sem("rec2_out")
        block = c.enter_context(nc.Block())
        SC_TURNS = EDGE_COLS // RING

        @block.sync
        def _(sp):
            for t, a in ((key_i[0], dst), (key_i[1], src)):
                sp.dma_start(t[:], a.rearrange("(p c) -> p c", p=L)).then_inc(keys_in, 16)
            sp.dma_start(type_i[:], edge_type.rearrange("(p c) -> p c", p=L)).then_inc(rest_in, 16)
            sp.dma_start(norm[:], edge_weight.rearrange("(p c) o -> p (c o)", p=L)).then_inc(rest_in, 16)
            for q in range(PARTS):
                if q > 0:
                    sp.wait_ge(attr_used, q)
                sp.dma_start(attr[:], edge_attr.rearrange("(p c) k -> p c k", p=L)
                             [:, q * C // PARTS:(q + 1) * C // PARTS, :]).then_inc(attr_in, 16)
            sp.wait_ge(filled, 2)
            sp.dma_start(T["slots1"].rearrange("(p q) w -> p (q w)", p=128),
                         K["rec"][:, 0:CHUNKS, :].rearrange("p q w -> p (q w)")).then_inc(filled_rows, 16)
            sp.wait_ge(filled, 4)
            slots2 = T["slots2"].rearrange("(p e q) w -> p e (q w)", p=128, e=8)
            for e in range(8):
                sp.dma_start(slots2[:, e, :], fill2[:].rearrange("p q w -> p (q w)")).then_inc(filled_rows, 16)
            for k in range(2):
                sp.wait_ge(tile_done, k + 1)
                sp.dma_start(T[f"tiles_of_half{k + 1}"].rearrange("(p j) -> p j", p=128), tile_i[k][:])\
                    .then_inc(tile_out, 16)
            sp.wait_ge(attr_used, PARTS)
            sp.wait_ge(rec2_ok, 3)
            sp.dma_start(T["edges2"].rearrange("(p c) w -> p c w", p=L), rec2[:]).then_inc(rec2_out, 16)
            sp.dma_start(T["rows2"].rearrange("(p c) -> p c", p=L), rows2_i[:]).then_inc(rec2_out, 16)
            sp.wait_ge(tile_out, 32)
            sp.wait_ge(rec2_out, 32)

        @block.gpsimd
        def _(pool):
            pool.memset(K["rec"][:], 0.0).then_inc(filled, 1)
            pool.wait_ge(filled, 1)
            pool.memset(K["rec"][:, :, 1:2], -1.0).then_inc(filled, 1)
            pool.memset(fill2[:], 0.0).then_inc(filled, 1)
            pool.wait_ge(filled, 3)
            pool.memset(fill2[:, :, 1:2], -1.0).then_inc(filled, 1)
            pool.wait_ge(filled_rows, 16 * 9)
            with pool.Fori(0, SC_TURNS) as i:
                for r in range(RING):
                    if r % HALF == 0:
                        pool.wait_ge(staged, i * 2 + (r // HALF + 1))
                        pool.sem_inc(issued, 1)
                    pool.indirect_dma_start(
                        out=T["slots1"], out_offset=bass.IndirectOffsetOnAxis(ap=row_stage[:, r:r + 1], axis=0),
                        in_=rec1_stage[:, r, :], in_offset=None).then_inc(scattered[r // HALF], 16)
            for h in range(2):
                pool.wait_ge(scattered[h], 16 * HALF * SC_TURNS)

        @block.scalar
        def _(act):
            def stage(i, h, first):
                s = slice(h * HALF, h * HALF + HALF)
                cols = bass.ds(i * RING + h * HALF, HALF)
                if not first:
                    act.wait_ge(scattered[h], i * (16 * HALF))
                act.copy(row_stage[:, s], row[0][:, cols]).then_inc(stage_step, 1)
                for w, t in enumerate((key[1], lane[0], rel_row)):
                    act.copy(rec1_stage[:, s, w], t[:, cols]).then_inc(stage_step, 1)
                act.copy(rec1_stage[:, s, 3], norm[:, cols]).then_inc(staged, 1)

            for q in range(PARTS):
                act.wait_ge(attr_in, 16 * (q + 1))
                act.copy(rec2[:, q * C // PARTS:(q + 1) * C // PARTS, 2:REC2], attr[:]).then_inc(attr_used, 1)
            act.wait_ge(rest_in, 32)
            act.wait_ge(rows_done, 1)
            for h in range(2):
                stage(0, h, True)
            for q in range(PARTS):
                act.wait_ge(rows_done, q + 1)
                act.sem_inc(passed, 1)
                with act.Fori(max(1, q * SC_TURNS // PARTS), (q + 1) * SC_TURNS // PARTS) as i:
                    for h in range(2):
                        stage(i, h, False)

        @block.tensor
        def _(pe):
            for k in range(2):
                pe.wait_ge(hist_done, k + 1)
                pe.matmul(count_ps[0:L, 0, 0:TILES], K["before"][0:L, 0:L], hist[:], start=True, stop=True)
                pe.matmul(count_ps[:, 1, 0:TILES], K["ones"][0:L, :], hist[:], start=True, stop=True)\
                    .then_inc(counted, 1)

        @block.vector
        def _(dve):
            step = Steps(dve, step_s)
            step(dve.memset(ones_c[:], 1.0))
            dve.wait_ge(keys_in, 32)
            step(dve.tensor_copy(key[0][:], key_i[0][:]))
            step(dve.tensor_copy(key[1][:], key_i[1][:]))
            dve.wait_ge(rest_in, 32)
            step(dve.tensor_copy(tmp[:], type_i[:]))
            step(dve.scalar_tensor_tensor(rel_row[:], key[1][:], float(RELS), tmp[:], ALU.mult, ALU.add))
            for k in range(2):
                step(dve.tensor_scalar(tmp_i[:], key[k][:], 1.0 / TILES, -0.49, ALU.mult, ALU.add))
                step(dve.tensor_copy(lane[k][:], tmp_i[:]))
                step(dve.scalar_tensor_tensor(bucket[:], lane[k][:], -float(TILES), key[k][:], ALU.mult, ALU.add))
                step(dve.tensor_single_scalar(tmp[:], bucket[:], 0.0, ALU.is_lt))
                step(dve.tensor_tensor(lane[k][:], lane[k][:], tmp[:], ALU.subtract))
                step(dve.scalar_tensor_tensor(bucket[:], tmp[:], float(TILES), bucket[:], ALU.mult, ALU.add))
                step(dve.tensor_single_scalar(tmp[:], bucket[:], float(TILES), ALU.is_ge))
                step(dve.tensor_tensor(lane[k][:], lane[k][:], tmp[:], ALU.add))
                step(dve.scalar_tensor_tensor(bucket[:], tmp[:], -float(TILES), bucket[:], ALU.mult, ALU.add))
                at = step.done
                with dve.Fori(0, TILES // GROUP) as t:
                    step.done = at + t
                    for n in range(GROUP):
                        col = bass.ds(t * GROUP + n, 1)
                        ins = dve.tensor_scalar(unused[:, n, :], bucket[:], K["iota_row"][0:L, col], 0.0,
                                                ALU.is_equal, ALU.add, accum_out=hist[:, col])
                    step(ins)
                step.done = at + TILES // GROUP
                dve.sem_inc(hist_done, 1)
                dve.wait_ge(counted, k + 1)
                step(dve.tensor_scalar(total_i[:], count_ps[:, 1, 0:TILES], float(SLOT - 1), None, ALU.add))
                step(dve.tensor_scalar(total_i[:], total_i[:], 7, None, ALU.arith_shift_right))
                step(dve.tensor_copy(chunks[:], total_i[:]))
                step(dve.tensor_tensor_scan(chunks_end[:], K["ones"][:, 0:TILES], chunks[:], 0.0, ALU.mult, ALU.add))
                step(dve.tensor_tensor(total[:], chunks_end[:], chunks[:], ALU.subtract))
                step(dve.tensor_scalar(total[:], total[:], float(SLOT), -1.0, ALU.mult, ALU.add))
                step(dve.tensor_tensor(base[:], total[0:L, :], count_ps[0:L, 0, 0:TILES], ALU.add))
                step(dve.tensor_tensor(
                    over[:], chunks_end[:, None, :].to_broadcast([128, TILE_COLS, TILES]),
                    K["chunk_no"][:, :, None].to_broadcast([128, TILE_COLS, TILES]), ALU.is_le))
                step(dve.tensor_reduce(tile_f[:].rearrange("p h k -> p (h k)"), over[:], AX.X, ALU.add))
                step(dve.tensor_single_scalar(tile_f[:], tile_f[:], float(TILES - 1), ALU.min))
                step(dve.tensor_copy(packed[:], tile_f[:, :, HALF - 1]))
                for n in reversed(range(HALF - 1)):
                    out = packed if n else tile_i[k]
                    step(dve.scalar_tensor_tensor(out[:], packed[:], float(1 << TILE_BITS), tile_f[:, :, n],
                                                  ALU.mult, ALU.add))
                dve.sem_inc(tile_done, 1)
                for q in range(PARTS):
                    cols = slice(q * C // PARTS, (q + 1) * C // PARTS)
                    part = [L, GROUP, C // PARTS]
                    step(dve.memset(row[k][:, cols], 0.0))
                    at = step.done
                    with dve.Fori(0, TILES // GROUP) as t:
                        step.done = at + t * 5
                        tiles = bass.ds(t * GROUP, GROUP)
                        step(dve.tensor_tensor(is_tile[:], bucket[:, None, cols].to_broadcast(part),
                                               K["iota_row"][0:L, tiles][:, :, None].to_broadcast(part),
                                               ALU.is_equal))
                        for n in range(GROUP):
                            ins = dve.tensor_tensor_scan(rank[:, n, :], ones_c[:, cols], is_tile[:, n, :],
                                                         base[:, bass.ds(t * GROUP + n, 1)], ALU.mult, ALU.add)
                        step(ins)
                        dve.sem_inc(passed, 1)
                        dve.tensor_copy(base[:, tiles], rank[:, :, C // PARTS - 1])
                        step(dve.tensor_tensor(is_tile[:], is_tile[:], rank[:], ALU.mult))
                        step(dve.tensor_reduce(found[:], is_tile[:].rearrange("p n c -> p c n"), AX.X, ALU.add))
                        step(dve.tensor_tensor(row[k][:, cols], row[k][:, cols], found[:], ALU.add))
                    step.done = at + TILES // GROUP * 5
                    step(dve.tensor_copy(tmp_i[:, cols], row[k][:, cols]))
                    step(dve.tensor_scalar(slot_i[:], tmp_i[:, cols], 7, None, ALU.arith_shift_right))
                    step(dve.tensor_scalar(tmp_i[:, cols], tmp_i[:, cols], SLOT - 1, None, ALU.bitwise_and))
                    step(dve.tensor_copy(slot_f[:], slot_i[:]))
                    step(dve.tensor_copy(tmp[:, cols], tmp_i[:, cols]))
                    step(dve.scalar_tensor_tensor(row[k][:, cols], tmp[:, cols], float(CHUNKS), slot_f[:],
                                                  ALU.mult, ALU.add))
                    dve.sem_inc(rows_done, 1)
            dve.tensor_copy(rec2[:, :, 0], key[0][:]).then_inc(rec2_ok, 1)
            dve.tensor_copy(rec2[:, :, 1], lane[1][:]).then_inc(rec2_ok, 1)
            dve.tensor_copy(rows2_i[:], row[1][:]).then_inc(rec2_ok, 1)


def load_slots(nc, K, T):
    with ExitStack() as c:
        loaded = semaphores(nc, c)("slots_loaded")
        block = c.enter_context(nc.Block())

        @block.sync
        def _(sp):
            sp.dma_start(K["rec"][:, 0:CHUNKS, :].rearrange("p q w -> p (q w)"),
                         T["slots1"].rearrange("(p q) w -> p (q w)", p=128)).then_inc(loaded, 16)
            for k in (1, 2):
                sp.dma_start(K[f"tile{k}"][:], T[f"tiles_of_half{k}"][0:CHUNKS // HALF]
                             .rearrange("(a q) -> a q", a=1)).then_inc(loaded, 16)
            sp.wait_ge(loaded, 48)


class CombinedWeight:

    def __init__(self, make, K, w):
        self.K, self.w = K, w
        self.loaded, self.tr_ok, self.wt_ok, self.prod_ok = (make(f"cw_{n}")
                                                             for n in ("loaded", "tr_ok", "wt_ok", "prod_ok"))

    def place(self, nc, c, rnd):
        self.rnd = rnd
        self.raw, self.wt = (c.enter_context(nc.sbuf_tensor(f"cw_{n}", [128, 2, STATE], F32)) for n in ("raw", "wt"))
        bank = [c.enter_context(nc.psum_tensor(f"cw_bank{i}", [128, 512], F32)) for i in range(4)]
        self.tr, self.prod = bank[0], bank

    def load(self, sp):
        sp.dma_start(self.raw[:], self.w[bass.ds(self.rnd, 1), :, :].rearrange("a (s p) m -> p (a s) m", p=128))\
            .then_inc(self.loaded, 16)

    def products(self, pe):
        pe.wait_ge(self.loaded, self.rnd * 16 + 16)
        for s in range(2):
            for m in range(2):
                last = pe.transpose(self.tr[:, (m * 2 + s) * 128:(m * 2 + s + 1) * 128],
                                    self.raw[:, s, m * 128:(m + 1) * 128], self.K["ident"][:])
        last.then_inc(self.tr_ok, 1)
        pe.wait_ge(self.wt_ok, self.rnd + 1)
        for s in range(2):
            for h in range(2):
                for m in range(2):
                    last = pe.matmul(self.prod[2 * s + h][:, 0:GATES // 2], self.wt[:, m, s * 128:(s + 1) * 128],
                                     self.K["w_ih_t"][:, m, h * GATES // 2:(h + 1) * GATES // 2],
                                     start=(m == 0), stop=(m == 1))
        last.then_inc(self.prod_ok, 1)

    def copies(self, act):
        act.wait_ge(self.tr_ok, self.rnd + 1)
        act.copy(self.wt[:].rearrange("p m s -> p (m s)"), self.tr[:]).then_inc(self.wt_ok, 1)
        act.wait_ge(self.prod_ok, self.rnd + 1)
        for s in range(2):
            for h in range(2):
                act.copy(self.K["w_comb"][:, s, h * GATES // 2:(h + 1) * GATES // 2],
                         self.prod[2 * s + h][:, 0:GATES // 2])


class GatherSems:
    def __init__(self, make, row_in, name):
        self.name = name

        def sem(n):
            return make(f"{name}_{n}")
        self.idx_staged = sem("idx_staged")
        self.weights_staged = sem("weights_staged")
        self.scaled = sem("scaled")
        self.issued = sem("issued")
        self.row_in = row_in
        self.onehot = sem("onehot")
        self.summed = sem("summed")
        self.psum_free = sem("psum_free")
        self.zeroed = sem("zeroed")
        self.started = sem("started")


def tile_word(eng, table, half):
    return eng.value_load(table[0:1, bass.ds(half, 1)], min_val=0, max_val=(1 << HALF * TILE_BITS) - 1)


def place(eng, word, k, stride):
    tile = ((word >> k * TILE_BITS) & ((1 << TILE_BITS) - 1)).with_bounds(min_val=0, max_val=TILES - 1)
    held = bass.RuntimeValue.of_register_unchecked(eng.to_reg(tile * stride))
    return held.with_bounds(min_val=0, max_val=(TILES - 1) * stride)


def gather_sum(nc, K, S, rnd, table, word, width, by_row=False, weighted=False, count=False,
               combined=None):
    NPS = HALF
    onehot, rows, idx = K["onehot"], K["rows"], K["idx"]
    agg, rec = K["agg"], K["rec"]
    halves = width // D
    agg_t = agg[:, 0:halves * NODES].rearrange("p (s n) -> p s n", s=halves)
    with ExitStack() as c:
        if weighted:
            weights = c.enter_context(nc.sbuf_tensor("edge_weights", [128, G_RING], F32))
        if combined:
            combined.place(nc, c, rnd)
        prod = [c.enter_context(nc.psum_tensor(f"{S.name}_prod{b}", [128, 512], F32)) for b in range(NPS)]
        block = c.enter_context(nc.Block())
        s_base = rnd * (CHUNKS + G_RING)
        f_base = rnd * (CHUNKS + NPS)

        if combined:
            @block.sync
            def _(sp):
                combined.load(sp)

        @block.scalar
        def _(act):
            def stage(i, h):
                s = slice(h * HALF, h * HALF + HALF)
                half = bass.ds(i * G_RING + h * HALF, HALF)
                act.wait_ge(S.summed, s_base + i * G_RING + (h * HALF + HALF))
                if weighted:
                    act.copy(weights[:, s], rec[:, half, 3]).then_inc(S.weights_staged, 1)
                act.copy(idx[:, s], rec[:, half, word]).then_inc(S.idx_staged, 1)

            def scale(i, h):
                act.wait_ge(S.row_in[h], i * (16 * HALF) + 16 * HALF)
                act.wait_ge(S.weights_staged, i * G_HALVES + (h + 1))
                for r in range(h * HALF, h * HALF + HALF):
                    last = act.activation(rows[:, r, 0:D], rows[:, r, 0:D], ACT.Copy, scale=weights[:, r:r + 1])
                last.then_inc(S.scaled, 1)

            act.wait_ge(S.summed, s_base + G_RING)
            act.sem_inc(S.started, 1)
            if weighted:
                for h in range(G_HALVES):
                    stage(0, h)
                    if h >= 2:
                        scale(0, h - 2)
                with act.Fori(1, TURNS) as i:
                    for h in range(G_HALVES):
                        stage(i, h)
                        if h >= 2:
                            scale(i, h - 2)
                        else:
                            scale(i - 1, h + 2)
                scale(TURNS - 1, 2)
                scale(TURNS - 1, 3)
            else:
                for h in range(G_HALVES):
                    stage(0, h)
                if combined:
                    combined.copies(act)
                with act.Fori(1, TURNS) as i:
                    for h in range(G_HALVES):
                        stage(i, h)

        @block.gpsimd
        def _(pool):
            with pool.Fori(0, TURNS) as i:
                for r in range(G_RING):
                    if r % HALF == 0:
                        pool.wait_ge(S.idx_staged, (rnd * TURNS + i) * G_HALVES + (r // HALF + 1))
                        pool.sem_inc(S.issued, 1)
                    pool.indirect_dma_start(
                        out=rows[:, r, 0:width], out_offset=None, in_=table,
                        in_offset=bass.IndirectOffsetOnAxis(ap=idx[:, r:r + 1], axis=0))\
                        .then_inc(S.row_in[r // HALF], 16)

        @block.tensor
        def _(pe):
            pe.sem_inc(S.summed, G_RING)
            if combined:
                combined.products(pe)
            with pe.Fori(0, TURNS) as i:
                for r in range(G_RING):
                    if r % HALF == 0:
                        pe.wait_ge(S.onehot, rnd * (TURNS * G_HALVES + 1) + i * G_HALVES + (r // HALF + 1))
                        if weighted:
                            pe.wait_ge(S.scaled, i * G_HALVES + (r // HALF + 1))
                        else:
                            pe.wait_ge(S.row_in[r // HALF], (rnd * TURNS + i) * (16 * HALF) + 16 * HALF)
                    pe.wait_ge(S.psum_free, f_base + i * G_RING + (r + 1))
                    p = prod[r % NPS]
                    oh = onehot[:, r // HALF, r % HALF, :]
                    if count:
                        pe.matmul(p[0:LANES, 2 * LANES:2 * LANES + 1], oh, K["ones"][:, 0:1], start=True, stop=True)
                    if by_row:
                        pe.matmul(p[0:LANES, 0:D], oh, rows[:, r, 0:D], start=True, stop=True)\
                            .then_inc(S.summed, 1)
                    else:
                        for s in range(halves):
                            last = pe.matmul(p[:, s * LANES:(s + 1) * LANES], rows[:, r, s * D:(s + 1) * D], oh,
                                             start=True, stop=True)
                        last.then_inc(S.summed, 1)

        @block.vector
        def _(dve):
            def build(chunk, h):
                dve.tensor_tensor(onehot[:, h], K["iota_row"][:, None, 0:LANES].to_broadcast([128, HALF, LANES]),
                                  rec[:, bass.ds(chunk, HALF), 1:2].to_broadcast([128, HALF, LANES]),
                                  ALU.is_equal).then_inc(S.onehot, 1)

            dve.memset(agg[:], 0.0).then_inc(S.zeroed, 1)
            if count:
                dve.memset(K["cnt"][:], 0.0).then_inc(S.zeroed, 1)
            dve.sem_inc(S.psum_free, NPS)
            build(0, 0)
            dve.wait_ge(S.zeroed, rnd + (2 if count else 1))
            dve.sem_inc(S.started, 1)
            stride = D if by_row else LANES
            with dve.Fori(0, TURNS) as i:
                for h in range(G_HALVES):
                    word = tile_word(dve, K["tile1"], i * G_HALVES + h)
                    dve.wait_ge(S.summed, s_base + i * G_RING + ((h + 1) * HALF))
                    build(i * G_RING + (h * HALF + HALF), (h + 1) % G_HALVES)
                    at = place(dve, word, 0, stride)
                    for r in range(h * HALF, h * HALF + HALF):
                        k = r % HALF
                        if count:
                            tile = place(dve, word, k, 1)
                        dve.wait_ge(S.summed, s_base + i * G_RING + (r + G_RING + 1))
                        dve.wait_ge(S.psum_free, f_base + i * G_RING + (r + NPS))
                        p = prod[r % NPS]
                        if count:
                            counts = K["cnt"][:, bass.ds(tile, 1)]
                            dve.tensor_tensor(counts, counts,
                                              p[0:LANES, 2 * LANES:2 * LANES + 1], ALU.add)
                        if by_row:
                            a = agg[0:LANES, bass.ds(at, D)]
                            dve.tensor_tensor(a, a, p[0:LANES, 0:D], ALU.add).then_inc(S.psum_free, 1)
                        else:
                            a = agg_t[:, :, bass.ds(at, LANES)]
                            dve.tensor_tensor(a, a, p[:, 0:halves * LANES]
                                              .rearrange("p (s n) -> p s n", s=halves), ALU.add)\
                                .then_inc(S.psum_free, 1)
                        if k < HALF - 1:
                            at = place(dve, word, k + 1, stride)


def rows_of(area, at):
    return area[0:LANES, at:at + TILES * D].rearrange("p (t f) -> p t f", t=TILES)


def transposed(area, halves):
    return area[:, 0:halves * NODES].rearrange("p (s n) -> p s n", s=halves)


ROWS_A, ROWS_B = 0, TILES * D


class Norm:

    def __init__(self, sb, sem):
        self.stats, self.mean_var = sb("stats", [LANES, 2, 6]), sb("mean_var", [LANES, 2, 2])
        self.rstd = sb("rstd", [LANES, 2])
        self.std = sb("std", [LANES, 2])
        self.var_ok, self.std_ok, self.dve_passed = sem("var_ok"), sem("std_ok"), sem("dve_passed")


def deviation(act, K, g, norm):
    act.wait_ge(norm.var_ok, g + 1)
    act.activation(norm.std[:], norm.mean_var[:, :, 1], ACT.Sqrt, bias=K["eps"][0:LANES, :]).then_inc(norm.std_ok, 1)


def phase(nc, name):
    c = ExitStack()

    def sb(n, shape, dt=F32):
        return c.enter_context(nc.sbuf_tensor(f"{name}_{n}", shape, dt))

    make = semaphores(nc, c)

    def sem(n):
        return make(f"{name}_{n}")

    def bank(n):
        return c.enter_context(nc.psum_tensor(f"{name}_{n}", [128, 512], F32))
    return c, sb, sem, bank


def layer0_nodes(nc, K, T, x, w_l, b_l, w_r, rel_weight):
    c, sb, sem, bank = phase(nc, "l0")
    with c:
        wl, wr, bl = sb("wl", [D, D]), sb("wr", [D, D]), sb("bl", [1, D])
        relw = sb("relw", [D, RELS * D])
        xs, aggs = sb("xs", [LANES, 2, D]), sb("aggs", [D, PAIR])
        xt, x1t = sb("xt", [D, 2, PAIR]), sb("x1t", [D, 2, PAIR])
        inv = sb("inv", [LANES, TILES])
        o, sq, y = (sb(n, [LANES, 2, D]) for n in ("o", "sq", "y"))
        x1 = sb("x1", [LANES, 2, 2, D])
        ss, l2, inv_norm = sb("ss", [LANES, 2]), sb("norm", [LANES, 2]), sb("inv_norm", [LANES, 2])
        norm = Norm(sb, sem)
        relrow = sb("relrow", [LANES, 2, 2, RELS * D])
        xt_ps, mean_ps, self_ps, x1t_ps = bank("xt_ps"), bank("mean_ps"), bank("self_ps"), bank("x1t_ps")
        rel_ps = [bank(f"rel_ps{i}") for i in range(4)]
        loaded, first_step = sem("loaded"), sem("first_step")
        product_step, sum_step, norm_step = sem("product_step"), sem("sum_step"), sem("norm_step")
        xs_ok, aggs_ok, xt_ps_ok, xt_ok, sums_ok = (
            sem(n) for n in ("xs_ok", "aggs_ok", "xt_ps_ok", "xt_ok", "sums_ok"))
        ss_ok, norm_ok, sums_used = sem("ss_ok"), sem("norm_ok"), sem("sums_used")
        x1_ok, x1_kept, x1t_ps_ok, x1t_ok = sem("x1_ok"), sem("x1_kept"), sem("x1t_ps_ok"), sem("x1t_ok")
        rel_ps_ok, rel_ok, stored = sem("rel_ps_ok"), sem("rel_ok"), [sem("stored0"), sem("stored1")]
        line = Pipeline(PAIRS, 2, 2, 4)
        number, exists, wait, run = line.number, line.exists, line.wait, line.run
        block = c.enter_context(nc.Block())
        xrows, x1rows = rows_of(K["state"], ROWS_A), rows_of(K["state"], ROWS_B)
        agg = K["agg"]

        @block.sync
        def _(sp):
            sp.dma_start(K["state"][0:LANES, 0:TILES * D], x.rearrange("(p t) f -> p (t f)", p=LANES))\
                .then_inc(loaded, 16)
            sp.dma_start(wl[:], w_l).then_inc(loaded, 16)
            sp.dma_start(wr[:], w_r).then_inc(loaded, 16)
            sp.dma_start(bl[:], b_l.rearrange("(a f) -> a f", a=1)).then_inc(loaded, 16)
            for r in range(RELS):
                sp.dma_start(relw[:, r * D:(r + 1) * D], rel_weight[r]).then_inc(loaded, 16)
            table = T["rel"].rearrange("(p t r) f -> p t (r f)", p=LANES, r=RELS)

            def step(i, off):
                if exists(i, off):
                    wait(sp, rel_ok, i, off, 4)
                    sp.dma_start(table[:, bass.ds(number(i, off) * 2, 2), :], relrow[:, off % 2])\
                        .then_inc(stored[off % 2], 16)
            run(sp, step)
            for q in range(2):
                sp.wait_ge(stored[q], 16 * ((PAIRS + 1 - q) // 2))

        @block.gpsimd
        def _(pool):
            def step(i, off):
                if exists(i, off + 2):
                    wait(pool, xt_ps_ok, i, off + 1)
                    pool.tensor_copy(xs[:], xrows[:, bass.ds(number(i, off + 2) * 2, 2), :]).then_inc(xs_ok, 1)
                if exists(i, off + 1):
                    wait(pool, sums_ok, i, off)
                    pool.tensor_copy(aggs[:], agg[:, bass.ds(number(i, off + 1) * PAIR, PAIR)]).then_inc(aggs_ok, 1)
                if exists(i, off - 2):
                    wait(pool, x1_ok, i, off - 2)
                    pool.tensor_copy(x1rows[:, bass.ds(number(i, off - 2) * 2, 2), :], x1[:, off % 2])\
                        .then_inc(x1_kept, 1)

            pool.wait_ge(loaded, 16 * 12)
            run(pool, step)

        @block.tensor
        def _(pe):
            def step(i, off):
                if exists(i, off + 1):
                    wait(pe, xs_ok, i, off + 1)
                    wait(pe, xt_ok, i, off)
                    for j in range(2):
                        last = pe.transpose(xt_ps[:, j * LANES:(j + 1) * LANES], xs[:, j, :],
                                            K["ident"][0:LANES, 0:LANES])
                    last.then_inc(xt_ps_ok, 1)
                if exists(i, off):
                    wait(pe, aggs_ok, i, off)
                    wait(pe, sums_used, i, off - 1)
                    for j in range(2):
                        pe.matmul(mean_ps[0:LANES, j * D:(j + 1) * D], aggs[:, j * LANES:(j + 1) * LANES], wl[:],
                                  start=True, stop=True)
                    wait(pe, xt_ok, i, off)
                    for j in range(2):
                        out = self_ps[0:LANES, j * D:(j + 1) * D]
                        pe.matmul(out, xt[:, off % 2, j * LANES:(j + 1) * LANES], wr[:], start=True, stop=False)
                        last = pe.matmul(out, K["ones"][0:1, 0:LANES], bl[:], start=False, stop=True)
                    last.then_inc(sums_ok, 1)
                if exists(i, off - 3):
                    wait(pe, x1_ok, i, off - 3)
                    wait(pe, x1t_ok, i, off - 4)
                    for j in range(2):
                        last = pe.transpose(x1t_ps[:, j * LANES:(j + 1) * LANES], x1[:, (off - 3) % 2, j, :],
                                            K["ident"][0:LANES, 0:LANES])
                    last.then_inc(x1t_ps_ok, 1)
                if exists(i, off - 4):
                    wait(pe, x1t_ok, i, off - 4)
                    for q in range(4):
                        if i is not None or off - 5 >= 0:
                            pe.wait_ge(rel_ok, number(i, off - 5) * 4 + (q + 1))
                        v = x1t[:, off % 2, (q // 2) * LANES:(q // 2 + 1) * LANES]
                        pe.matmul(rel_ps[q][0:LANES, :], v, relw[:, (q % 2) * 512:(q % 2 + 1) * 512],
                                  start=True, stop=True).then_inc(rel_ps_ok, 1)

            pe.wait_ge(loaded, 16 * 12)
            run(pe, step)

        @block.scalar
        def _(act):
            def step(i, off):
                if exists(i, off + 1):
                    wait(act, xt_ps_ok, i, off + 1)
                    wait(act, sums_ok, i, off - 1)
                    act.copy(xt[:, (off + 1) % 2, :], xt_ps[:, 0:PAIR]).then_inc(xt_ok, 1)
                if exists(i, off - 3):
                    wait(act, x1t_ps_ok, i, off - 3)
                    wait(act, rel_ps_ok, i, off - 5, 4)
                    act.copy(x1t[:, (off - 3) % 2, :], x1t_ps[:, 0:PAIR]).then_inc(x1t_ok, 1)
                if exists(i, off - 4):
                    if i is not None or off - 6 >= 0:
                        turn = (off - 6) // 2 if i is None else i + (off - 6) // 2
                        act.wait_ge(stored[off % 2], turn * 16 + 16)
                    for q in range(4):
                        act.wait_ge(rel_ps_ok, number(i, off - 4) * 4 + (q + 1))
                        act.copy(relrow[:, off % 2, q // 2, (q % 2) * 512:(q % 2 + 1) * 512],
                                 rel_ps[q][0:LANES, :]).then_inc(rel_ok, 1)
                if exists(i, off - 1):
                    deviation(act, K, number(i, off - 1), norm)
                if exists(i, off):
                    wait(act, ss_ok, i, off)
                    act.activation(l2[:], ss[:], ACT.Sqrt).then_inc(norm_ok, 1)

            run(act, step)

        @block.vector
        def _(dve):
            product, total, scaled = Steps(dve, product_step), Steps(dve, sum_step), Steps(dve, norm_step)

            def step(i, off):
                if exists(i, off - 2):
                    scaled.done = number(i, off - 2)
                    wait(dve, norm.std_ok, i, off - 2)
                    scaled(dve.reciprocal(norm.rstd[:], norm.std[:]))
                    wait(dve, x1_kept, i, off - 4)
                    wait(dve, x1t_ps_ok, i, off - 4)
                    for j in range(2):
                        last = dve.tensor_scalar(x1[:, off % 2, j, :], y[:, j, :], norm.mean_var[:, j, 0:1],
                                                 norm.rstd[:, j:j + 1], ALU.subtract, ALU.mult)
                    last.then_inc(x1_ok, 1)
                if exists(i, off - 1):
                    total.done = number(i, off - 1) * 3
                    wait(dve, norm_ok, i, off - 1)
                    total(dve.reciprocal(inv_norm[:], l2[:]))
                    wait(dve, x1_ok, i, off - 2)
                    for j in range(2):
                        last = dve.scalar_tensor_tensor(
                            y[:, j, :], o[:, j, :], inv_norm[:, j:j + 1],
                            xrows[:, bass.ds(number(i, off - 1) * 2 + j, 1), :].rearrange("p a f -> p (a f)"),
                            ALU.mult, ALU.add)
                    total(last)
                    for j in range(2):
                        last = dve.bn_stats(norm.stats[:, j, :], y[:, j, :])
                    total(last)
                    dve.sem_inc(norm.dve_passed, 1)
                    for j in range(2):
                        last = dve.bn_aggr(norm.mean_var[:, j, :], norm.stats[:, j, :])
                    last.then_inc(norm.var_ok, 1)
                if exists(i, off):
                    product.done = number(i, off) * 4
                    wait(dve, sums_ok, i, off)
                    for j in range(2):
                        last = dve.tensor_scalar(o[:, j, :], mean_ps[0:LANES, j * D:(j + 1) * D],
                                                 inv[:, bass.ds(number(i, off) * 2 + j, 1)], None, ALU.mult)
                    product(last)
                    product(dve.tensor_tensor(o[:], o[:], self_ps[0:LANES, 0:2 * D]
                                              .rearrange("p (j f) -> p j f", j=2), ALU.add))
                    dve.sem_inc(sums_used, 1)
                    product(dve.tensor_tensor(sq[:], o[:], o[:], ALU.mult))
                    wait(dve, norm_ok, i, off - 1)
                    product(dve.tensor_reduce(ss[:], sq[:], AX.X, ALU.add))
                    dve.tensor_single_scalar(ss[:], ss[:], NORM_EPS * NORM_EPS, ALU.max).then_inc(ss_ok, 1)

            first = Steps(dve, first_step)
            first(dve.tensor_single_scalar(inv[:], K["cnt"][:], 1.0, ALU.max))
            first(dve.reciprocal(inv[:], inv[:]))
            run(dve, step)


def layer1_nodes(nc, K, T, bias):
    c, sb, sem, bank = phase(nc, "l1")
    with c:
        ZERO_TILES = TILES // 5
        bias_all = sb("bias_all", [LANES, D])
        zeros = sb("zeros", [LANES, ZERO_TILES, D])
        y, x2 = sb("y", [LANES, 2, D]), sb("x2", [LANES, 2, 2, D])
        norm = Norm(sb, sem)
        tr = bank("tr")
        loaded, cleared, zeroed = sem("loaded"), sem("cleared"), sem("zeroed")
        sum_step, norm_step = sem("sum_step"), sem("norm_step")
        x2_ok, tr_ok, kept, stored = sem("x2_ok"), sem("tr_ok"), sem("kept"), [sem("stored0"), sem("stored1")]
        line = Pipeline(PAIRS, 2, 0, 2)
        number, exists, wait, run = line.number, line.exists, line.wait, line.run
        block = c.enter_context(nc.Block())
        sums = rows_of(K["agg"], ROWS_A)
        rows = rows_of(K["state"], ROWS_B)

        @block.sync
        def _(sp):
            sp.dma_start(bias_all[:], bias.rearrange("(a f) -> a f", a=1).to_broadcast([LANES, D]))\
                .then_inc(loaded, 16)
            state = T["state"].rearrange("(p t) w -> p t w", p=LANES)
            x2_table = T["x2"].rearrange("(p t) f -> p t f", p=LANES)
            sp.wait_ge(cleared, 1)
            for q in range(TILES // ZERO_TILES):
                sp.dma_start(state[:, q * ZERO_TILES:(q + 1) * ZERO_TILES, D:STATE], zeros[:]).then_inc(zeroed, 16)

            def step(i, off):
                if exists(i, off):
                    wait(sp, x2_ok, i, off)
                    pair = bass.ds(number(i, off) * 2, 2)
                    sp.dma_start(x2_table[:, pair, :], x2[:, off % 2]).then_inc(stored[off % 2], 16)
                    sp.dma_start(state[:, pair, 0:D], x2[:, off % 2]).then_inc(stored[off % 2], 16)
            run(sp, step)
            sp.wait_ge(zeroed, 16 * (TILES // ZERO_TILES))
            for q in range(2):
                sp.wait_ge(stored[q], 32 * ((PAIRS + 1 - q) // 2))

        @block.tensor
        def _(pe):
            def step(i, off):
                if exists(i, off):
                    wait(pe, x2_ok, i, off)
                    wait(pe, kept, i, off - 1)
                    for j in range(2):
                        last = pe.transpose(tr[:, j * LANES:(j + 1) * LANES], x2[:, off % 2, j, :],
                                            K["ident"][0:LANES, 0:LANES])
                    last.then_inc(tr_ok, 1)
            run(pe, step)

        @block.scalar
        def _(act):
            def step(i, off):
                if exists(i, off - 2):
                    wait(act, tr_ok, i, off - 2)
                    act.copy(K["state"][:, bass.ds(number(i, off - 2) * PAIR, PAIR)], tr[:, 0:PAIR]).then_inc(kept, 1)
                if exists(i, off):
                    deviation(act, K, number(i, off), norm)
            run(act, step)

        @block.vector
        def _(dve):
            total, scaled = Steps(dve, sum_step), Steps(dve, norm_step)

            def step(i, off):
                if exists(i, off - 1):
                    scaled.done = number(i, off - 1)
                    wait(dve, norm.std_ok, i, off - 1)
                    scaled(dve.reciprocal(norm.rstd[:], norm.std[:]))
                    wait(dve, tr_ok, i, off - 3)
                    if i is not None or off - 3 >= 0:
                        turn = (off - 3) // 2 if i is None else i + (off - 3) // 2
                        dve.wait_ge(stored[(off - 1) % 2], turn * 32 + 32)
                    for j in range(2):
                        last = dve.tensor_scalar(x2[:, (off - 1) % 2, j, :], y[:, j, :], norm.mean_var[:, j, 0:1],
                                                 norm.rstd[:, j:j + 1], ALU.subtract, ALU.mult)
                    last.then_inc(x2_ok, 1)
                if exists(i, off):
                    total.done = number(i, off) * 3
                    wait(dve, x2_ok, i, off - 1)
                    pair = bass.ds(number(i, off) * 2, 2)
                    total(dve.tensor_tensor(y[:], sums[:, pair, :],
                                            bias_all[:, None, :].to_broadcast([LANES, 2, D]), ALU.add))
                    dve.sem_inc(norm.dve_passed, 1)
                    total(dve.scalar_tensor_tensor(y[:], y[:], 0.0, rows[:, pair, :], ALU.max, ALU.add))
                    for j in range(2):
                        last = dve.bn_stats(norm.stats[:, j, :], y[:, j, :])
                    total(last)
                    dve.sem_inc(norm.dve_passed, 1)
                    for j in range(2):
                        last = dve.bn_aggr(norm.mean_var[:, j, :], norm.stats[:, j, :])
                    last.then_inc(norm.var_ok, 1)

            dve.memset(zeros[:], 0.0).then_inc(cleared, 1)
            dve.wait_ge(loaded, 16)
            run(dve, step)
            dve.memset(K["state"][:, NODES:2 * NODES], 0.0)


def gated_weights(nc, K, w_ih, w_hh, b_ih, b_hh, l0_w, l1_w):
    c, sb, sem, bank = phase(nc, "gw")
    with c:
        jobs = []
        plan = (("w_ih", w_ih, K["w_ih_t"]), ("w_hh", w_hh, K["w_hh_t"]), ("l0_w", l0_w, K["l0_t"]),
                ("l1_w", l1_w, K["l1_t"]))
        raw = []
        for name, w, t in plan:
            raw.append(sb(name, [128, w.shape[0] // 128, w.shape[1]]))
            for q in range(w.shape[0] // 128):
                for k in range(w.shape[1] // 128):
                    jobs.append((raw[-1][:, q, k * 128:(k + 1) * 128], t[:, k, q * 128:(q + 1) * 128]))
        b_raw = [sb("b_ih", [128, 6]), sb("b_hh", [128, 6])]
        tr = [bank("tr0"), bank("tr1")]
        loaded, tr_ok, tr_used = sem("loaded"), sem("tr_ok"), sem("tr_used")
        block = c.enter_context(nc.Block())

        @block.sync
        def _(sp):
            for (name, w, t), r in zip(plan, raw):
                sp.dma_start(r[:], w.rearrange("(q p) k -> p q k", p=128)).then_inc(loaded, 16)
            with nc.allow_non_contiguous_dma(reason="a few biases by partition"):
                for b, r in zip((b_ih, b_hh), b_raw):
                    sp.dma_start(r[:], b.rearrange("(q p) -> p q", p=128)).then_inc(loaded, 16)

        @block.tensor
        def _(pe):
            pe.wait_ge(loaded, 16 * 6)
            for n, (src, _) in enumerate(jobs):
                if n >= 2:
                    pe.wait_ge(tr_used, n - 1)
                pe.transpose(tr[n % 2][:, 0:128], src, K["ident"][:]).then_inc(tr_ok, 1)

        @block.scalar
        def _(act):
            for n, (_, dst) in enumerate(jobs):
                act.wait_ge(tr_ok, n + 1)
                act.copy(dst, tr[n % 2][:, 0:128]).then_inc(tr_used, 1)

        @block.vector
        def _(dve):
            dve.wait_ge(loaded, 16 * 6)
            dve.tensor_tensor(K["b_rz"][:], b_raw[0][:, 0:4], b_raw[1][:, 0:4], ALU.add)
            dve.tensor_copy(K["b_n"][:, 0, :], b_raw[0][:, 4:6])
            dve.tensor_copy(K["b_n"][:, 1, :], b_raw[1][:, 4:6])


class GateSems:
    def __init__(self, make):
        def sem(n):
            return make(f"gru_{n}")
        self.r_ps, self.z_ps, self.n_ps, self.h_ps = sem("r_ps"), sem("z_ps"), sem("n_ps"), sem("h_ps")
        self.r_ok, self.z_ok = sem("r_ok"), sem("z_ok")
        self.t_ok, self.u_ok, self.n_ok = sem("t_ok"), sem("u_ok"), sem("n_ok")
        self.step, self.new_ok = sem("step"), sem("new_ok")
        self.tr_ok, self.row_ok = sem("tr_ok"), sem("row_ok")
        self.row_free, self.stored = sem("row_free"), sem("stored")
        self.edges_in, self.staged, self.issued = sem("edges_in"), sem("staged"), sem("issued")


def gated_update(nc, K, T, S, scattered, rnd, rounds):
    cols = EDGE_COLS // rounds
    turns = cols // RING
    assert cols * rounds == EDGE_COLS and turns * RING == cols
    c, sb, sem, bank = phase(nc, "gru")
    with c:
        gr, gz, u, ng, dd, new = (sb(n, [128, 2, PAIR]) for n in ("gr", "gz", "u", "ng", "dd", "new"))
        row = sb("row", [LANES, 2, STATE])
        targets = sb("targets", [LANES, cols], I32)
        target_stage, edge_stage = sb("target_stage", [LANES, RING], I32), sb("edge_stage", [LANES, RING, REC2])
        edges = K["rows"][0:LANES].rearrange("p r w -> p (r w)")[:, 0:cols * REC2]\
            .rearrange("p (c w) -> p c w", w=REC2)
        r_b, z_b, n_b, h_b, tr = (bank(n) for n in ("r", "z", "n", "h", "tr"))
        block = c.enter_context(nc.Block())
        state, agg = transposed(K["state"], 2), transposed(K["agg"], 2)
        w_comb, w_hh = K["w_comb"], K["w_hh_t"]
        base = rnd * PAIRS
        credit = rnd * (PAIRS + 1)

        def half(b, s):
            return b[:, s * PAIR:(s + 1) * PAIR]

        @block.tensor
        def _(pe):
            def gates(g, first):
                pair = bass.ds(g * PAIR, PAIR)

                def product(b, gate, sums, states):
                    for s in range(2):
                        terms = [(w_comb, agg, k) for k in range(2) if sums] + \
                                [(w_hh, state, k) for k in range(2) if states]
                        out = slice(gate * STATE + s * 128, gate * STATE + (s + 1) * 128)
                        for n, (w, v, k) in enumerate(terms):
                            last = pe.matmul(half(b, s), w[:, k, out], v[:, k, pair],
                                             start=(n == 0), stop=(n == len(terms) - 1))
                    return last

                if not first:
                    pe.wait_ge(S.r_ok, base + g)
                product(r_b, 0, True, True).then_inc(S.r_ps, 1)
                if not first:
                    pe.wait_ge(S.t_ok, base + g)
                product(h_b, 2, False, True).then_inc(S.h_ps, 1)
                if not first:
                    pe.wait_ge(S.u_ok, base + g)
                product(n_b, 2, True, False).then_inc(S.n_ps, 1)
                if not first:
                    pe.wait_ge(S.z_ok, base + g)
                product(z_b, 1, True, True).then_inc(S.z_ps, 1)

            def rows(g):
                pe.wait_ge(S.new_ok, base + g + 1)
                pe.wait_ge(S.row_ok, credit + g + 1)
                for j in range(2):
                    for s in range(2):
                        last = pe.transpose(tr[0:LANES, (j * 2 + s) * 128:(j * 2 + s + 1) * 128],
                                            new[:, s, j * LANES:(j + 1) * LANES], K["ident"][:])
                last.then_inc(S.tr_ok, 1)

            pe.sem_inc(S.tr_ok, 1)
            gates(0, True)
            with pe.Fori(0, PAIRS - 1) as g:
                gates(g + 1, False)
                rows(g)
            rows(PAIRS - 1)

        @block.scalar
        def _(act):
            def gate(g):
                act.wait_ge(S.r_ps, base + g + 1)
                act.activation(gr[:, 0, :], half(r_b, 0), ACT.Sigmoid, bias=K["b_rz"][:, 0:1])
                act.activation(gr[:, 1, :], half(r_b, 1), ACT.Sigmoid, bias=K["b_rz"][:, 1:2]).then_inc(S.r_ok, 1)
                act.wait_ge(S.z_ps, base + g + 1)
                act.activation(gz[:, 0, :], half(z_b, 0), ACT.Sigmoid, bias=K["b_rz"][:, 2:3])
                act.activation(gz[:, 1, :], half(z_b, 1), ACT.Sigmoid, bias=K["b_rz"][:, 3:4]).then_inc(S.z_ok, 1)
                act.wait_ge(S.u_ok, base + g + 1)
                act.activation(ng[:, 0, :], u[:, 0, :], ACT.Tanh, bias=K["b_n"][:, 0, 0:1])
                act.activation(ng[:, 1, :], u[:, 1, :], ACT.Tanh, bias=K["b_n"][:, 0, 1:2]).then_inc(S.n_ok, 1)

            def rows(g):
                act.wait_ge(S.tr_ok, credit + g + 2)
                act.wait_ge(S.row_free, credit + g + 1)
                act.copy(row[:].rearrange("p j w -> p (j w)"), tr[0:LANES, :]).then_inc(S.row_ok, 1)

            act.sem_inc(S.row_ok, 1)
            gate(0)
            with act.Fori(0, PAIRS - 1) as g:
                act.wait_ge(S.new_ok, base + g + 1)
                gate(g + 1)
                rows(g)
            rows(PAIRS - 1)

        @block.vector
        def _(dve):
            step = Steps(dve, S.step)
            with dve.Fori(0, PAIRS) as g:
                step.done = (base + g) * 6
                pair = bass.ds(g * PAIR, PAIR)
                dve.wait_ge(S.r_ok, base + g + 1)
                dve.wait_ge(S.h_ps, base + g + 1)
                for s in range(2):
                    last = dve.scalar_tensor_tensor(u[:, s, :], half(h_b, s), K["b_n"][:, 1, s:s + 1], gr[:, s, :],
                                                    ALU.add, ALU.mult)
                step(last)
                dve.sem_inc(S.t_ok, 1)
                dve.wait_ge(S.n_ps, base + g + 1)
                step(dve.tensor_tensor(u[:], u[:], n_b[:, 0:2 * PAIR].rearrange("p (s n) -> p s n", s=2), ALU.add))
                dve.sem_inc(S.u_ok, 1)
                dve.wait_ge(S.n_ok, base + g + 1)
                dve.wait_ge(S.z_ok, base + g + 1)
                step(dve.tensor_tensor(dd[:], state[:, :, pair], ng[:], ALU.subtract))
                step(dve.tensor_tensor(dd[:], dd[:], gz[:], ALU.mult))
                dve.wait_ge(S.tr_ok, credit + g + 1)
                step(dve.tensor_tensor(new[:], dd[:], ng[:], ALU.add))
                dve.sem_inc(S.new_ok, 1)
                step(dve.tensor_copy(state[:, :, pair], new[:]))

        @block.gpsimd
        def _(pool):
            def turn(i, first):
                for h in range(2):
                    stage = slice(h * HALF, h * HALF + HALF)
                    at = bass.ds(i * RING + h * HALF, HALF)
                    if not first:
                        pool.wait_ge(scattered[h], (rnd * turns + i) * (16 * HALF))
                    pool.tensor_copy(target_stage[:, stage], targets[:, at]).then_inc(S.staged, 1)
                    pool.tensor_copy(edge_stage[:, stage, :], edges[:, at, :]).then_inc(S.staged, 1)
                    pool.wait_ge(S.staged, (rnd * turns + i) * 4 + (2 * h + 2))
                    pool.sem_inc(S.issued, 1)
                    for r in range(h * HALF, h * HALF + HALF):
                        pool.indirect_dma_start(
                            out=T["slots2"],
                            out_offset=bass.IndirectOffsetOnAxis(ap=target_stage[:, r:r + 1], axis=0),
                            in_=edge_stage[:, r, :], in_offset=None).then_inc(scattered[h], 16)

            pool.wait_ge(S.edges_in, rnd * 32 + 32)
            pool.sem_inc(S.issued, 1)
            turn(0, True)
            with pool.Fori(1, turns) as i:
                turn(i, False)
            for h in range(2):
                pool.wait_ge(scattered[h], (rnd + 1) * (turns * 16 * HALF))
            pool.sem_inc(S.issued, 1)

        @block.sync
        def _(sp):
            part = bass.ds(rnd * cols, cols)
            sp.dma_start(targets[:], T["rows2"].rearrange("(p c) -> p c", p=LANES)[:, part]).then_inc(S.edges_in, 16)
            sp.dma_start(edges, T["edges2"].rearrange("(p c) w -> p c w", p=LANES)[:, part, :])\
                .then_inc(S.edges_in, 16)
            table = T["state"].rearrange("(p t) w -> p t w", p=LANES)
            sp.sem_inc(S.row_free, 1)
            with sp.Fori(0, PAIRS) as g:
                sp.wait_ge(S.row_ok, credit + g + 2)
                sp.dma_start(table[:, bass.ds(g * 2, 2), :], row[:]).then_inc(S.stored, 16)
                sp.wait_ge(S.stored, (base + g) * 16 + 16)
                sp.sem_inc(S.row_free, 1)


def layer2_nodes(nc, K, T, l0_b, l1_b, e_w1, e_b1):
    c, sb, sem, bank = phase(nc, "l2")
    with c:
        b0, b1 = sb("b0", [128, 2]), sb("b1", [LANES, D])
        w_edge = sb("w_edge", [D, 2, D])
        b_edge = sb("b_edge", [1, D])
        xs, xt = sb("xs", [LANES, 2, D]), sb("xt", [D, 2, PAIR])
        hid = sb("hid", [D, 2, 2, PAIR])
        y, x3, x3t = sb("y", [LANES, 2, D]), sb("x3", [LANES, 2, 2, D]), sb("x3t", [D, 2, PAIR])
        colrow = sb("colrow", [LANES, 2, 2, D])
        norm = Norm(sb, sem)
        xt_ps, hid_ps, y_ps, x3t_ps, proj_ps = (bank(n) for n in ("xt_ps", "hid_ps", "y_ps", "x3t_ps", "proj_ps"))
        loaded, sum_step, norm_step = sem("loaded"), sem("sum_step"), sem("norm_step")
        xs_ok, xt_ps_ok, xt_ok, hid_ps_ok, hid_ok, y_ps_ok, y_used = (
            sem(n) for n in ("xs_ok", "xt_ps_ok", "xt_ok", "hid_ps_ok", "hid_ok", "y_ps_ok", "y_used"))
        x3_ok, x3_kept, x3t_ps_ok, x3t_ok = sem("x3_ok"), sem("x3_kept"), sem("x3t_ps_ok"), sem("x3t_ok")
        proj_ps_ok, proj_ok, stored = sem("proj_ps_ok"), sem("proj_ok"), [sem("stored0"), sem("stored1")]
        line = Pipeline(PAIRS, 2, 2, 4)
        number, exists, wait, run = line.number, line.exists, line.wait, line.run
        block = c.enter_context(nc.Block())
        rows, source_rows = rows_of(K["agg"], ROWS_A), rows_of(K["agg"], ROWS_B)
        state = transposed(K["state"], 2)
        LOADED = 16 * 6

        @block.sync
        def _(sp):
            sp.dma_start(rows, T["x2"].rearrange("(p t) f -> p t f", p=LANES)).then_inc(loaded, 16)
            with nc.allow_non_contiguous_dma(reason="a few biases by partition"):
                sp.dma_start(b0[:], l0_b.rearrange("(q p) -> p q", p=128)).then_inc(loaded, 16)
            sp.dma_start(b1[:], l1_b.rearrange("(a f) -> a f", a=1).to_broadcast([LANES, D])).then_inc(loaded, 16)
            for k in range(2):
                sp.dma_start(w_edge[:, k, :], e_w1[k * D:(k + 1) * D, :]).then_inc(loaded, 16)
            sp.dma_start(b_edge[:], e_b1.rearrange("(a f) -> a f", a=1)).then_inc(loaded, 16)
            table = T["xcol"].rearrange("(p t) f -> p t f", p=LANES)

            def step(i, off):
                if exists(i, off):
                    wait(sp, proj_ok, i, off)
                    sp.dma_start(table[:, bass.ds(number(i, off) * 2, 2), :], colrow[:, off % 2])\
                        .then_inc(stored[off % 2], 16)
            run(sp, step)
            for q in range(2):
                sp.wait_ge(stored[q], 16 * ((PAIRS + 1 - q) // 2))

        @block.gpsimd
        def _(pool):
            def step(i, off):
                if exists(i, off + 2):
                    wait(pool, xt_ps_ok, i, off + 1)
                    pool.tensor_copy(xs[:], rows[:, bass.ds(number(i, off + 2) * 2, 2), :]).then_inc(xs_ok, 1)
                if exists(i, off - 2):
                    wait(pool, x3_ok, i, off - 2)
                    pool.tensor_copy(rows[:, bass.ds(number(i, off - 2) * 2, 2), :], x3[:, off % 2])\
                        .then_inc(x3_kept, 1)

            pool.wait_ge(loaded, LOADED)
            run(pool, step)

        @block.tensor
        def _(pe):
            def step(i, off):
                if exists(i, off + 1):
                    wait(pe, xs_ok, i, off + 1)
                    wait(pe, xt_ok, i, off)
                    for j in range(2):
                        last = pe.transpose(xt_ps[:, j * LANES:(j + 1) * LANES], xs[:, j, :],
                                            K["ident"][0:LANES, 0:LANES])
                    last.then_inc(xt_ps_ok, 1)
                if exists(i, off):
                    wait(pe, xt_ok, i, off)
                    wait(pe, hid_ok, i, off - 1)
                    for s in range(2):
                        for k in range(3):
                            v = xt[:, off % 2, :] if k == 2 else state[:, k, bass.ds(number(i, off) * PAIR, PAIR)]
                            last = pe.matmul(hid_ps[:, s * PAIR:(s + 1) * PAIR],
                                             K["l0_t"][:, k, s * 128:(s + 1) * 128], v,
                                             start=(k == 0), stop=(k == 2))
                    last.then_inc(hid_ps_ok, 1)
                if exists(i, off - 1):
                    wait(pe, hid_ok, i, off - 1)
                    wait(pe, y_used, i, off - 2)
                    for j in range(2):
                        for k in range(2):
                            last = pe.matmul(y_ps[0:LANES, j * D:(j + 1) * D],
                                             hid[:, (off - 1) % 2, k, j * LANES:(j + 1) * LANES],
                                             K["l1_t"][:, k, :], start=(k == 0), stop=(k == 1))
                    last.then_inc(y_ps_ok, 1)
                if exists(i, off - 3):
                    wait(pe, x3_ok, i, off - 3)
                    wait(pe, x3t_ok, i, off - 4)
                    for j in range(2):
                        last = pe.transpose(x3t_ps[:, j * LANES:(j + 1) * LANES], x3[:, (off - 3) % 2, j, :],
                                            K["ident"][0:LANES, 0:LANES])
                    last.then_inc(x3t_ps_ok, 1)
                if exists(i, off - 4):
                    wait(pe, x3t_ok, i, off - 4)
                    wait(pe, proj_ok, i, off - 5)
                    for j in range(2):
                        v = x3t[:, off % 2, j * LANES:(j + 1) * LANES]
                        at_source, at_dest = (proj_ps[0:LANES, (2 * j + k) * D:(2 * j + k + 1) * D]
                                              for k in range(2))
                        pe.matmul(at_source, v, w_edge[:, 0, :], start=True, stop=False)
                        pe.matmul(at_source, K["ones"][0:1, 0:LANES], b_edge[:], start=False, stop=True)
                        last = pe.matmul(at_dest, v, w_edge[:, 1, :], start=True, stop=True)
                    last.then_inc(proj_ps_ok, 1)

            pe.wait_ge(loaded, LOADED)
            run(pe, step)

        @block.scalar
        def _(act):
            def step(i, off):
                if exists(i, off + 1):
                    wait(act, xt_ps_ok, i, off + 1)
                    wait(act, hid_ps_ok, i, off - 1)
                    act.copy(xt[:, (off + 1) % 2, :], xt_ps[:, 0:PAIR]).then_inc(xt_ok, 1)
                if exists(i, off - 3):
                    wait(act, x3t_ps_ok, i, off - 3)
                    wait(act, proj_ps_ok, i, off - 5)
                    act.copy(x3t[:, (off - 3) % 2, :], x3t_ps[:, 0:PAIR]).then_inc(x3t_ok, 1)
                if exists(i, off):
                    wait(act, hid_ps_ok, i, off)
                    wait(act, y_ps_ok, i, off - 2)
                    for s in range(2):
                        last = act.activation(hid[:, off % 2, s, :], hid_ps[:, s * PAIR:(s + 1) * PAIR], ACT.Relu,
                                              bias=b0[:, s:s + 1])
                    last.then_inc(hid_ok, 1)
                if exists(i, off - 4):
                    wait(act, proj_ps_ok, i, off - 4)
                    if i is not None or off - 6 >= 0:
                        turn = (off - 6) // 2 if i is None else i + (off - 6) // 2
                        act.wait_ge(stored[off % 2], turn * 16 + 16)
                    proj = proj_ps[0:LANES, :].rearrange("p (j k f) -> p j k f", j=2, k=2)
                    act.copy(source_rows[:, bass.ds(number(i, off - 4) * 2, 2), :], proj[:, :, 0, :])
                    act.copy(colrow[:, off % 2], proj[:, :, 1, :]).then_inc(proj_ok, 1)
                if exists(i, off - 1):
                    deviation(act, K, number(i, off - 1), norm)

            act.wait_ge(loaded, LOADED)
            run(act, step)

        @block.vector
        def _(dve):
            total, scaled = Steps(dve, sum_step), Steps(dve, norm_step)

            def step(i, off):
                if exists(i, off - 2):
                    scaled.done = number(i, off - 2)
                    wait(dve, norm.std_ok, i, off - 2)
                    scaled(dve.reciprocal(norm.rstd[:], norm.std[:]))
                    wait(dve, x3_kept, i, off - 4)
                    wait(dve, x3t_ps_ok, i, off - 4)
                    for j in range(2):
                        last = dve.tensor_scalar(x3[:, off % 2, j, :], y[:, j, :], norm.mean_var[:, j, 0:1],
                                                 norm.rstd[:, j:j + 1], ALU.subtract, ALU.mult)
                    last.then_inc(x3_ok, 1)
                if exists(i, off - 1):
                    total.done = number(i, off - 1) * 3
                    wait(dve, y_ps_ok, i, off - 1)
                    wait(dve, x3_ok, i, off - 2)
                    total(dve.tensor_tensor(y[:], y_ps[0:LANES, 0:2 * D].rearrange("p (j f) -> p j f", j=2),
                                            b1[:, None, :].to_broadcast([LANES, 2, D]), ALU.add))
                    dve.sem_inc(y_used, 1)
                    total(dve.scalar_tensor_tensor(y[:], y[:], 0.0, rows[:, bass.ds(number(i, off - 1) * 2, 2), :],
                                                   ALU.max, ALU.add))
                    for j in range(2):
                        last = dve.bn_stats(norm.stats[:, j, :], y[:, j, :])
                    total(last)
                    dve.sem_inc(norm.dve_passed, 1)
                    for j in range(2):
                        last = dve.bn_aggr(norm.mean_var[:, j, :], norm.stats[:, j, :])
                    last.then_inc(norm.var_ok, 1)

            dve.wait_ge(loaded, LOADED)
            run(dve, step)


def edge_mlp(nc, K, T, row_in, e_w1, e_w2, e_b2):
    c, sb, sem, bank = phase(nc, "l3")
    with c:
        HALVES = CHUNKS // HALF
        W = HALF * D
        LEAD = 3
        w_attr = sb("w_attr", [HALF * REC2, W])
        w2, b2 = sb("w2", [D, D]), sb("b2", [128, D])
        slots = sb("slots", [128, DEEP, HALF, REC2])
        idx = sb("idx", [128, FETCH * HALF], I32)
        gathered = sb("gathered", [128, FETCH, W])
        onehot = sb("onehot", [128, DEEP, HALF, LANES])
        onehot_t, slots_t = sb("onehot_t", [LANES, 2, HALF * SLOT]), sb("slots_t", [HALF * REC2, 2, SLOT])
        pre1, hid, hid_t = sb("pre1", [128, W]), sb("hid", [128, 2, W]), sb("hid_t", [D, 2, HALF * SLOT])
        pre2, msg = sb("pre2", [128, W]), sb("msg", [128, 2, W])
        onehot_ps, slots_ps, hid_ps, hid_t_ps, msg_ps, sum_ps = (
            bank(n) for n in ("onehot_ps", "slots_ps", "hid_ps", "hid_t_ps", "msg_ps", "sum_ps"))
        loaded, zeroed = sem("loaded"), sem("zeroed")
        slots_in = [sem(f"slots_in{q}") for q in range(DEEP)]
        idx_ok, issued, onehot_ok = sem("idx_ok"), sem("issued"), sem("onehot_ok")
        tr_ps_ok, tr_ok = sem("tr_ps_ok"), sem("tr_ok")
        hid_ps_ok, pre1_ok, hid_ok = sem("hid_ps_ok"), sem("pre1_ok"), sem("hid_ok")
        hid_t_ps_ok, hid_t_ok = sem("hid_t_ps_ok"), sem("hid_t_ok")
        msg_ps_ok, pre2_ok, msg_ok = sem("msg_ps_ok"), sem("pre2_ok"), sem("msg_ok")
        sum_ok, added = sem("sum_ok"), sem("added")
        block = c.enter_context(nc.Block())
        source_rows = K["agg"][0:LANES, ROWS_B:ROWS_B + TILES * D]
        sums = K["state"]

        line = Pipeline(HALVES, DEEP, LEAD, LEAD)
        number, exists, wait_half, run = line.number, line.exists, line.wait, line.run

        def wait_slots(eng, i, off):
            turn = off // DEEP if i is None else i + off // DEEP
            eng.wait_ge(slots_in[off % DEEP], turn * 16 + 16)

        @block.sync
        def _(sp):
            sp.wait_ge(zeroed, 2)
            for k in range(HALF):
                sp.dma_start(w_attr[k * REC2 + 2:(k + 1) * REC2, k * D:(k + 1) * D], e_w1[2 * D:2 * D + ATTR, :])\
                    .then_inc(loaded, 16)
            sp.dma_start(w2[:], e_w2).then_inc(loaded, 16)
            sp.dma_start(b2[:], e_b2.rearrange("(a f) -> a f", a=1).to_broadcast([128, D])).then_inc(loaded, 16)
            table = T["slots2"].rearrange("(p q) w -> p q w", p=128)

            def load(i, off):
                wait_half(sp, tr_ps_ok, i, off - DEEP)
                wait_half(sp, idx_ok, i, off - DEEP)
                sp.dma_start(slots[:, off % DEEP], table[:, bass.ds(number(i, off) * HALF, HALF), :])\
                    .then_inc(slots_in[off % DEEP], 16)
            for j in range(DEEP):
                load(None, j)
            with sp.Fori(0, HALVES // DEEP - 1) as i:
                for q in range(DEEP):
                    load(i, DEEP + q)

        @block.gpsimd
        def _(pool):
            with pool.Fori(0, HALVES // FETCH) as i:
                for q in range(FETCH):
                    pool.wait_ge(idx_ok, i * FETCH + (q + 1))
                    pool.sem_inc(issued, 1)
                    for k in range(HALF):
                        r = q * HALF + k
                        pool.indirect_dma_start(
                            out=gathered[:, q, k * D:(k + 1) * D], out_offset=None, in_=T["xcol"],
                            in_offset=bass.IndirectOffsetOnAxis(ap=idx[:, r:r + 1], axis=0)).then_inc(row_in[q], 16)

        @block.tensor
        def _(pe):
            def step(i, off):
                if exists(i, off + 1):
                    q = (off + 1) % DEEP
                    wait_half(pe, onehot_ok, i, off + 1)
                    wait_half(pe, tr_ok, i, off)
                    for k in range(HALF):
                        pe.transpose(onehot_ps[0:LANES, k * SLOT:(k + 1) * SLOT], onehot[:, q, k, :], K["ident"][:])
                    pe.transpose(slots_ps[0:HALF * REC2, 0:SLOT], slots[:, q].rearrange("p k w -> p (k w)"),
                                 K["ident"][:])\
                        .then_inc(tr_ps_ok, 1)
                if exists(i, off):
                    word = tile_word(pe, K["tile2"], number(i, off))
                    wait_half(pe, tr_ok, i, off)
                    wait_half(pe, pre1_ok, i, off - 1)
                    pe.matmul(hid_ps[:], slots_t[:, off % 2, :], w_attr[:], start=True, stop=False)
                    for k in range(HALF):
                        last = pe.matmul(hid_ps[:, k * D:(k + 1) * D],
                                         onehot_t[:, off % 2, k * SLOT:(k + 1) * SLOT],
                                         source_rows[:, bass.ds(place(pe, word, k, D), D)],
                                         start=False, stop=(k == HALF - 1))
                    last.then_inc(hid_ps_ok, 1)
                if exists(i, off - 1):
                    wait_half(pe, hid_ok, i, off - 1)
                    wait_half(pe, hid_t_ok, i, off - 2)
                    for k in range(HALF):
                        last = pe.transpose(hid_t_ps[:, k * SLOT:(k + 1) * SLOT],
                                            hid[:, (off - 1) % 2, k * D:(k + 1) * D], K["ident"][:])
                    last.then_inc(hid_t_ps_ok, 1)
                if exists(i, off - 2):
                    wait_half(pe, hid_t_ok, i, off - 2)
                    wait_half(pe, pre2_ok, i, off - 3)
                    for k in range(HALF):
                        last = pe.matmul(msg_ps[:, k * D:(k + 1) * D],
                                         hid_t[:, off % 2, k * SLOT:(k + 1) * SLOT], w2[:], start=True, stop=True)
                    last.then_inc(msg_ps_ok, 1)
                if exists(i, off - 3):
                    wait_half(pe, msg_ok, i, off - 3)
                    if i is not None or off - 4 >= 0:
                        pe.wait_ge(added, number(i, off - 3) * HALF)
                    for k in range(HALF):
                        last = pe.matmul(sum_ps[:, k * LANES:(k + 1) * LANES],
                                         msg[:, (off - 3) % 2, k * D:(k + 1) * D], onehot[:, (off - 3) % DEEP, k, :],
                                         start=True, stop=True)
                    last.then_inc(sum_ok, 1)

            pe.wait_ge(loaded, 96)
            run(pe, step)

        @block.scalar
        def _(act):
            def step(i, off):
                if exists(i, off + 3):
                    q = (off + 3) % FETCH
                    wait_slots(act, i, off + 3)
                    wait_half(act, pre1_ok, i, off - 1)
                    act.copy(idx[:, q * HALF:(q + 1) * HALF], slots[:, (off + 3) % DEEP, :, 0]).then_inc(idx_ok, 1)
                if exists(i, off + 1):
                    b = (off + 1) % 2
                    wait_half(act, tr_ps_ok, i, off + 1)
                    wait_half(act, hid_ps_ok, i, off - 1)
                    act.copy(onehot_t[:, b, :], onehot_ps[0:LANES, :])
                    act.copy(slots_t[:, b, :], slots_ps[0:HALF * REC2, 0:SLOT]).then_inc(tr_ok, 1)
                if exists(i, off - 1):
                    wait_half(act, hid_t_ps_ok, i, off - 1)
                    wait_half(act, msg_ps_ok, i, off - 3)
                    act.copy(hid_t[:, (off - 1) % 2, :], hid_t_ps[:]).then_inc(hid_t_ok, 1)
                if exists(i, off):
                    wait_half(act, pre1_ok, i, off)
                    wait_half(act, hid_t_ps_ok, i, off - 2)
                    act.activation(hid[:, off % 2, :], pre1[:], ACT.Silu).then_inc(hid_ok, 1)
                if exists(i, off - 2):
                    wait_half(act, pre2_ok, i, off - 2)
                    wait_half(act, sum_ok, i, off - 4)
                    act.activation(msg[:, off % 2, :], pre2[:], ACT.Silu).then_inc(msg_ok, 1)

            run(act, step)

        @block.vector
        def _(dve):
            def step(i, off):
                if exists(i, off - 3):
                    word = tile_word(dve, K["tile2"], number(i, off - 3))
                if exists(i, off + 2):
                    q = (off + 2) % DEEP
                    wait_slots(dve, i, off + 2)
                    wait_half(dve, sum_ok, i, off + 2 - DEEP)
                    dve.tensor_tensor(onehot[:, q], K["iota_row"][:, None, 0:LANES].to_broadcast([128, HALF, LANES]),
                                      slots[:, q, :, 1:2].to_broadcast([128, HALF, LANES]), ALU.is_equal)\
                        .then_inc(onehot_ok, 1)
                if exists(i, off):
                    wait_half(dve, hid_ps_ok, i, off)
                    turn = off // FETCH if i is None else i * (DEEP // FETCH) + off // FETCH
                    dve.wait_ge(row_in[off % FETCH], turn * (16 * HALF) + 16 * HALF)
                    wait_half(dve, hid_ok, i, off - 1)
                    dve.tensor_tensor(pre1[:], hid_ps[:], gathered[:, off % FETCH, :], ALU.add).then_inc(pre1_ok, 1)
                if exists(i, off - 2):
                    wait_half(dve, msg_ps_ok, i, off - 2)
                    wait_half(dve, msg_ok, i, off - 3)
                    dve.tensor_tensor(pre2[:].rearrange("p (k f) -> p k f", k=HALF),
                                      msg_ps[:].rearrange("p (k f) -> p k f", k=HALF),
                                      b2[:, None, :].to_broadcast([128, HALF, D]), ALU.add).then_inc(pre2_ok, 1)
                if exists(i, off - 3):
                    at = place(dve, word, 0, LANES)
                    wait_half(dve, sum_ok, i, off - 3)
                    for k in range(HALF):
                        if i is not None or (off - 3) * HALF + k > 0:
                            dve.wait_ge(added, number(i, off - 3) * HALF + k)
                        a = sums[:, bass.ds(at, LANES)]
                        dve.tensor_tensor(a, a, sum_ps[:, k * LANES:(k + 1) * LANES], ALU.add).then_inc(added, 1)
                        if k < HALF - 1:
                            at = place(dve, word, k + 1, LANES)

            dve.memset(w_attr[:], 0.0).then_inc(zeroed, 1)
            dve.memset(sums[:, 0:NODES], 0.0).then_inc(zeroed, 1)
            dve.wait_ge(zeroed, 2)
            dve.wait_ge(loaded, 96)
            run(dve, step)


def layer3_nodes(nc, K, n_w1, n_b1, n_w2, n_b2, out):
    c, sb, sem, bank = phase(nc, "l4")
    with c:
        w1, w2 = sb("w1", [D, 2, D]), sb("w2", [D, D])
        b1, b2 = sb("b1", [D, 1]), sb("b2", [LANES, D])
        xs, xt, hid = sb("xs", [LANES, 2, D]), sb("xt", [D, 2, PAIR]), sb("hid", [D, 2, PAIR])
        y = sb("y", [LANES, 2, 2, D])
        stats, mean_var = sb("stats", [LANES, 2, 6]), sb("mean_var", [LANES, TILES, 2])
        pair_mean_var = sb("pair_mean_var", [LANES, 2, 2])
        std, rstd = sb("std", [LANES, TILES]), sb("rstd", [LANES, TILES])
        PARTS = 5
        xt_ps, hid_ps, y_ps = bank("xt_ps"), bank("hid_ps"), bank("y_ps")
        loaded, row_step = sem("loaded"), sem("row_step")
        xs_ok, xt_ps_ok, xt_ok, hid_ps_ok, hid_ok, y_ps_ok, y_used, y_ok, y_kept, var_kept = (
            sem(n) for n in ("xs_ok", "xt_ps_ok", "xt_ok", "hid_ps_ok", "hid_ok", "y_ps_ok", "y_used", "y_ok",
                             "y_kept", "var_kept"))
        passed, std_ok, rstd_ok, part_ok, stored = (sem(n) for n in ("passed", "std_ok", "rstd_ok", "part_ok",
                                                                     "stored"))
        line = Pipeline(PAIRS, 2, 2, 1)
        number, exists, wait, run = line.number, line.exists, line.wait, line.run
        block = c.enter_context(nc.Block())
        rows = rows_of(K["agg"], ROWS_A)
        sums = K["state"]

        @block.sync
        def _(sp):
            for k in range(2):
                sp.dma_start(w1[:, k, :], n_w1[k * D:(k + 1) * D, :]).then_inc(loaded, 16)
            sp.dma_start(w2[:], n_w2).then_inc(loaded, 16)
            sp.dma_start(b1[:], n_b1.rearrange("(p a) -> p a", a=1)).then_inc(loaded, 16)
            sp.dma_start(b2[:], n_b2.rearrange("(a f) -> a f", a=1).to_broadcast([LANES, D])).then_inc(loaded, 16)
            for q in range(PARTS):
                t = slice(q * TILES // PARTS, (q + 1) * TILES // PARTS)
                sp.wait_ge(part_ok, q + 1)
                sp.dma_start(out.rearrange("(p t) f -> p t f", p=LANES)[:, t, :], rows[:, t, :]).then_inc(stored, 16)
            sp.wait_ge(stored, 16 * PARTS)

        @block.gpsimd
        def _(pool):
            def step(i, off):
                if exists(i, off + 2):
                    wait(pool, xt_ps_ok, i, off + 1)
                    pool.tensor_copy(xs[:], rows[:, bass.ds(number(i, off + 2) * 2, 2), :]).then_inc(xs_ok, 1)
                if exists(i, off - 1):
                    wait(pool, y_ok, i, off - 1)
                    pool.tensor_copy(rows[:, bass.ds(number(i, off - 1) * 2, 2), :], y[:, (off - 1) % 2])\
                        .then_inc(y_kept, 1)

            run(pool, step)

        @block.tensor
        def _(pe):
            def step(i, off):
                if exists(i, off + 1):
                    wait(pe, xs_ok, i, off + 1)
                    wait(pe, xt_ok, i, off)
                    for j in range(2):
                        last = pe.transpose(xt_ps[:, j * LANES:(j + 1) * LANES], xs[:, j, :],
                                            K["ident"][0:LANES, 0:LANES])
                    last.then_inc(xt_ps_ok, 1)
                if exists(i, off):
                    wait(pe, xt_ok, i, off)
                    wait(pe, hid_ok, i, off - 1)
                    pe.matmul(hid_ps[:, 0:PAIR], w1[:, 0, :], xt[:, off % 2, :], start=True, stop=False)
                    pe.matmul(hid_ps[:, 0:PAIR], w1[:, 1, :], sums[:, bass.ds(number(i, off) * PAIR, PAIR)],
                              start=False, stop=True).then_inc(hid_ps_ok, 1)
                if exists(i, off - 1):
                    wait(pe, hid_ok, i, off - 1)
                    wait(pe, y_used, i, off - 2)
                    for j in range(2):
                        last = pe.matmul(y_ps[0:LANES, j * D:(j + 1) * D],
                                         hid[:, (off - 1) % 2, j * LANES:(j + 1) * LANES], w2[:],
                                         start=True, stop=True)
                    last.then_inc(y_ps_ok, 1)

            pe.wait_ge(loaded, 80)
            run(pe, step)

        @block.scalar
        def _(act):
            def step(i, off):
                if exists(i, off + 1):
                    wait(act, xt_ps_ok, i, off + 1)
                    wait(act, hid_ps_ok, i, off - 1)
                    act.copy(xt[:, (off + 1) % 2, :], xt_ps[:, 0:PAIR]).then_inc(xt_ok, 1)
                if exists(i, off):
                    wait(act, hid_ps_ok, i, off)
                    wait(act, y_ps_ok, i, off - 2)
                    act.activation(hid[:, off % 2, :], hid_ps[:, 0:PAIR], ACT.Silu, bias=b1[:]).then_inc(hid_ok, 1)

            act.wait_ge(loaded, 80)
            run(act, step)
            act.wait_ge(var_kept, PAIRS)
            act.activation(std[:], mean_var[:, :, 1], ACT.Sqrt, bias=K["eps"][0:LANES, :]).then_inc(std_ok, 1)

        @block.vector
        def _(dve):
            row = Steps(dve, row_step)

            def step(i, off):
                if exists(i, off - 1):
                    g = number(i, off - 1)
                    new = y[:, (off - 1) % 2]
                    row.done = g * 4
                    wait(dve, y_ps_ok, i, off - 1)
                    wait(dve, y_kept, i, off - 3)
                    row(dve.tensor_tensor(new, y_ps[0:LANES, 0:2 * D].rearrange("p (j f) -> p j f", j=2),
                                          b2[:, None, :].to_broadcast([LANES, 2, D]), ALU.add))
                    dve.sem_inc(y_used, 1)
                    row(dve.scalar_tensor_tensor(new, rows[:, bass.ds(g * 2, 2), :], 2.0, new, ALU.mult, ALU.add))
                    dve.sem_inc(y_ok, 1)
                    for j in range(2):
                        last = dve.bn_stats(stats[:, j, :], new[:, j, :])
                    row(last)
                    dve.sem_inc(passed, 1)
                    wait(dve, var_kept, i, off - 2)
                    dve.sem_inc(passed, 1)
                    for j in range(2):
                        last = dve.bn_aggr(pair_mean_var[:, j, :], stats[:, j, :])
                    row(last)
                    dve.sem_inc(passed, 1)
                    dve.tensor_copy(mean_var[:, bass.ds(g * 2, 2), :], pair_mean_var[:]).then_inc(var_kept, 1)

            dve.wait_ge(loaded, 80)
            run(dve, step)
            dve.wait_ge(y_kept, PAIRS)
            dve.wait_ge(std_ok, 1)
            dve.reciprocal(rstd[:], std[:]).then_inc(rstd_ok, 1)
            dve.wait_ge(rstd_ok, 1)
            for q in range(PARTS):
                for t in range(q * TILES // PARTS, (q + 1) * TILES // PARTS):
                    ins = dve.tensor_scalar(rows[:, t, :], rows[:, t, :], mean_var[:, t, 0:1], rstd[:, t:t + 1],
                                            ALU.subtract, ALU.mult)
                ins.then_inc(part_ok, 1)


def gnn(nc, x, src, dst, edge_attr_16, edge_type_8, edge_weight1, L0_gnn_W_l, L0_gnn_b_l, L0_gnn_W_r,
        L1_gnn_weight, L1_gnn_bias, L2_gnn_W, L2_gnn_w_ih, L2_gnn_w_hh, L2_gnn_b_ih, L2_gnn_b_hh,
        L2_gnn_l0_w, L2_gnn_l0_b, L2_gnn_l1_w, L2_gnn_l1_b, L3_gnn_eW1, L3_gnn_eb1, L3_gnn_eW2, L3_gnn_eb2,
        L3_gnn_nW1, L3_gnn_nb1, L3_gnn_nW2, L3_gnn_nb2, out):
    with ExitStack() as c:
        K = {}

        def buffers(*specs):
            for name, shape, *dt in specs:
                K[name] = c.enter_context(nc.sbuf_tensor(name, shape, *(dt or [F32])))

        T = tables(nc, c)
        buffers(("ident", [128, 128]), ("iota_row", [128, 128]), ("ones", [128, 128]), ("before", [128, 128]),
                ("chunk_no", [128, TILE_COLS]), ("eps", [128, 1]), ("rec", [128, PAD_CHUNKS, REC1]),
                ("tile1", [1, CHUNKS // HALF], I32),
                ("tile2", [1, CHUNKS // HALF], I32))
        constants(nc, K)

        def sems(name, n):
            return [c.enter_context(nc.semaphore(f"{name}{r}")) for r in range(n)]

        sort_edges(nc, K, T, sems("scattered1_", 2), src, dst, edge_attr_16, edge_type_8, edge_weight1)
        load_slots(nc, K, T)
        buffers(("agg", [128, 2 * TILES * D]), ("state", [128, 2 * TILES * D]))
        with ExitStack() as g:
            def scoped(*specs):
                for name, shape, *dt in specs:
                    K[name] = g.enter_context(nc.sbuf_tensor(name, shape, *(dt or [F32])))

            scoped(("onehot", [128, G_HALVES, HALF, LANES]), ("rows", [128, G_RING, STATE]),
                   ("idx", [128, G_RING], I32))
            with ExitStack() as q:
                K["cnt"] = q.enter_context(nc.sbuf_tensor("cnt", [LANES, TILES], F32))
                gather_s = GatherSems(semaphores(nc, q), sems("g0_row_in", G_HALVES), "g0")
                gather_sum(nc, K, gather_s, 0, x, 0, D, count=True)
                layer0_nodes(nc, K, T, x, L0_gnn_W_l, L0_gnn_b_l, L0_gnn_W_r, L1_gnn_weight)
            with ExitStack() as q:
                gather_s = GatherSems(semaphores(nc, q), sems("g1_row_in", G_HALVES), "g1")
                gather_sum(nc, K, gather_s, 0, T["rel"], 2, D, by_row=True, weighted=True)
                layer1_nodes(nc, K, T, L1_gnn_bias)
            scoped(("w_ih_t", [128, 2, GATES]), ("w_hh_t", [128, 2, GATES]), ("w_comb", [128, 2, GATES]),
                   ("l0_t", [128, 3, 256]), ("l1_t", [128, 2, D]), ("b_rz", [128, 4]), ("b_n", [128, 2, 2]))
            gated_weights(nc, K, L2_gnn_w_ih, L2_gnn_w_hh, L2_gnn_b_ih, L2_gnn_b_hh, L2_gnn_l0_w, L2_gnn_l1_w)
            with ExitStack() as q:
                rounds = L2_gnn_W.shape[0]
                scattered = sems("scattered2_", 2)
                gather_s = GatherSems(semaphores(nc, q), sems("g2_row_in", G_HALVES), "g2")
                combined, gate_s = CombinedWeight(semaphores(nc, q), K, L2_gnn_W), GateSems(semaphores(nc, q))
                with nc.Fori(0, rounds) as rnd:
                    gather_sum(nc, K, gather_s, rnd, T["state"], 0, STATE, combined=combined)
                    gated_update(nc, K, T, gate_s, scattered, rnd, rounds)
            layer2_nodes(nc, K, T, L2_gnn_l0_b, L2_gnn_l1_b, L3_gnn_eW1, L3_gnn_eb1)
        edge_mlp(nc, K, T, sems("edge_row_in", FETCH), L3_gnn_eW1, L3_gnn_eW2, L3_gnn_eb2)
        layer3_nodes(nc, K, L3_gnn_nW1, L3_gnn_nb1, L3_gnn_nW2, L3_gnn_nb2, out)


_INS = ["x", "src", "dst", "edge_attr_16", "edge_type_8", "edge_weight1", "L0_gnn_W_l", "L0_gnn_b_l", "L0_gnn_W_r",
        "L1_gnn_weight", "L1_gnn_bias", "L2_gnn_W", "L2_gnn_w_ih", "L2_gnn_w_hh", "L2_gnn_b_ih", "L2_gnn_b_hh",
        "L2_gnn_l0_w", "L2_gnn_l0_b", "L2_gnn_l1_w", "L2_gnn_l1_b", "L3_gnn_eW1", "L3_gnn_eb1", "L3_gnn_eW2",
        "L3_gnn_eb2", "L3_gnn_nW1", "L3_gnn_nb1", "L3_gnn_nW2", "L3_gnn_nb2"]
_OUTS = [((NODES, D), "float32")]


def kernel(**inputs):
    import numpy as _np
    import concourse.bacc as _bacc
    from concourse import mybir as _mybir
    from concourse.bass_utils import run_bass_kernel_spmd as _run

    nc = _bacc.Bacc("TRN2", target_bir_lowering=False, num_devices=1)
    arrays, args = {}, []
    for name in _INS:
        a = _np.ascontiguousarray(inputs[name])
        arrays[f"in_{name}_dram"] = a
        args.append(nc.dram_tensor(f"in_{name}_dram", a.shape, _mybir.dt.from_np(a.dtype), kind="ExternalInput").ap())
    for i, (shape, dtype) in enumerate(_OUTS):
        dt = _mybir.dt.from_np(_np.dtype(dtype))
        args.append(nc.dram_tensor(f"out_{i}_dram", shape, dt, kind="ExternalOutput").ap())
    gnn(nc, *args)
    r = _run(nc, [arrays], core_ids=[0])
    got = tuple(r.results[0][f"out_{i}_dram"] for i in range(len(_OUTS)))
    return got[0]
```
